# Optimizing a Trainium2 kernel written in Bass

```python
import numpy as np
import jax
import jax.numpy as jnp

def _softmax(x, axis=-1):
    return jax.nn.softmax(x, axis=axis)

def _gelu(x):
    return jax.nn.gelu(x, approximate=True)

def _silu(x):
    return jax.nn.silu(x)

def _sigmoid(x):
    return jax.nn.sigmoid(x)

def _layernorm(x, axis=-1, eps=1e-05):
    m = jnp.mean(x, axis=axis, keepdims=True)
    v = jnp.var(x, axis=axis, keepdims=True)
    return (x - m) / jnp.sqrt(v + eps)

def _scatter_add(tgt, idx, src, axis=0):
    return tgt.at[idx].add(src)

def _segment_sum(src, seg, n):
    return jax.ops.segment_sum(src, seg, n)
kernel_name = 'mk_prb_d2_jaxref_r4_7cb4f4'

def setup_inputs(seed: int=0):
    np.random.seed(seed)
    _w = jnp.asarray

    def _L0_attn_setup():
        import jax, jax.numpy as jnp
        import numpy as np
        import math
        P = 64
        H = 256
        B = 8
        L = 1024
        R_MIN, R_MAX, THETA_MAX = (0.9, 0.999, math.pi)

        def _map_theta_to_A(thetas, G_diag, steps):
            cos_t = jnp.cos(thetas)
            tan_sq = jnp.tan(thetas) ** 2
            sqrt_term = 4.0 * jnp.sqrt(steps ** 4 / cos_t ** 2 + steps ** 5 * G_diag / cos_t ** 2)
            common = steps ** 2 * (-4.0 - 2.0 * steps * G_diag - 4.0 * tan_sq - 2.0 * steps * G_diag * tan_sq)
            denom = 2.0 * steps ** 4 * (1.0 + tan_sq)
            A_plus = (sqrt_term - common) / denom
            A_minus = (-sqrt_term - common) / denom
            return jnp.where(thetas > math.pi / 2, A_plus, A_minus)

        def _binary_operator(q_i, q_j):
            A_i, b_i = q_i
            A_j, b_j = q_j
            iA, iB, iC, iD = jnp.split(A_i, 4, axis=-1)
            jA, jB, jC, jD = jnp.split(A_j, 4, axis=-1)
            A_new = jnp.concatenate([jA * iA + jB * iC, jA * iB + jB * iD, jC * iA + jD * iC, jC * iB + jD * iD], axis=-1)
            b_i1, b_i2 = jnp.split(b_i, 2, axis=-2)
            new_b1 = jA[..., None] * b_i1 + jB[..., None] * b_i2
            new_b2 = jC[..., None] * b_i1 + jD[..., None] * b_i2
            return (A_new, jnp.concatenate([new_b1, new_b2], axis=-2) + b_j)

        def _forward(x, steps_raw, G_raw, A_raw, B_mat, C_mat, D_vec):
            steps = jax.nn.sigmoid(steps_raw)
            G_diag = jax.nn.relu(G_raw)
            A_diag = jax.nn.relu(A_raw)
            Bu = jnp.einsum('blh,pht->blpt', x, B_mat)
            S = 1.0 + steps * G_diag
            alpha = steps ** 2 * A_diag / S
            alpha = 1.99 * jnp.tanh(alpha / 1.99)
            M = jnp.concatenate([1.0 / S, -alpha / steps, steps / S, 1.0 - alpha])
            M_exp = jnp.broadcast_to(M, (x.shape[0], x.shape[1], 4 * steps.shape[0]))
            step_b = steps[None, None, :, None]
            S_b = S[None, None, :, None]
            F1 = step_b * (1.0 / S_b) * Bu
            F2 = step_b ** 2 * (1.0 / S_b) * Bu
            F_mat = jnp.concatenate([F1, F2], axis=-2)
            _, xs = jax.lax.associative_scan(_binary_operator, (M_exp, F_mat), axis=1)
            ys = xs[..., steps.shape[0]:, :]
            Cy = jnp.einsum('blpt,hpt->blht', ys, C_mat)
            return Cy[..., 0] - Cy[..., 1] + x * D_vec
        key = jax.random.key(seed)
        k1, k2, k3, k4, k5, k6, k7 = jax.random.split(key, 7)
        x = jax.random.normal(k1, (B, L, H), dtype=jnp.float32)
        steps_raw = 0.5 * jax.random.normal(k2, (P,), dtype=jnp.float32)
        steps = jax.nn.sigmoid(steps_raw)
        mags = jnp.sqrt(jax.random.uniform(k3, (P,)) * (R_MAX ** 2 - R_MIN ** 2) + R_MIN ** 2)
        G_raw = (1.0 - mags ** 2) / (steps * mags ** 2)
        theta = jax.random.uniform(k4, (P,)) * THETA_MAX
        A_raw = _map_theta_to_A(theta, jax.nn.relu(G_raw), steps)
        std_b = 1.0 / math.sqrt(H)
        B_mat = jax.random.uniform(k5, (P, H, 2), minval=-std_b, maxval=std_b, dtype=jnp.float32)
        std_c = 1.0 / math.sqrt(P)
        C_mat = jax.random.uniform(k6, (H, P, 2), minval=-std_c, maxval=std_c, dtype=jnp.float32)
        D_vec = jax.random.normal(k7, (H,), dtype=jnp.float32)
        return {'input_sequence': x, 'steps_raw': steps_raw, 'G_raw': G_raw, 'A_raw': A_raw, 'B_mat': B_mat, 'C_mat': C_mat, 'D_vec': D_vec}
    _L0_attn_in = _L0_attn_setup()

    def _L0_ffn_setup():
        import jax, jax.numpy as jnp
        import numpy as np
        MAX_VAL = 100.0
        key = jax.random.key(seed)
        k1, k2, k3 = jax.random.split(key, 3)
        B, S, D_IN, D_OUT = (4, 2048, 256, 256)
        x = jax.random.normal(k1, (B, S, D_IN), dtype=jnp.float32)
        weights = jax.random.normal(k2, (D_OUT, D_IN), dtype=jnp.float32)
        scale = jnp.ones((D_OUT,), dtype=jnp.float32)
        bias = jax.random.normal(k3, (D_OUT,), dtype=jnp.float32)
        return {'x': x, 'weights': weights, 'scale': scale, 'bias': bias}
    _L0_ffn_in = _L0_ffn_setup()

    def _L1_attn_setup():
        import jax, jax.numpy as jnp
        import numpy as np
        import math
        D_MODEL = 256
        N_HEADS = 16
        HEAD_DIM = D_MODEL // N_HEADS
        BATCH = 2
        SEQ = 512

        def _get_slopes(n_heads):

            def p2(n):
                start = 2.0 ** (-8.0 / n)
                return [start * start ** i for i in range(n)]
            if math.log2(n_heads).is_integer():
                return jnp.asarray(p2(n_heads), dtype=jnp.float32)
            cp = 2 ** math.floor(math.log2(n_heads))
            extra = p2(2 * cp)[::2][:n_heads - cp]
            return jnp.asarray(p2(cp) + extra, dtype=jnp.float32)
        key = jax.random.key(seed)
        k1, k2, k3 = jax.random.split(key, 3)
        x = jax.random.normal(k1, (BATCH, SEQ, D_MODEL), dtype=jnp.float32)
        W_qkv = jax.random.normal(k2, (D_MODEL, 3 * D_MODEL), dtype=jnp.float32) * D_MODEL ** (-0.5)
        b_qkv = jnp.zeros((3 * D_MODEL,), dtype=jnp.float32)
        W_out = jax.random.normal(k3, (D_MODEL, D_MODEL), dtype=jnp.float32) * D_MODEL ** (-0.5)
        b_out = jnp.zeros((D_MODEL,), dtype=jnp.float32)
        return {'x': x, 'W_qkv': W_qkv, 'b_qkv': b_qkv, 'W_out': W_out, 'b_out': b_out}
    _L1_attn_in = _L1_attn_setup()

    def _L1_ffn_setup():
        import jax, jax.numpy as jnp
        import numpy as np
        HID = 256
        NH = 16
        NKV = 4
        HD = HID // NH
        E = 8
        TOPK = 2
        FFN = 512
        EPS = 1e-05
        THETA = 10000.0

        def _rmsnorm(x, w):
            var = jnp.mean(x * x, axis=-1, keepdims=True)
            return x * jax.lax.rsqrt(var + EPS) * w

        def _rope_tables(S):
            inv_freq = 1.0 / THETA ** (jnp.arange(0, HD, 2, dtype=jnp.float32) / HD)
            freqs = jnp.arange(S, dtype=jnp.float32)[:, None] * inv_freq[None, :]
            emb = jnp.concatenate([freqs, freqs], axis=-1)
            return (jnp.cos(emb), jnp.sin(emb))

        def _apply_rope(t, cos, sin):
            t1, t2 = jnp.split(t, 2, axis=-1)
            rot = jnp.concatenate([-t2, t1], axis=-1)
            return t * cos[None, :, None, :] + rot * sin[None, :, None, :]
        key = jax.random.key(seed)
        ks = jax.random.split(key, 6)
        B, S = (1, 512)
        x = jax.random.normal(ks[0], (B, S, HID), dtype=jnp.float32)
        wqkv = jax.random.normal(ks[1], ((NH + 2 * NKV) * HD, HID), dtype=jnp.float32) * 0.02
        wo = jax.random.normal(ks[2], (HID, NH * HD), dtype=jnp.float32) * 0.02
        gate_w = jax.random.normal(ks[3], (E, HID), dtype=jnp.float32) * 0.02
        w13 = jax.random.normal(ks[4], (E, 2 * FFN, HID), dtype=jnp.float32) * 0.02
        w2 = jax.random.normal(ks[5], (E, HID, FFN), dtype=jnp.float32) * 0.02
        return {'x': x, 'ln1_w': jnp.ones((HID,), jnp.float32), 'ln2_w': jnp.ones((HID,), jnp.float32), 'wqkv': wqkv, 'wo': wo, 'gate_w': gate_w, 'w13': w13, 'w2': w2}
    _L1_ffn_in = _L1_ffn_setup()
    _d = {'L0_attn_input_sequence': _L0_attn_in['input_sequence'], 'L0_attn_steps_raw': _L0_attn_in['steps_raw'], 'L0_attn_G_raw': _L0_attn_in['G_raw'], 'L0_attn_A_raw': _L0_attn_in['A_raw'], 'L0_attn_B_mat': _L0_attn_in['B_mat'], 'L0_attn_C_mat': _L0_attn_in['C_mat'], 'L0_attn_D_vec': _L0_attn_in['D_vec'], 'L0_ffn_weights': _L0_ffn_in['weights'], 'L0_ffn_scale': _L0_ffn_in['scale'], 'L0_ffn_bias': _L0_ffn_in['bias'], 'L1_attn_W_qkv': _L1_attn_in['W_qkv'], 'L1_attn_b_qkv': _L1_attn_in['b_qkv'], 'L1_attn_W_out': _L1_attn_in['W_out'], 'L1_attn_b_out': _L1_attn_in['b_out'], 'L1_ffn_ln1_w': _L1_ffn_in['ln1_w'], 'L1_ffn_ln2_w': _L1_ffn_in['ln2_w'], 'L1_ffn_wqkv': _L1_ffn_in['wqkv'], 'L1_ffn_wo': _L1_ffn_in['wo'], 'L1_ffn_gate_w': _L1_ffn_in['gate_w'], 'L1_ffn_w13': _L1_ffn_in['w13'], 'L1_ffn_w2': _L1_ffn_in['w2']}
    _x0 = _d['L0_attn_input_sequence']
    _d['L0_attn_input_sequence'] = jax.random.normal(jax.random.fold_in(jax.random.key(seed), 1), (2, 2048, 256), dtype=_x0.dtype)
    del _x0
    return _d

def reference(L0_attn_input_sequence, L0_attn_steps_raw, L0_attn_G_raw, L0_attn_A_raw, L0_attn_B_mat, L0_attn_C_mat, L0_attn_D_vec, L0_ffn_weights, L0_ffn_scale, L0_ffn_bias, L1_attn_W_qkv, L1_attn_b_qkv, L1_attn_W_out, L1_attn_b_out, L1_ffn_ln1_w, L1_ffn_ln2_w, L1_ffn_wqkv, L1_ffn_wo, L1_ffn_gate_w, L1_ffn_w13, L1_ffn_w2):

    def _L0_attn_ref(input_sequence, steps_raw, G_raw, A_raw, B_mat, C_mat, D_vec):
        import jax, jax.numpy as jnp
        import numpy as np
        import math
        P = 64
        H = 256
        B = 8
        L = 1024
        R_MIN, R_MAX, THETA_MAX = (0.9, 0.999, math.pi)

        def _map_theta_to_A(thetas, G_diag, steps):
            cos_t = jnp.cos(thetas)
            tan_sq = jnp.tan(thetas) ** 2
            sqrt_term = 4.0 * jnp.sqrt(steps ** 4 / cos_t ** 2 + steps ** 5 * G_diag / cos_t ** 2)
            common = steps ** 2 * (-4.0 - 2.0 * steps * G_diag - 4.0 * tan_sq - 2.0 * steps * G_diag * tan_sq)
            denom = 2.0 * steps ** 4 * (1.0 + tan_sq)
            A_plus = (sqrt_term - common) / denom
            A_minus = (-sqrt_term - common) / denom
            return jnp.where(thetas > math.pi / 2, A_plus, A_minus)

        def _binary_operator(q_i, q_j):
            A_i, b_i = q_i
            A_j, b_j = q_j
            iA, iB, iC, iD = jnp.split(A_i, 4, axis=-1)
            jA, jB, jC, jD = jnp.split(A_j, 4, axis=-1)
            A_new = jnp.concatenate([jA * iA + jB * iC, jA * iB + jB * iD, jC * iA + jD * iC, jC * iB + jD * iD], axis=-1)
            b_i1, b_i2 = jnp.split(b_i, 2, axis=-2)
            new_b1 = jA[..., None] * b_i1 + jB[..., None] * b_i2
            new_b2 = jC[..., None] * b_i1 + jD[..., None] * b_i2
            return (A_new, jnp.concatenate([new_b1, new_b2], axis=-2) + b_j)

        def _forward(x, steps_raw, G_raw, A_raw, B_mat, C_mat, D_vec):
            steps = jax.nn.sigmoid(steps_raw)
            G_diag = jax.nn.relu(G_raw)
            A_diag = jax.nn.relu(A_raw)
            Bu = jnp.einsum('blh,pht->blpt', x, B_mat)
            S = 1.0 + steps * G_diag
            alpha = steps ** 2 * A_diag / S
            alpha = 1.99 * jnp.tanh(alpha / 1.99)
            M = jnp.concatenate([1.0 / S, -alpha / steps, steps / S, 1.0 - alpha])
            M_exp = jnp.broadcast_to(M, (x.shape[0], x.shape[1], 4 * steps.shape[0]))
            step_b = steps[None, None, :, None]
            S_b = S[None, None, :, None]
            F1 = step_b * (1.0 / S_b) * Bu
            F2 = step_b ** 2 * (1.0 / S_b) * Bu
            F_mat = jnp.concatenate([F1, F2], axis=-2)
            _, xs = jax.lax.associative_scan(_binary_operator, (M_exp, F_mat), axis=1)
            ys = xs[..., steps.shape[0]:, :]
            Cy = jnp.einsum('blpt,hpt->blht', ys, C_mat)
            return Cy[..., 0] - Cy[..., 1] + x * D_vec
        return _forward(input_sequence, steps_raw, G_raw, A_raw, B_mat, C_mat, D_vec)

    def _L0_ffn_ref(x, weights, scale, bias):
        import jax, jax.numpy as jnp
        import numpy as np
        MAX_VAL = 100.0
        w = (weights >= 0.0).astype(x.dtype) * 2.0 - 1.0
        y = jnp.einsum('bsi,oi->bso', x, w)
        y = y * scale + bias
        y = jnp.clip(y, -MAX_VAL, MAX_VAL)
        return y

    def _L1_attn_ref(x, W_qkv, b_qkv, W_out, b_out):
        import jax, jax.numpy as jnp
        import numpy as np
        import math
        D_MODEL = 256
        N_HEADS = 16
        HEAD_DIM = D_MODEL // N_HEADS
        BATCH = 2
        SEQ = 512

        def _get_slopes(n_heads):

            def p2(n):
                start = 2.0 ** (-8.0 / n)
                return [start * start ** i for i in range(n)]
            if math.log2(n_heads).is_integer():
                return jnp.asarray(p2(n_heads), dtype=jnp.float32)
            cp = 2 ** math.floor(math.log2(n_heads))
            extra = p2(2 * cp)[::2][:n_heads - cp]
            return jnp.asarray(p2(cp) + extra, dtype=jnp.float32)
        B, S, D = x.shape
        H, hd = (N_HEADS, HEAD_DIM)
        qkv = x @ W_qkv + b_qkv
        qkv = qkv.reshape(B, S, 3, H, hd).transpose(2, 0, 3, 1, 4)
        Q, K, V = (qkv[0], qkv[1], qkv[2])
        scores = jnp.einsum('bhqd,bhkd->bhqk', Q, K) / math.sqrt(hd)
        pos = jnp.arange(S)
        rel = pos[None, :] - pos[:, None]
        slopes = _get_slopes(H)
        alibi = slopes[:, None, None] * rel.astype(jnp.float32)
        scores = scores + alibi[None]
        causal = rel <= 0
        scores = jnp.where(causal[None, None], scores, -jnp.inf)
        attn = jax.nn.softmax(scores, axis=-1)
        out = jnp.einsum('bhqk,bhkd->bqhd', attn, V).reshape(B, S, D)
        return out @ W_out + b_out

    def _L1_ffn_ref(x, ln1_w, ln2_w, wqkv, wo, gate_w, w13, w2):
        import jax, jax.numpy as jnp
        import numpy as np
        HID = 256
        NH = 16
        NKV = 4
        HD = HID // NH
        E = 8
        TOPK = 2
        FFN = 512
        EPS = 1e-05
        THETA = 10000.0

        def _rmsnorm(x, w):
            var = jnp.mean(x * x, axis=-1, keepdims=True)
            return x * jax.lax.rsqrt(var + EPS) * w

        def _rope_tables(S):
            inv_freq = 1.0 / THETA ** (jnp.arange(0, HD, 2, dtype=jnp.float32) / HD)
            freqs = jnp.arange(S, dtype=jnp.float32)[:, None] * inv_freq[None, :]
            emb = jnp.concatenate([freqs, freqs], axis=-1)
            return (jnp.cos(emb), jnp.sin(emb))

        def _apply_rope(t, cos, sin):
            t1, t2 = jnp.split(t, 2, axis=-1)
            rot = jnp.concatenate([-t2, t1], axis=-1)
            return t * cos[None, :, None, :] + rot * sin[None, :, None, :]
        B, S, _ = x.shape
        h = _rmsnorm(x, ln1_w)
        qkv = jnp.einsum('bsh,oh->bso', h, wqkv)
        q = qkv[..., :NH * HD].reshape(B, S, NH, HD)
        k = qkv[..., NH * HD:(NH + NKV) * HD].reshape(B, S, NKV, HD)
        v = qkv[..., (NH + NKV) * HD:].reshape(B, S, NKV, HD)
        cos, sin = _rope_tables(S)
        q = _apply_rope(q, cos, sin)
        k = _apply_rope(k, cos, sin)
        groups = NH // NKV
        k = jnp.repeat(k, groups, axis=2)
        v = jnp.repeat(v, groups, axis=2)
        scale = HD ** (-0.5)
        scores = jnp.einsum('bqhd,bkhd->bhqk', q, k) * scale
        causal = jnp.tril(jnp.ones((S, S), dtype=bool))
        scores = jnp.where(causal[None, None], scores, jnp.finfo(scores.dtype).min)
        probs = jax.nn.softmax(scores, axis=-1)
        attn = jnp.einsum('bhqk,bkhd->bqhd', probs, v).reshape(B, S, NH * HD)
        x = x + jnp.einsum('bso,ho->bsh', attn, wo)
        h = _rmsnorm(x, ln2_w).reshape(-1, HID)
        T = h.shape[0]
        logits = jnp.einsum('th,eh->te', h, gate_w)
        rprobs = jax.nn.softmax(logits.astype(jnp.float32), axis=-1)
        topw, topi = jax.lax.top_k(rprobs, TOPK)
        topw = topw / jnp.sum(topw, axis=-1, keepdims=True)
        wfull = jnp.zeros((T, E), jnp.float32).at[jnp.arange(T)[:, None], topi].set(topw)
        wfull = wfull.astype(h.dtype)
        out = jnp.zeros((T, HID), h.dtype)
        for e in range(E):
            w1 = w13[e, :FFN]
            w3 = w13[e, FFN:]
            g = jax.nn.silu(h @ w1.T) * (h @ w3.T)
            out = out + jnp.einsum('tf,hf->th', g, w2[e]) * wfull[:, e:e + 1]
        return x + out.reshape(B, S, HID)
    x = L0_attn_input_sequence
    xn = _layernorm(x, axis=-1)
    x = x + _L0_attn_ref(xn, L0_attn_steps_raw, L0_attn_G_raw, L0_attn_A_raw, L0_attn_B_mat, L0_attn_C_mat, L0_attn_D_vec) + _L0_ffn_ref(xn, L0_ffn_weights, L0_ffn_scale, L0_ffn_bias)
    xn = _layernorm(x, axis=-1)
    x = x + _L1_attn_ref(xn, L1_attn_W_qkv, L1_attn_b_qkv, L1_attn_W_out, L1_attn_b_out) + _L1_ffn_ref(xn, L1_ffn_ln1_w, L1_ffn_ln2_w, L1_ffn_wqkv, L1_ffn_wo, L1_ffn_gate_w, L1_ffn_w13, L1_ffn_w2)
    return x

_drawn_inputs = setup_inputs


def setup_inputs(seed=0):
    import zlib

    import numpy as np

    out = dict(_drawn_inputs(seed))
    spreads = {'L0_ffn_scale': (1.0, 0.2),
     'L1_attn_b_qkv': (0.0, 0.8),
     'L1_attn_b_out': (0.0, 2.0),
     'L1_ffn_ln1_w': (1.0, 0.6),
     'L1_ffn_ln2_w': (1.0, 0.6)}
    factors = {'L1_attn_W_qkv': 2.886,
     'L1_attn_W_out': 2.787,
     'L1_ffn_wqkv': 8.0,
     'L1_ffn_wo': 8.0,
     'L1_ffn_gate_w': 8.0,
     'L1_ffn_w13': 8.0,
     'L1_ffn_w2': 8.0}
    for name, (base, spread) in spreads.items():
        noise = np.random.default_rng([zlib.crc32(name.encode()), seed]).standard_normal(out[name].shape)
        drawn = base * np.exp(spread * noise) if base else spread * noise
        out[name] = jnp.asarray(drawn.astype(out[name].dtype))
    for name, factor in factors.items():
        out[name] = (out[name] * factor).astype(out[name].dtype)
    return out
```

```python
from contextlib import ExitStack

import concourse.bass as bass
from concourse import mybir

ALU = mybir.AluOpType
ACT = mybir.ActivationFunctionType
AX = mybir.AxisListType
F32 = mybir.dt.float32
BF16 = mybir.dt.bfloat16
ds = bass.ds

P = 128
B, L, D = 2, 2048, 256
TOK = B * L
KD = D // P
TPB = 4
BT = TPB * P
NBLK = TOK // BT
LN_EPS = 1e-5
CHUNK = 32
NCH = L // CHUNK
LOCAL_LEVELS = 5
CARRY_LEVELS = 6
NPOW = LOCAL_LEVELS + CARRY_LEVELS
CLIP = 100.0
HEADS, HD = 16, 16
GH = 4
NG = HEADS // GH
NGB = B * NG
KV = 4
VW = 32
AUG = 15
PROD_Q = (0, 0, 1, 1, 0, 2)
PROD_K = (0, 1, 0, 1, 2, 0)
NPROD = len(PROD_Q)
ROWS = AUG + NPROD * HD
MROW = 12
MASKED = -1e30
NE, FFN = 8, 512
FT = FFN // P
SCALE = HD ** -0.5


class Chain:

    def __init__(self, eng, sem):
        self.eng, self.sem, self.start, self.n = eng, sem, 0, 0

    def did(self, ins):
        ins.then_inc(self.sem, 1)
        self.n += 1

    def settle(self):
        self.eng.wait_ge(self.sem, self.start + self.n)

    def enter(self, i, per):
        self.first, self.per = self.start + self.n, per
        self.start, self.n = i * per + self.first, 0

    def leave(self, times):
        assert self.n == self.per, (self.n, self.per)
        self.start, self.n = self.first + times * self.per, 0


def front(nc, A, M):
    with ExitStack() as ctx:
        def sb(name, shape, dt=F32):
            return ctx.enter_context(nc.sbuf_tensor(name, shape, dt))

        def sem(name):
            return nc.alloc_semaphore(name)

        x_in = [sb(f"f_x{s}", [P, TPB, D]) for s in range(2)]
        xn = [sb(f"f_xn{s}", [P, TPB, D]) for s in range(2)]
        stats = sb("f_stats", [P, TPB, 6])
        rs_pad = sb("f_pad", [P, 1])
        mv = sb("f_mv", [P, TPB, 2])
        sd = sb("f_sd", [P, TPB])
        rs = sb("f_rs", [P, TPB])
        b_mat = sb("f_bmat", [P, KD, P])
        par = sb("f_par", [P, 3])
        cf = sb("f_cf", [P, 16])
        tmp = sb("f_tmp", [P, 16])
        tr = [M["ps"][k] for k in range(KD)]
        bu = M["ps"][2]
        ident, xnT, f1, f2, pw = M["ident"], M["xnT"], M["f1"], M["f2"], M["pw"]
        s_const, s_const2 = sem("front_consts_loaded"), sem("front_params_loaded")
        s_x = [sem(f"front_x_loaded{s}") for s in range(2)]
        s_xfree = sem("front_x_free")
        s_var, s_sd = sem("front_var_ready"), sem("front_sd_ready")
        s_xn, s_tr = sem("front_xn_ready"), sem("front_transposed")
        s_xnT, s_bu, s_f = sem("front_xnT_ready"), sem("front_bu_ready"), sem("front_bu_scaled")
        s_dve, s_exp, s_arg, s_tanh, s_cf = (sem("front_dve"), sem("front_exp"), sem("front_tanh_arg"),
                                             sem("front_tanh"), sem("front_coefs"))
        AHEAD = 2 * KD
        x_d = A["x"].rearrange("b (n p) d -> p (b n) d", p=P)
        block = ctx.enter_context(nc.Block())

        @block.sync
        def _(sp):
            for c, name in enumerate(("steps", "G", "A")):
                for half in range(2):
                    sp.dma_start(par[64 * half:64 * half + 64, c:c + 1],
                                 A[name].rearrange("(p a) -> p a", a=1)).then_inc(s_const2, 16)
            with sp.Fori(0, NBLK // 2) as ip:
                for s in range(2):
                    sp.wait_ge(s_xfree, ip * 2 + (s + 1))
                    sp.dma_start(x_in[s][:, :, :], x_d[:, ds((ip * 2 + s) * TPB, TPB), :]).then_inc(s_x[s], 16)

        @block.gpsimd
        def _(pool):
            pool.dma_start(ident[:, :], A["c_ident"]).then_inc(s_const, 16)
            pool.dma_start(b_mat[:, :, :], A["b_mat"].rearrange("(k p) m -> p k m", p=P)).then_inc(s_const, 16)

        C = {n: cf[:, i:i + 1] for i, n in enumerate(
            ("e", "e1", "step", "G", "A", "sg", "S", "iS", "s2", "al", "z", "th", "c1", "c2"))}

        @block.scalar
        def _(act):
            act.sem_inc(s_f, 2)
            act.wait_ge(s_const2, 96)
            nc.scalar.activation(C["e"], par[:, 0:1], ACT.Exp, scale=-1.0).then_inc(s_exp, 1)
            act.wait_ge(s_arg, 1)
            nc.scalar.activation(C["th"], C["z"], ACT.Tanh, scale=1.0 / 1.99).then_inc(s_tanh, 1)
            act.wait_ge(s_cf, 1)
            with act.Fori(0, NBLK // 2) as ip:
                for s in range(2):
                    blk = ip * 2 + s
                    act.wait_ge(s_var, blk + 1)
                    nc.scalar.activation(sd[:, :], mv[:, :, 1], ACT.Sqrt).then_inc(s_sd, 1)
                    for k in range(KD):
                        act.wait_ge(s_tr, blk * KD + (AHEAD + k + 1))
                        nc.scalar.activation(xnT[:, k, ds(blk * BT, BT)], tr[k][:, :], ACT.Copy).then_inc(s_xnT, 1)
                    act.wait_ge(s_bu, blk + 1)
                    nc.scalar.activation(f1[:, ds(blk * BT, BT)], bu[:, :], ACT.Copy,
                                         scale=C["c1"]).then_inc(s_f, 1)
                    nc.scalar.activation(f2[:, ds(blk * BT, BT)], bu[:, :], ACT.Copy,
                                         scale=C["c2"]).then_inc(s_f, 1)

        @block.tensor
        def _(pe):
            pe.sem_inc(s_tr, AHEAD)
            pe.wait_ge(s_const, 32)
            with pe.Fori(0, NBLK // 2) as ip:
                for s in range(2):
                    blk = ip * 2 + s
                    pe.wait_ge(s_xn, blk + 1)
                    for k in range(KD):
                        for j in range(TPB):
                            ins = pe.transpose(tr[k][:, j * P:(j + 1) * P], xn[s][:, j, k * P:(k + 1) * P],
                                               ident[:, :])
                        ins.then_inc(s_tr, 1)
                    pe.wait_ge(s_xnT, blk * KD + KD)
                    pe.wait_ge(s_f, blk * 2 + 2)
                    for k in range(KD):
                        ins = pe.matmul(bu[:, :], b_mat[:, k, :], xnT[:, k, ds(blk * BT, BT)],
                                        start=(k == 0), stop=(k == KD - 1))
                    ins.then_inc(s_bu, 1)

        @block.vector
        def _(dve):
            ch = Chain(dve, s_dve)
            dve.sem_inc(s_xfree, 2)
            v = nc.vector
            dve.wait_ge(s_exp, 1)
            ch.did(v.tensor_scalar(C["e1"], C["e"], 1.0, None, ALU.add))
            ch.did(v.tensor_scalar(C["G"], par[:, 1:2], 0.0, None, ALU.max))
            ch.did(v.tensor_scalar(C["A"], par[:, 2:3], 0.0, None, ALU.max))
            ch.settle()
            ch.did(v.reciprocal(C["step"], C["e1"]))
            ch.settle()
            ch.did(v.tensor_tensor(C["sg"], C["step"], C["G"], ALU.mult))
            ch.did(v.tensor_tensor(C["s2"], C["step"], C["step"], ALU.mult))
            ch.settle()
            ch.did(v.tensor_scalar(C["S"], C["sg"], 1.0, None, ALU.add))
            ch.did(v.tensor_tensor(C["al"], C["s2"], C["A"], ALU.mult))
            ch.settle()
            ch.did(v.reciprocal(C["iS"], C["S"]))
            ch.settle()
            v.tensor_tensor(C["z"], C["al"], C["iS"], ALU.mult).then_inc(s_arg, 1)
            ch.did(v.tensor_tensor(C["c1"], C["step"], C["iS"], ALU.mult))
            ch.settle()
            ch.did(v.tensor_tensor(C["c2"], C["step"], C["c1"], ALU.mult))
            ch.did(v.tensor_copy(pw[:, 0, 0:1], C["iS"]))
            ch.did(v.tensor_copy(pw[:, 0, 2:3], C["c1"]))
            dve.wait_ge(s_tanh, 1)
            ch.did(v.tensor_scalar(pw[:, 0, 3:4], C["th"], -1.99, 1.0, ALU.mult, ALU.add))
            ch.did(v.scalar_tensor_tensor(pw[:, 0, 1:2], C["th"], -1.99, C["e1"], ALU.mult, ALU.mult))
            ch.settle()
            for n in range(1, NPOW):
                a, b, c, d = (pw[:, n - 1, i:i + 1] for i in range(4))
                bc, trc = tmp[:, 0:1], tmp[:, 1:2]
                ch.did(v.tensor_tensor(bc, b, c, ALU.mult))
                ch.did(v.tensor_tensor(trc, a, d, ALU.add))
                ch.settle()
                ch.did(v.scalar_tensor_tensor(pw[:, n, 0:1], a, a, bc, ALU.mult, ALU.add))
                ch.did(v.scalar_tensor_tensor(pw[:, n, 3:4], d, d, bc, ALU.mult, ALU.add))
                ch.did(v.tensor_tensor(pw[:, n, 1:2], b, trc, ALU.mult))
                ch.did(v.tensor_tensor(pw[:, n, 2:3], c, trc, ALU.mult))
                ch.settle()
            r1, r2 = M["r1"], M["r2"]
            ch.did(v.tensor_copy(r1[:, 0:1], pw[:, 0, 2:3]))
            ch.did(v.tensor_copy(r2[:, 0:1], pw[:, 0, 3:4]))
            ch.settle()
            for n in range(LOCAL_LEVELS):
                w = 1 << n
                a, b, c, d = (pw[:, n, i:i + 1] for i in range(4))
                t = M["rtmp"]
                ch.did(v.tensor_scalar(t[:, 0, 0:w], r2[:, 0:w], c, None, ALU.mult))
                ch.did(v.tensor_scalar(t[:, 1, 0:w], r2[:, 0:w], d, None, ALU.mult))
                ch.settle()
                ch.did(v.scalar_tensor_tensor(r1[:, w:2 * w], r1[:, 0:w], a, t[:, 0, 0:w], ALU.mult, ALU.add))
                ch.did(v.scalar_tensor_tensor(r2[:, w:2 * w], r1[:, 0:w], b, t[:, 1, 0:w], ALU.mult, ALU.add))
                ch.settle()
            dve.sem_inc(s_cf, 1)
            with dve.Fori(0, NBLK // 2) as ip:
                ch.enter(ip, 2 * (2 * TPB + 1))
                for s in range(2):
                    blk = ip * 2 + s
                    dve.wait_ge(s_x[s], ip * 16 + 16)
                    for j in range(TPB):
                        ch.did(v.bn_stats(stats[:, j, :], x_in[s][:, j, :]))
                    ch.settle()
                    v.tensor_copy(rs_pad[:, :], stats[:, 0, 0:1])
                    for j in range(TPB):
                        ch.did(v.bn_aggr(mv[:, j, :], stats[:, j, :]))
                    ch.settle()
                    v.tensor_scalar(mv[:, :, 1], mv[:, :, 1], LN_EPS, None, ALU.add).then_inc(s_var, 1)
                    dve.wait_ge(s_sd, blk + 1)
                    ch.did(v.reciprocal(rs[:, :], sd[:, :]))
                    ch.settle()
                    dve.wait_ge(s_tr, blk * KD + (AHEAD - KD))
                    for j in range(TPB):
                        ins = v.tensor_scalar(xn[s][:, j, :], x_in[s][:, j, :], mv[:, j, 0:1], rs[:, j:j + 1],
                                              ALU.subtract, ALU.mult)
                    ins.then_inc(s_xn, 1)
                    dve.wait_ge(s_xn, blk + 1)
                    dve.sem_inc(s_xfree, 1)
            ch.leave(NBLK // 2)


def recurrence(nc, A, M):
    f1, f2, pw, r1, r2 = M["f1"], M["f2"], M["pw"], M["r1"], M["r2"]
    with ExitStack() as ctx:
        def sb(name, shape, dt=F32):
            return ctx.enter_context(nc.sbuf_tensor(name, shape, dt))

        t1 = sb("r_t1", [P, B * NCH])
        t2 = sb("r_t2", [P, B * NCH])
        g = [[sb(f"r_g{i}{c}", [P, B, NCH]) for c in range(2)] for i in range(2)]
        s_dve = nc.alloc_semaphore("rec_dve")
        block = ctx.enter_context(nc.Block())
        f1v = f1[:, :].rearrange("p (c i) -> p c i", i=CHUNK)
        f2v = f2[:, :].rearrange("p (c i) -> p c i", i=CHUNK)
        y = f2[:, :].rearrange("p (b c i) -> p b c i", b=B, i=CHUNK)

        @block.vector
        def _(dve):
            ch = Chain(dve, s_dve)
            v = nc.vector
            a, b, c, d = (pw[:, 0, i:i + 1] for i in range(4))
            with dve.Fori(0, CHUNK - 1) as i:
                ch.enter(i, 4)
                p1, p2 = f1v[:, :, ds(i, 1)], f2v[:, :, ds(i, 1)]
                n1, n2 = f1v[:, :, ds(i + 1, 1)], f2v[:, :, ds(i + 1, 1)]
                u1, u2 = (t[:, :].rearrange("p (c o) -> p c o", o=1) for t in (t1, t2))
                ch.did(v.scalar_tensor_tensor(u1, p2, b, n1, ALU.mult, ALU.add))
                ch.did(v.scalar_tensor_tensor(u2, p2, d, n2, ALU.mult, ALU.add))
                ch.settle()
                ch.did(v.scalar_tensor_tensor(n1, p1, a, u1, ALU.mult, ALU.add))
                ch.did(v.scalar_tensor_tensor(n2, p1, c, u2, ALU.mult, ALU.add))
                ch.settle()
            ch.leave(CHUNK - 1)
            fv = f1[:, :].rearrange("p (b c i) -> p b c i", b=B, i=CHUNK)
            ch.did(v.tensor_copy(g[0][0][:, :, :], fv[:, :, :, CHUNK - 1]))
            ch.did(v.tensor_copy(g[0][1][:, :, :], y[:, :, :, CHUNK - 1]))
            ch.settle()
            for lev in range(CARRY_LEVELS):
                w = 1 << lev
                a, b, c, d = (pw[:, LOCAL_LEVELS + lev, i:i + 1] for i in range(4))
                old, new = g[lev % 2], g[1 - lev % 2]
                u1 = t1[:, :].rearrange("p (b c) -> p b c", b=B)[:, :, w:]
                u2 = t2[:, :].rearrange("p (b c) -> p b c", b=B)[:, :, w:]
                ch.did(v.scalar_tensor_tensor(u1, old[1][:, :, 0:NCH - w], b, old[0][:, :, w:], ALU.mult, ALU.add))
                ch.did(v.scalar_tensor_tensor(u2, old[1][:, :, 0:NCH - w], d, old[1][:, :, w:], ALU.mult, ALU.add))
                ch.did(v.tensor_copy(new[0][:, :, 0:w], old[0][:, :, 0:w]))
                ch.did(v.tensor_copy(new[1][:, :, 0:w], old[1][:, :, 0:w]))
                ch.settle()
                ch.did(v.scalar_tensor_tensor(new[0][:, :, w:], old[0][:, :, 0:NCH - w], a, u1, ALU.mult, ALU.add))
                ch.did(v.scalar_tensor_tensor(new[1][:, :, w:], old[0][:, :, 0:NCH - w], c, u2, ALU.mult, ALU.add))
                ch.settle()
            g1, g2 = g[CARRY_LEVELS % 2]
            with dve.Fori(0, CHUNK // 4) as i4:
                ch.enter(i4, 8)
                for o in range(4):
                    yi = y[:, :, 1:, ds(i4 * 4 + o, 1)].rearrange("p b c o -> p b (c o)")
                    ch.did(v.scalar_tensor_tensor(yi, g1[:, :, 0:NCH - 1], r1[:, ds(i4 * 4 + o, 1)], yi,
                                                  ALU.mult, ALU.add))
                ch.settle()
                for o in range(4):
                    yi = y[:, :, 1:, ds(i4 * 4 + o, 1)].rearrange("p b c o -> p b (c o)")
                    ch.did(v.scalar_tensor_tensor(yi, g2[:, :, 0:NCH - 1], r2[:, ds(i4 * 4 + o, 1)], yi,
                                                  ALU.mult, ALU.add))
            ch.leave(CHUNK // 4)


def middle(nc, A, M):
    with ExitStack() as ctx:
        def sb(name, shape, dt=F32):
            return ctx.enter_context(nc.sbuf_tensor(name, shape, dt))

        def sem(name):
            return nc.alloc_semaphore(name)

        ps, ident, xnT, y = M["ps"], M["ident"], M["xnT"], M["f2"]
        x_in = [sb(f"m_x{s}", [P, TPB, D]) for s in range(2)]
        x1 = [sb(f"m_x1{s}", [P, TPB, D]) for s in range(2)]
        xn2 = [sb(f"m_xn2{s}", [P, TPB, D]) for s in range(2)]
        h = sb("m_h", [P, TPB, D])
        u = sb("m_u", [P, KD, BT])
        f = sb("m_f", [P, KD, BT])
        fs = sb("m_fs", [P, KD, BT])
        xT = sb("m_xT", [P, KD, BT])
        hT = sb("m_hT", [P, KD, BT])
        sq = sb("m_sq", [P, TPB, D])
        stats = sb("m_stats", [P, TPB, 6])
        rs_pad = sb("m_pad", [P, 1])
        mv = sb("m_mv", [P, TPB, 2])
        ms = sb("m_ms", [P, TPB])
        msv = sb("m_msv", [P, TPB])
        sd = sb("m_sd", [P, 2, TPB])
        rs = sb("m_rs", [P, 2, TPB])
        c_mat = sb("m_c", [P, D])
        w_raw = sb("m_wraw", [P, KD, D])
        w_sgn = sb("m_wsgn", [P, KD, D])
        cols = sb("m_cols", [P, KD, 4])
        wa = sb("m_wa", [P, KD, 3 * D])
        ba = sb("m_ba", [P, 4])
        baq = sb("m_baq", [P, KD])
        bv = sb("m_bv", [P, D])
        wb = sb("m_wb", [P, KD, 2 * D + 3 * KV * HD])
        cos, sin = sb("m_cos", [P, L]), sb("m_sin", [P, L])
        va = sb("m_va", [P, TPB, HEADS, VW])
        vb = sb("m_vb", [P, TPB, KV, VW])
        NS = 7
        xf = [sb(f"m_xf{i}", [P, BT]) for i in range(2)]
        rot = sb("m_rot", [P, BT])
        rr = [sb(f"m_rr{i}", [P, BT]) for i in range(2)]
        part = [sb(f"m_part{i}", [P, 3, BT], BF16) for i in range(2)]

        s_w = sem("mid_weights_loaded")
        s_wp = sem("mid_weights_prepared")
        s_x = [sem(f"mid_x_loaded{s}") for s in range(2)]
        s_c, s_f, s_fs = sem("mid_cy_ready"), sem("mid_ffn_ready"), sem("mid_ffn_scaled")
        s_u, s_ut = sem("mid_u_ready"), sem("mid_u_transposed")
        s_x1, s_var, s_sd, s_xn = sem("mid_x1_ready"), sem("mid_var_ready"), sem("mid_sd_ready"), sem("mid_xn_ready")
        s_sq, s_h = sem("mid_squares_summed"), sem("mid_h_ready")
        s_xt, s_xT = sem("mid_xn_transposed"), sem("mid_xT_ready")
        s_ht, s_hT = sem("mid_h_transposed"), sem("mid_hT_ready")
        s_pr, s_pa, s_pd = sem("mid_projected"), sem("mid_taken_by_act"), sem("mid_taken_by_dve")
        s_hi, s_mid, s_xf, s_r, s_lo = (sem("mid_high_part"), sem("mid_middle_part"), sem("mid_rope_ready"),
                                        sem("mid_rest"), sem("mid_low_part"))
        s_va = sem("mid_v_ready")
        s_st = [sem(f"mid_rows_stored{s}") for s in range(2)]
        s_pst = [sem(f"mid_parts_stored{i}") for i in range(2)]
        s_vst = sem("mid_v_stored")
        s_ms, s_rsd = sem("mid_mean_square"), sem("mid_rms_ready")
        s_dve, s_act, s_zero = sem("mid_dve"), sem("mid_act"), sem("mid_zeroed")
        x_d = A["x"].rearrange("b (n p) d -> p (b n) d", p=P)
        x1_d = M["x1_d"].rearrange("(n p) d -> p n d", p=P)
        xn_d = M["xn_d"].rearrange("(n p) d -> p n d", p=P)
        va_d = M["va_d"].rearrange("(n p) c -> p n c", p=P)
        vb_d = M["vb_d"].rearrange("(n p) c -> p n c", p=P)
        NW = 12
        NDVE = 6
        BANK = [6, 7, 4, 5]
        block = ctx.enter_context(nc.Block())

        @block.gpsimd
        def _(pool):
            nc.gpsimd.memset(va[:, :, :, :], 0.0)
            nc.gpsimd.memset(vb[:, :, :, :], 0.0).then_inc(s_zero, 1)
            pool.wait_ge(s_zero, 1)
            nc.gpsimd.memset(va[:, :, :, HD:HD + 1], 1.0)
            nc.gpsimd.memset(vb[:, :, :, HD:HD + 1], 1.0).then_inc(s_zero, 1)
            with pool.Fori(0, NBLK // 2) as ip:
                for s in range(2):
                    blk = ip * 2 + s
                    pool.wait_ge(s_x1, blk + 1)
                    pool.dma_start(x_in[s][:, :, :], x_d[:, ds(blk * TPB, TPB), :]).then_inc(s_x[s], 16)

        @block.sync
        def _(sp):
            for free in (*s_pst, *s_st, s_vst):
                sp.sem_inc(free, 16)
            for dst, src in ((c_mat[:, :], A["c_mat"]),
                             (w_raw[:, :, :], A["w_ffn"].rearrange("(k p) m -> p k m", p=P)),
                             (wa[:, :, :], A["w_qkv"].rearrange("(k p) m -> p k m", p=P)),
                             (wb[:, :, :], A["w_b"].rearrange("(k p) m -> p k m", p=P)),
                             (cos[:, :], A["c_cos"]), (sin[:, :], A["c_sin"]),
                             (cols[:, :, 0], A["D"].rearrange("(k p) -> p k", p=P)),
                             (cols[:, :, 1], A["scale"].rearrange("(k p) -> p k", p=P)),
                             (cols[:, :, 2], A["bias"].rearrange("(k p) -> p k", p=P)),
                             (cols[:, :, 3], A["ln1"].rearrange("(k p) -> p k", p=P)),
                             (ba[:, :], A["b_qkv"][0:2 * D].rearrange("(k p) -> p k", p=P))):
                with nc.allow_non_contiguous_dma(reason="a vector, one feature per partition"):
                    sp.dma_start(dst, src).then_inc(s_w, 16)
            sp.dma_start(bv[:, :], A["b_qkv"][2 * D:3 * D].partition_broadcast(P)).then_inc(s_w, 16)
            with sp.Fori(0, NBLK // 2) as ip:
                b = ip // 2
                for s in range(2):
                    blk = ip * 2 + s
                    tok = (ip % 2) * (2 * BT) + s * BT
                    sp.wait_ge(s_xn, blk + 1)
                    sp.dma_start(x1_d[:, ds(blk * TPB, TPB), :], x1[s][:, :, :]).then_inc(s_st[s], 16)
                    sp.dma_start(xn_d[:, ds(blk * TPB, TPB), :], xn2[s][:, :, :]).then_inc(s_st[s], 16)
                    for m in range(NS):
                        if m == 4:
                            sp.wait_ge(s_va, blk * 2 + 1)
                            sp.dma_start(va_d[:, ds(blk * TPB, TPB), :],
                                         va[:, :, :, :].rearrange("p j h c -> p j (h c)")).then_inc(s_vst, 16)
                        sp.wait_ge(s_lo, blk * NS + (m + 1))
                        i = (s * NS + m) % 2
                        if m < 6:
                            dram = (M["qa_d"], M["qa_d"], M["ka_d"], M["ka_d"], M["qb_d"], M["qb_d"])[m]
                            row, n = b * D + (m % 2) * P, P
                        else:
                            dram, row, n = M["kb_d"], b * (KV * HD), KV * HD
                        sp.dma_start(dram[:, ds(row, n), ds(tok, BT)].rearrange("a f t -> f a t"),
                                     part[i][0:n, :, :]).then_inc(s_pst[i], 16)
                    sp.wait_ge(s_va, blk * 2 + 2)
                    sp.dma_start(vb_d[:, ds(blk * TPB, TPB), :],
                                 vb[:, :, :, :].rearrange("p j h c -> p j (h c)")).then_inc(s_vst, 16)
            for i in range(2):
                sp.wait_ge(s_pst[i], NBLK * NS // 2 * 16 + 16)
                sp.wait_ge(s_st[i], NBLK // 2 * 32 + 16)
            sp.wait_ge(s_vst, NBLK * 32 + 16)

        @block.tensor
        def _(pe):
            pe.wait_ge(s_wp, 1)
            with pe.Fori(0, NBLK // 2) as ip:
                for s in range(2):
                    blk = ip * 2 + s
                    for k in range(KD):
                        pe.matmul(ps[k][:, :], c_mat[:, k * P:(k + 1) * P], y[:, ds(blk * BT, BT)],
                                  start=True, stop=True).then_inc(s_c, 1)
                    for k in range(KD):
                        for c in range(KD):
                            ins = pe.matmul(ps[2 + k][:, :], w_sgn[:, c, k * P:(k + 1) * P],
                                            xnT[:, c, ds(blk * BT, BT)], start=(c == 0), stop=(c == KD - 1))
                        ins.then_inc(s_f, 1)
                    pe.wait_ge(s_pa, blk * 4 + 4)
                    pe.wait_ge(s_pd, blk * NDVE + 1)
                    pe.wait_ge(s_u, blk * KD + KD)
                    for j in range(TPB):
                        for k in range(KD):
                            o = (j % 2) * D + k * P
                            ins = pe.transpose(ps[4 + j // 2][:, o:o + P], u[:, k, j * P:(j + 1) * P], ident[:, :])
                        if j % 2:
                            ins.then_inc(s_ut, 1)
                    pe.wait_ge(s_xn, blk + 1)
                    for k in range(KD):
                        for j in range(TPB):
                            ins = pe.transpose(ps[k][:, j * P:(j + 1) * P], xn2[s][:, j, k * P:(k + 1) * P],
                                               ident[:, :])
                        ins.then_inc(s_xt, 1)
                    pe.wait_ge(s_h, blk + 1)
                    for k in range(KD):
                        for j in range(TPB):
                            ins = pe.transpose(ps[2 + k][:, j * P:(j + 1) * P], h[:, j, k * P:(k + 1) * P],
                                               ident[:, :])
                        ins.then_inc(s_ht, 1)

                    def features(n, w, at, m, src):
                        for c in range(KD):
                            ins = pe.matmul(ps[BANK[n % 4]][0:m, :], w[:, c, at:at + m], src[:, c, :],
                                            start=(c == 0), stop=(c == KD - 1))
                        ins.then_inc(s_pr, 1)

                    def values(n, w, at, m, src, tiles):
                        for i, j in enumerate(tiles):
                            for c in range(KD):
                                ins = pe.matmul(ps[BANK[n % 4]][:, i * m:(i + 1) * m], src[:, c, j * P:(j + 1) * P],
                                                w[:, c, at:at + m], start=(c == 0), stop=(c == KD - 1))
                        ins.then_inc(s_pr, 1)

                    pe.wait_ge(s_xT, blk * KD + KD)
                    for n in range(4):
                        features(n, wa, n * P, P, xT)
                    pe.wait_ge(s_pa, blk * 4 + 5)
                    values(4, wa, 2 * D, D, xT, (0, 1))
                    pe.wait_ge(s_pa, blk * 4 + 6)
                    values(5, wa, 2 * D, D, xT, (2, 3))
                    pe.wait_ge(s_hT, blk * KD + KD)
                    pe.wait_ge(s_pa, blk * 4 + 7)
                    features(6, wb, 0, P, hT)
                    pe.wait_ge(s_pa, blk * 4 + 8)
                    features(7, wb, D, P, hT)
                    pe.wait_ge(s_pd, blk * NDVE + 2)
                    features(8, wb, P, P, hT)
                    pe.wait_ge(s_pd, blk * NDVE + 3)
                    features(9, wb, D + P, P, hT)
                    pe.wait_ge(s_pd, blk * NDVE + 4)
                    features(10, wb, 2 * D, KV * HD, hT)
                    features(11, wb, 2 * D + KV * HD, KV * HD, hT)
                    pe.wait_ge(s_pd, blk * NDVE + 5)
                    values(12, wb, 2 * D + 2 * KV * HD, KV * HD, hT, range(TPB))

        @block.scalar
        def _(act):
            sc = nc.scalar
            act.sem_inc(s_pa, 4)
            act.wait_ge(s_wp, 1)
            with act.Fori(0, NBLK // 2) as ip:
                for s in range(2):
                    blk = ip * 2 + s
                    for k in range(KD):
                        act.wait_ge(s_f, blk * KD + (k + 1))
                        sc.activation(f[:, k, :], ps[2 + k][:, :], ACT.Identity, bias=cols[:, k, 2:3],
                                      scale=cols[:, k, 1:2]).then_inc(s_fs, 1)
                    act.wait_ge(s_var, blk + 1)
                    sc.activation(sd[:, 0, :], mv[:, :, 1], ACT.Sqrt).then_inc(s_sd, 1)
                    act.wait_ge(s_xn, blk + 1)
                    for j in range(TPB):
                        ins = sc.activation(sq[:, j, :], xn2[s][:, j, :], ACT.Square, accum_out=ms[:, j:j + 1])
                    ins.then_inc(s_sq, 1)
                    for k in range(KD):
                        act.wait_ge(s_xt, blk * KD + (k + 1))
                        sc.activation(xT[:, k, :], ps[k][:, :], ACT.Copy).then_inc(s_xT, 1)
                    act.wait_ge(s_ms, blk + 1)
                    sc.activation(sd[:, 1, :], msv[:, :], ACT.Sqrt).then_inc(s_rsd, 1)

                    def parts(m):
                        i = (s * NS + m) % 2
                        n = P if m < 6 else KV * HD
                        k = blk * NS + m
                        act.wait_ge(s_pst[i], ip * (NS * 16) + ((s * NS + m) // 2 * 16 + 16))
                        sc.activation(part[i][0:n, 0, :], xf[i][0:n, :], ACT.Copy).then_inc(s_hi, 1)
                        act.wait_ge(s_r, k + 3)
                        sc.activation(part[i][0:n, 1, :], rr[i][0:n, :], ACT.Copy).then_inc(s_mid, 1)

                    for m in range(4):
                        act.wait_ge(s_pr, blk * 13 + (m + 1))
                        act.wait_ge(s_r, blk * NS + (m + 1))
                        sc.activation(xf[(s * NS + m) % 2][:, :], ps[BANK[m]][:, :], ACT.Identity,
                                      bias=(baq[:, m:m + 1] if m < 2 else ba[:, m:m + 1]),
                                      scale=(SCALE if m < 2 else 1.0)).then_inc(s_pa, 1)
                        act.wait_ge(s_pa, blk * 4 + (m + 5))
                        parts(m)
                        if m == 1:
                            for k in range(KD):
                                act.wait_ge(s_ht, blk * KD + (k + 1))
                                sc.activation(hT[:, k, :], ps[2 + k][:, :], ACT.Copy,
                                              scale=cols[:, k, 3:4]).then_inc(s_hT, 1)
                    for m in range(4, NS):
                        act.wait_ge(s_xf, blk * 3 + (m - 3))
                        parts(m)

        @block.vector
        def _(dve):
            ch = Chain(dve, s_dve)
            v = nc.vector
            dve.sem_inc(s_x1, 2)
            dve.sem_inc(s_pd, 1)
            dve.sem_inc(s_r, 2)
            dve.wait_ge(s_w, NW * 16)
            dve.wait_ge(s_zero, 2)
            ch.did(v.tensor_scalar(w_sgn[:, :, :], w_raw[:, :, :], 0.0, 2.0, ALU.is_ge, ALU.mult))
            ch.did(v.tensor_scalar(c_mat[P // 2:P, :], c_mat[P // 2:P, :], -1.0, None, ALU.mult))
            ch.did(v.tensor_scalar(baq[:, :], ba[:, 0:KD], SCALE, None, ALU.mult))
            ch.settle()
            v.tensor_scalar(w_sgn[:, :, :], w_sgn[:, :, :], -1.0, None, ALU.add).then_inc(s_wp, 1)
            with dve.Fori(0, NBLK // 2) as ip:
                b = ip // 2
                ch.enter(ip, 2 * (2 * KD + 2 * TPB + 2 + 3))
                for s in range(2):
                    blk = ip * 2 + s
                    tok = (ip % 2) * (2 * BT) + s * BT
                    for k in range(KD):
                        dve.wait_ge(s_fs, blk * KD + (k + 1))
                        ch.did(v.tensor_scalar(fs[:, k, :], f[:, k, :], -CLIP, CLIP, ALU.max, ALU.min))
                        dve.wait_ge(s_c, blk * KD + (k + 1))
                        ch.did(v.scalar_tensor_tensor(u[:, k, :], xnT[:, k, ds(blk * BT, BT)], cols[:, k, 0:1],
                                                      ps[k][:, :], ALU.mult, ALU.add))
                        ch.settle()
                        v.tensor_tensor(u[:, k, :], u[:, k, :], fs[:, k, :], ALU.add).then_inc(s_u, 1)
                    dve.wait_ge(s_x[s], ip * 16 + 16)
                    dve.wait_ge(s_st[s], ip * 32 + 16)
                    for q in range(2):
                        dve.wait_ge(s_ut, blk * 2 + (q + 1))
                        ins = v.tensor_tensor(x1[s][:, 2 * q:2 * q + 2, :],
                                              ps[4 + q][:, :].rearrange("p (j d) -> p j d", j=2),
                                              x_in[s][:, 2 * q:2 * q + 2, :], ALU.add)
                    ins.then_inc(s_x1, 1)
                    dve.wait_ge(s_x1, blk + 3)
                    for j in range(TPB):
                        ch.did(v.bn_stats(stats[:, j, :], x1[s][:, j, :]))
                    ch.settle()
                    v.tensor_copy(rs_pad[:, :], stats[:, 0, 0:1])
                    for j in range(TPB):
                        ch.did(v.bn_aggr(mv[:, j, :], stats[:, j, :]))
                    ch.settle()
                    v.tensor_scalar(mv[:, :, 1], mv[:, :, 1], LN_EPS, None, ALU.add).then_inc(s_var, 1)
                    dve.wait_ge(s_sd, blk + 1)
                    ch.did(v.reciprocal(rs[:, 0, :], sd[:, 0, :]))
                    ch.settle()
                    for j in range(TPB):
                        ins = v.tensor_scalar(xn2[s][:, j, :], x1[s][:, j, :], mv[:, j, 0:1], rs[:, 0, j:j + 1],
                                              ALU.subtract, ALU.mult)
                    ins.then_inc(s_xn, 1)
                    dve.wait_ge(s_sq, blk + 1)
                    v.tensor_scalar(msv[:, :], ms[:, :], 1.0 / D, LN_EPS, ALU.mult, ALU.add).then_inc(s_ms, 1)
                    dve.wait_ge(s_rsd, blk + 1)
                    ch.did(v.reciprocal(rs[:, 1, :], sd[:, 1, :]))
                    ch.settle()
                    for j in range(TPB):
                        ins = v.tensor_scalar(h[:, j, :], xn2[s][:, j, :], rs[:, 1, j:j + 1], None, ALU.mult)
                    ins.then_inc(s_h, 1)

                    def rest(m):
                        i = (s * NS + m) % 2
                        n = P if m < 6 else KV * HD
                        k = blk * NS + m
                        dve.wait_ge(s_hi, k + 1)
                        v.tensor_tensor(rr[i][0:n, :], xf[i][0:n, :], part[i][0:n, 0, :], ALU.subtract).then_inc(s_r, 1)
                        dve.wait_ge(s_mid, k + 1)
                        v.tensor_tensor(part[i][0:n, 2, :], rr[i][0:n, :], part[i][0:n, 1, :],
                                        ALU.subtract).then_inc(s_lo, 1)

                    for m in range(4):
                        rest(m)
                    dve.wait_ge(s_vst, blk * 32 + 16)
                    for q in range(2):
                        dve.wait_ge(s_pr, blk * 13 + (5 + q))
                        for i in range(2):
                            ins = v.tensor_tensor(
                                va[:, 2 * q + i, :, 0:HD],
                                ps[BANK[q]][:, i * D:(i + 1) * D].rearrange("p (h c) -> p h c", c=HD),
                                bv[:, :].rearrange("p (h c) -> p h c", c=HD), ALU.add)
                        ins.then_inc(s_pd, 1)
                    dve.wait_ge(s_pd, blk * NDVE + 3)
                    dve.sem_inc(s_va, 1)
                    for m in range(4, NS):
                        i = (s * NS + m) % 2
                        n = P if m < 6 else KV * HD
                        a, r = (6, 8, 10)[m - 4], (7, 9, 11)[m - 4]
                        sc = SCALE if m < 6 else 1.0
                        dve.wait_ge(s_pr, blk * 13 + (r + 1))
                        ch.did(v.scalar_tensor_tensor(xf[i][0:n, :], ps[BANK[a % 4]][0:n, :], sc,
                                                      cos[0:n, ds(tok, BT)], ALU.mult, ALU.mult))
                        v.scalar_tensor_tensor(rot[0:n, :], ps[BANK[r % 4]][0:n, :], sc, sin[0:n, ds(tok, BT)],
                                               ALU.mult, ALU.mult).then_inc(s_pd, 1)
                        dve.wait_ge(s_pd, blk * NDVE + m)
                        v.tensor_tensor(xf[i][0:n, :], xf[i][0:n, :], rot[0:n, :], ALU.add).then_inc(s_xf, 1)
                        rest(m)
                    dve.wait_ge(s_pr, blk * 13 + 13)
                    v.tensor_copy(vb[:, :, :, 0:HD].rearrange("p j h c -> p (j h) c"),
                                  ps[BANK[0]][:, 0:TPB * KV * HD].rearrange("p (n c) -> p n c", c=HD)).then_inc(s_pd, 1)
                    dve.wait_ge(s_pd, blk * NDVE + 7)
                    dve.sem_inc(s_va, 1)
            ch.leave(NBLK // 2)


STEPS = 2 * NGB
QB = 512
NQB = L // QB
KT = L // P
LAG = 4
NPB = 8
WIDE = 1024
NMAX = GH * KT + GH * KT // 2


def score_tiles():
    return [(qb, kt, h) for qb in range(NQB) for kt in range(4 * (qb + 1)) for h in range(GH)]


def max_tiles():
    return [(h, qt, k0, min(WIDE, (qt + 1) * P - k0))
            for h in range(GH) for qt in range(KT) for k0 in range(0, (qt + 1) * P, WIDE)]


def columns(qb, kt):
    return max(0, kt * P - qb * QB)


def order(first, last):
    scores, maxes = ([] if first else score_tiles()), ([] if last else max_tiles())
    total_s = sum(QB - columns(qb, kt) for qb, kt, _ in scores)
    total_m = sum(w for *_, w in maxes)
    todo, done_s, done_m, m, out = [], 0, 0, 0, []
    for u in range(len(scores)):
        while m < len(maxes) and done_m * total_s <= 1.12 * total_m * done_s:
            out.append(("max", m))
            done_m += maxes[m][3]
            m += 1
            if m == len(maxes):
                todo.append((u + 12, "rows"))
        for at, what in [t for t in todo if t[0] == u]:
            out.append((what, 0))
        todo = [t for t in todo if t[0] != u]
        out.append(("score", u))
        done_s += QB - columns(*scores[u][:2])
        if u >= LAG:
            out.append(("value", u - LAG))
        if u + 1 < len(scores) and scores[u + 1][0] != scores[u][0]:
            todo.append((u + LAG + 8, "turn"))
    for u in range(max(0, len(scores) - LAG), len(scores)):
        out.append(("value", u))
    for m in range(m, len(maxes)):
        out.append(("max", m))
        if m == len(maxes) - 1:
            todo.append((0, "rows"))
    out += [(what, 0) for _, what in sorted(todo)]
    if scores:
        out.append(("turn", 0))
    n = 0
    for i, (what, _) in enumerate(out):
        if what == "turn":
            out[i] = (what, n)
            n += 1
    return out


def attention(nc, A, M):
    with ExitStack() as ctx:
        def sb(name, shape, dt=F32):
            return ctx.enter_context(nc.sbuf_tensor(name, shape, dt))

        def sem(name):
            return nc.alloc_semaphore(name)

        ps, ident = M["ps"], M["ident"]
        q_op = [sb(f"a_q{i}", [ROWS, GH, L], BF16) for i in range(3)]
        k_op = [sb(f"a_k{i}", [ROWS, GH, L], BF16) for i in range(3)]
        v_op = [sb(f"a_v{i}", [P, KT, GH * VW]) for i in range(3)]
        prob = [sb(f"a_p{i}", [P, QB]) for i in range(NPB)]
        identb = sb("a_identb", [P, P], BF16)
        mask_q = sb("a_maskq", [P, P], BF16)
        mask_k = sb("a_maskk", [P, P], BF16)
        mx = sb("a_mx", [P, GH, KT, 2])
        mneg = sb("a_mneg", [P, GH, KT])
        mrest = sb("a_mrest", [P, GH * KT])
        mpart = sb("a_mpart", [P, 3, P], BF16)
        mrow = sb("a_mrow", [GH * KT, 3, P], BF16)
        o_sb = [sb(f"a_o{i}", [P, QB]) for i in range(2)]
        rec = sb("a_rec", [P, 4, GH])
        o_row = [sb(f"a_orow{i}", [P, 4, GH * HD]) for i in range(2)]
        ps_max = [M["banks"][:, 2 * n:2 * n + 2, :].rearrange("p a b -> p (a b)") for n in range(2)]
        ps_s = [ps[4], ps[5]]
        ps_o, ps_t = ps[6], ps[7]
        ps_tb = ps_t.bitcast(BF16)
        turned = ps_t.rearrange("p (j h c) -> p j h c", j=4, h=GH)

        s_c, s_z = sem("att_consts_loaded"), sem("att_zeroed")
        s_q = [sem(f"att_operands_loaded{i}") for i in range(3)]
        s_v = [sem(f"att_values_loaded{i}") for i in range(3)]
        s_mr = [sem(f"att_max_rows_stored{i}") for i in range(3)]
        s_mt = sem("att_max_tile_scored")
        s_md = sem("att_max_tile_reduced")
        s_sc = sem("att_scored")
        s_ex = sem("att_exp_done")
        s_pv = sem("att_value_product")
        s_oe = sem("att_out_copied")
        s_tt = sem("att_turned")
        s_te = sem("att_turned_taken")
        s_mp = sem("att_max_parts_ready")
        s_os = [sem(f"att_rows_stored{i}") for i in range(2)]
        s_dve = sem("att_dve")
        MAXES_AHEAD, SCORES_AHEAD, TURNS_AHEAD = 2, 2, NQB + 1
        tiles, maxes = score_tiles(), max_tiles()
        NSC, NMX = len(tiles), len(maxes)
        USES = NQB + 1
        NL = (2 * NPROD + 2) * 16
        va_d = M["va_d"].rearrange("(k p) c -> p k c", p=P)
        vb_d = M["vb_d"].rearrange("(k p) c -> p k c", p=P)

        def run(eng, step):
            for r0 in (0, NGB):
                with eng.Fori(0, 2) as i:
                    for r in range(3):
                        step(r0 + r, i)
                step(r0 + 6, 0)
                step(r0 + 7, 0)

        def before(t, n):
            return t * n

        def filled(r, i):
            return i + (r // 3 + 1)

        def uses_in(work):
            return {e: n for n, e in enumerate(e for e in work if e[0] in ("rows", "turn"))}

        def work_of(r):
            return order(False, r == STEPS - 1)

        def uses_before(t):
            return t * USES + 1

        WORK = order(False, False)
        LAST_TURNS = {n: uses_in(WORK)[("turn", n)] for n in range(NQB)}
        block = ctx.enter_context(nc.Block())

        @block.sync
        def _(sp):
            def load(r, i):
                t, o = r + i * 3, r % 3
                second = r >= NGB
                heads = 1 if second else GH
                tb = t - NGB if second else t
                b = tb // NG
                g = tb % NG
                q_d, k_d = (M["qb_d"], M["kb_d"]) if second else (M["qa_d"], M["ka_d"])
                for n in range(NPROD):
                    at = AUG + n * HD
                    sp.dma_start(q_op[o][at:at + HD, :, :],
                                 q_d[PROD_Q[n], ds(tb * (GH * HD), GH * HD), :].rearrange("(h d) t -> d h t", d=HD)
                                 ).then_inc(s_q[o], 16)
                    sp.dma_start(k_op[o][at:at + HD, 0:heads, :],
                                 k_d[PROD_K[n], ds(tb * (heads * HD), heads * HD), :].rearrange(
                                     "(h d) t -> d h t", d=HD)).then_inc(s_q[o], 16)
                if second:
                    sp.dma_start(q_op[o][0:AUG, :, :], A["c_qb"]).then_inc(s_q[o], 16)
                    sp.dma_start(k_op[o][0:AUG, 0, :], A["c_kb"]).then_inc(s_q[o], 16)
                    sp.dma_start(v_op[o][:, :, 0:VW],
                                 vb_d[:, ds(b * KT, KT), ds(g * VW, VW)]).then_inc(s_v[o], 16)
                else:
                    sp.dma_start(q_op[o][0:AUG, :, :], A["c_qa"][:, ds(g * GH, GH), :]).then_inc(s_q[o], 16)
                    sp.dma_start(k_op[o][0:AUG, :, :], A["c_ka"][:, ds(g * GH, GH), :]).then_inc(s_q[o], 16)
                    sp.dma_start(v_op[o][:, :, :],
                                 va_d[:, ds(b * KT, KT), ds(g * GH * VW, GH * VW)]).then_inc(s_v[o], 16)

            def rows(r, i, use):
                sp.wait_ge(s_te, use + 2)
                for c in range(3):
                    sp.dma_start(q_op[r % 3][MROW + c:MROW + c + 1, :, :].rearrange("o h (k p) -> o (h k) p", p=P),
                                 mrow[:, c, :]
                                 ).then_inc(s_mr[r % 3], 16)

            for o in range(2):
                sp.sem_inc(s_os[o], 16)
            for dst, src in ((identb, "c_identb"), (mask_q, "c_maskq"), (mask_k, "c_maskk")):
                sp.dma_start(dst[:, :], A[src]).then_inc(s_c, 16)
            load(0, 0)
            load(1, 0)
            rows(0, 0, 0)

            def step(r, i):
                t = r + i * 3
                if r + 2 < STEPS:
                    sp.wait_ge(s_pv, before(t, NSC) + NPB)
                    load(r + 2, i)
                tb = t - NGB if r >= NGB else t
                b, g = tb // NG, tb % NG
                ao = M["ao_d"][r // NGB].rearrange("(k p) c -> p k c", p=P)
                for (what, n), use in uses_in(work_of(r)).items():
                    if what == "rows":
                        rows(r + 1, i, uses_before(t) + use)
                    else:
                        sp.wait_ge(s_te, uses_before(t) + (use + 2))
                        sp.dma_start(ao[:, ds(b * KT + n * 4, 4), ds(g * (GH * HD), GH * HD)],
                                     o_row[n % 2][:, :, :]).then_inc(s_os[n % 2], 16)

            run(sp, step)
            for o in range(2):
                sp.wait_ge(s_os[o], STEPS * NQB // 2 * 16 + 16)

        @block.gpsimd
        def _(pool):
            nc.gpsimd.memset(mpart[:, :, :], 0.0).then_inc(s_z, 1)

        @block.tensor
        def _(pe):
            pe.sem_inc(s_tt, TURNS_AHEAD)
            pe.sem_inc(s_pv, NPB)
            pe.wait_ge(s_c, 48)
            pe.wait_ge(s_z, 1)

            def max_tile(r, i, t, m):
                h, qt, k0, w = maxes[m]
                o, hk = r % 3, (0 if r >= NGB else h)
                n = before(t, NMX) + m
                pe.wait_ge(s_md, n + 1)
                for c in range(0, w, QB):
                    wc = min(QB, w - c)
                    out = ps_max[m % 2][:, c:c + wc]
                    diagonal = k0 + c + wc == (qt + 1) * P
                    ins = pe.matmul(out, q_op[o][:, h, qt * P:(qt + 1) * P],
                                    k_op[o][:, hk, k0 + c:k0 + c + wc], start=True, stop=not diagonal)
                    if diagonal:
                        ins = pe.matmul(out[:, wc - P:wc], identb[:, :], mask_q[:, :], start=False, stop=True)
                ins.then_inc(s_mt, 1)

            def turn_rows(n_step, use):
                pe.wait_ge(s_mp, n_step + 1)
                pe.wait_ge(s_te, use + 1)
                for c in range(3):
                    ins = pe.transpose(ps_tb[:, c * P:(c + 1) * P], mpart[:, c, :], identb[:, :])
                ins.then_inc(s_tt, 1)

            pe.wait_ge(s_q[0], NL)
            for what, m in order(True, False):
                if what == "max":
                    max_tile(0, 0, 0, m)
                else:
                    turn_rows(0, 0)

            def step(r, i):
                t, o = r + i * 3, r % 3
                work = work_of(r)
                use = uses_in(work)
                if r + 1 < STEPS:
                    pe.wait_ge(s_q[(r + 1) % 3], filled(r + 1, i) * NL)
                pe.wait_ge(s_v[o], filled(r, i) * 16)
                pe.wait_ge(s_mr[o], filled(r, i) * 48)
                for what, n in work:
                    if what == "max":
                        max_tile(r + 1, i, t + 1, n)
                    elif what == "rows":
                        turn_rows(t + 1, uses_before(t) + use[("rows", 0)])
                    elif what == "score":
                        qb, kt, h = tiles[n]
                        c0, hk = columns(qb, kt), (0 if r >= NGB else h)
                        out = ps_s[n % 2]
                        pe.wait_ge(s_ex, before(t, NSC) + (n + 1))
                        diagonal = kt >= 4 * qb
                        ins = pe.matmul(out[:, c0:QB], k_op[o][:, hk, kt * P:(kt + 1) * P],
                                        q_op[o][:, h, qb * QB + c0:(qb + 1) * QB], start=True, stop=not diagonal)
                        if diagonal:
                            ins = pe.matmul(out[:, c0:c0 + P], identb[:, :], mask_k[:, :], start=False, stop=True)
                        ins.then_inc(s_sc, 1)
                    elif what == "value":
                        qb, kt, h = tiles[n]
                        c0, hk = columns(qb, kt), (0 if r >= NGB else h)
                        if kt == 0 and h == 0:
                            pe.wait_ge(s_oe, before(t, NQB) + (qb + 1))
                        pe.wait_ge(s_ex, before(t, NSC) + (n + 1 + SCORES_AHEAD))
                        pe.matmul(ps_o[VW * h:VW * h + VW, c0:QB], v_op[o][:, kt, hk * VW:hk * VW + VW],
                                  prob[n % NPB][:, c0:QB], start=(kt == 0), stop=(kt == 4 * qb + 3)
                                  ).then_inc(s_pv, 1)
                    else:
                        pe.wait_ge(s_oe, before(t, NQB) + (n + 2))
                        pe.wait_ge(s_te, uses_before(t) + (use[("turn", n)] + 1))
                        for j in range(4):
                            ins = pe.transpose(ps_t[:, j * P:(j + 1) * P], o_sb[n % 2][:, j * P:(j + 1) * P],
                                               ident[:, :])
                        ins.then_inc(s_tt, 1)

            run(pe, step)

        @block.scalar
        def _(act):
            act.sem_inc(s_ex, SCORES_AHEAD)
            act.sem_inc(s_oe, 1)

            def step(r, i):
                t = r + i * 3
                for what, n in work_of(r):
                    if what == "score":
                        qb, kt, h = tiles[n]
                        c0 = columns(qb, kt)
                        act.wait_ge(s_sc, before(t, NSC) + (n + 1))
                        act.wait_ge(s_pv, before(t, NSC) + (n + 1))
                        nc.scalar.activation(prob[n % NPB][:, c0:QB], ps_s[n % 2][:, c0:QB], ACT.Exp
                                             ).then_inc(s_ex, 1)
                    elif what == "value" and (n + 1 == NSC or tiles[n + 1][0] != tiles[n][0]):
                        qb = tiles[n][0]
                        act.wait_ge(s_pv, before(t, NSC) + (n + 1 + NPB))
                        at = (uses_before(t) + LAST_TURNS[qb - 2] if qb >= 2
                              else uses_before(t) - USES + LAST_TURNS[qb + 2])
                        act.wait_ge(s_tt, at + (1 + TURNS_AHEAD))
                        nc.scalar.activation(o_sb[qb % 2][:, :], ps_o[:, :], ACT.Copy).then_inc(s_oe, 1)

            run(act, step)

        @block.vector
        def _(dve):
            v = nc.vector
            ch = Chain(dve, s_dve)
            dve.sem_inc(s_md, MAXES_AHEAD)
            dve.sem_inc(s_te, 1)
            dve.wait_ge(s_z, 1)
            NSTEP = 5 + NQB

            def max_tile(t, m):
                h, qt, k0, w = maxes[m]
                dve.wait_ge(s_mt, before(t, NMX) + (m + 1))
                v.tensor_reduce(mx[:, h, qt, k0 // WIDE:k0 // WIDE + 1], ps_max[m % 2][:, 0:w], AX.X,
                                ALU.max).then_inc(s_md, 1)

            def rows(t, use, link, settle):
                half = WIDE // P
                dve.wait_ge(s_md, before(t, NMX) + (NMX + MAXES_AHEAD))
                link(v.tensor_reduce(mneg[:, :, half:], mx[:, :, half:, :], AX.X, ALU.max, negate=True))
                link(v.tensor_scalar(mneg[:, :, 0:half], mx[:, :, 0:half, 0], -1.0, None, ALU.mult))
                settle()
                flat = mneg[:, :, :].rearrange("p h k -> p (h k)")
                n = GH * KT
                link(v.tensor_copy(mpart[:, 0, 0:n], flat))
                settle()
                link(v.tensor_tensor(mrest[:, :], flat, mpart[:, 0, 0:n], ALU.subtract))
                settle()
                link(v.tensor_copy(mpart[:, 1, 0:n], mrest[:, :]))
                settle()
                v.tensor_tensor(mpart[:, 2, 0:n], mrest[:, :], mpart[:, 1, 0:n], ALU.subtract).then_inc(s_mp, 1)
                dve.wait_ge(s_tt, use + (1 + TURNS_AHEAD))
                v.tensor_copy(mrow[:, :, :], ps_tb[0:n, 0:3 * P].rearrange("p (c q) -> p c q", c=3)
                              ).then_inc(s_te, 1)

            for what, m in order(True, False):
                if what == "max":
                    max_tile(0, m)
                else:
                    rows(0, 0, ch.did, ch.settle)

            def step(r, i):
                t = r + i * 3
                work = work_of(r)
                use = uses_in(work)
                for what, n in work:
                    if what == "max":
                        max_tile(t + 1, n)
                    elif what == "rows":
                        dve.wait_ge(s_mr[r % 3], filled(r, i) * 48)
                        rows(t + 1, uses_before(t) + use[("rows", 0)], ch.did, ch.settle)
                    elif what == "turn":
                        dve.wait_ge(s_tt, uses_before(t) + (use[("turn", n)] + 1 + TURNS_AHEAD))
                        ch.did(v.reciprocal(rec[:, :, :], turned[:, :, :, HD]))
                        ch.settle()
                        dve.wait_ge(s_os[n % 2], before(t, NQB // 2 * 16) + (n // 2 * 16 + 16))
                        v.tensor_tensor(o_row[n % 2][:, :, :].rearrange("p j (h c) -> p j h c", h=GH),
                                        turned[:, :, :, 0:HD],
                                        rec[:, :, :].unsqueeze(3).to_broadcast([P, 4, GH, HD]), ALU.mult
                                        ).then_inc(s_te, 1)

            for r0 in (0, NGB):
                with dve.Fori(0, 2) as i:
                    ch.enter(i, 3 * NSTEP)
                    for r in range(3):
                        step(r0 + r, i)
                ch.leave(2)
                step(r0 + 6, 0)
                step(r0 + 7, 0)


def after(nc, A, M):
    with ExitStack() as ctx:
        def sb(name, shape, dt=F32):
            return ctx.enter_context(nc.sbuf_tensor(name, shape, dt))

        def sem(name):
            return nc.alloc_semaphore(name)

        ps, ident, res, h2T, wts = M["ps"], M["ident"], M["res"], M["h2T"], M["wts"]
        NT = TOK // P
        ao = [[sb(f"p_ao{a}{s}", [P, TPB, D]) for s in range(2)] for a in range(2)]
        x1 = [sb(f"p_x1{s}", [P, TPB, D]) for s in range(2)]
        xn = [sb(f"p_xn{s}", [P, TPB, D]) for s in range(2)]
        aoT = [sb(f"p_aoT{a}", [P, KD, BT]) for a in range(2)]
        w = [sb(f"p_w{a}", [P, KD, D]) for a in range(2)]
        bo = sb("p_bo", [P, D])
        xp = sb("p_xp", [P, TPB, D])
        r = sb("p_r", [P, TPB, D])
        sq = sb("p_sq", [P, TPB, D])
        h2 = sb("p_h2", [P, TPB, D])
        ms, msv, sd, rs = (sb(f"p_{n}", [P, TPB]) for n in ("ms", "msv", "sd", "rs"))
        ln2 = sb("p_ln2", [P, KD])
        gate = sb("p_gate", [P, KD, NE])
        lgT = sb("p_lgT", [P, BT])
        lg = sb("p_lg", [P, NT, NE])
        rank = sb("p_rank", [P, NE])
        ex, pr, eq, one1, one2, p2 = (sb(f"p_{n}", [P, NT, NE]) for n in ("ex", "pr", "eq", "one1", "one2", "p2"))
        m1, m2, rk, sm, rsm = (sb(f"p_{n}", [P, NT]) for n in ("m1", "m2", "rk", "sm", "rsm"))

        s_w, s_z = sem("post_weights_loaded"), sem("post_zeroed")
        s_in = [sem(f"post_rows_loaded{s}") for s in range(2)]
        s_at, s_aoT = sem("post_attention_turned"), sem("post_aoT_ready")
        s_pj, s_xp = sem("post_projected"), sem("post_residual_ready")
        s_sq, s_ms, s_sd = sem("post_squares_summed"), sem("post_mean_square"), sem("post_rms_ready")
        s_h, s_ht, s_hT = sem("post_h_ready"), sem("post_h_turned"), sem("post_hT_ready")
        s_lt, s_lc, s_lx, s_lg = (sem("post_logits_transposed"), sem("post_logits_copied"),
                                  sem("post_logits_turned"), sem("post_logits_ready"))
        s_arg, s_ex = sem("post_exp_argument"), sem("post_exp")
        s_dve = sem("post_dve")
        rows = [M["ao_d"][0], M["ao_d"][1], M["x1_d"], M["xn_d"]]
        rows = [d.rearrange("(n p) d -> p n d", p=P) for d in rows]
        block = ctx.enter_context(nc.Block())

        @block.sync
        def _(sp):
            for dst, src in ((w[0][:, :, :], A["w_out"].rearrange("(k p) m -> p k m", p=P)),
                             (w[1][:, :, :], A["wo"].rearrange("(k p) m -> p k m", p=P)),
                             (gate[:, :, :], A["gate"].rearrange("(k p) m -> p k m", p=P)),
                             (ln2[:, :], A["ln2"].rearrange("(k p) -> p k", p=P)),
                             (bo[:, :], A["b_out"].partition_broadcast(P)),
                             (rank[:, :], A["c_rank"])):
                with nc.allow_non_contiguous_dma(reason="a vector, one feature per partition"):
                    sp.dma_start(dst, src).then_inc(s_w, 16)
            with sp.Fori(0, NBLK // 2) as ip:
                for s in range(2):
                    blk = ip * 2 + s
                    sp.wait_ge(s_xp, blk + 1)
                    for tile, d in zip((ao[0][s], ao[1][s], x1[s], xn[s]), rows):
                        sp.dma_start(tile[:, :, :], d[:, ds(blk * TPB, TPB), :]).then_inc(s_in[s], 16)

        @block.gpsimd
        def _(pool):
            nc.gpsimd.memset(lgT[:, :], 0.0).then_inc(s_z, 1)

        @block.tensor
        def _(pe):
            pe.wait_ge(s_w, 96)
            pe.wait_ge(s_z, 1)
            with pe.Fori(0, NBLK // 2) as ip:
                for s in range(2):
                    blk = ip * 2 + s
                    pe.wait_ge(s_in[s], ip * 64 + 64)
                    for a in range(2):
                        for k in range(KD):
                            for j in range(TPB):
                                ins = pe.transpose(ps[2 * a + k][:, j * P:(j + 1) * P],
                                                   ao[a][s][:, j, k * P:(k + 1) * P], ident[:, :])
                            ins.then_inc(s_at, 1)
                    for a in range(2):
                        pe.wait_ge(s_aoT, blk * 4 + (2 * a + 2))
                        for j in range(TPB):
                            for k in range(KD):
                                ins = pe.matmul(ps[4 + 2 * a + j // 2][:, j % 2 * D:(j % 2 + 1) * D],
                                                aoT[a][:, k, j * P:(j + 1) * P], w[a][:, k, :],
                                                start=(k == 0), stop=(k == KD - 1))
                        ins.then_inc(s_pj, 1)
                    pe.wait_ge(s_h, blk + 1)
                    for k in range(KD):
                        for j in range(TPB):
                            ins = pe.transpose(ps[k][:, j * P:(j + 1) * P], h2[:, j, k * P:(k + 1) * P], ident[:, :])
                        ins.then_inc(s_ht, 1)
                    pe.wait_ge(s_hT, blk * KD + KD)
                    for k in range(KD):
                        ins = pe.matmul(ps[2][0:NE, :], gate[:, k, :], h2T[:, k, ds(blk * BT, BT)],
                                        start=(k == 0), stop=(k == KD - 1))
                    ins.then_inc(s_lt, 1)
                    pe.wait_ge(s_lc, blk + 1)
                    for j in range(TPB):
                        ins = pe.transpose(ps[3][:, j * P:(j + 1) * P], lgT[:, j * P:(j + 1) * P], ident[:, :])
                    ins.then_inc(s_lx, 1)
                    pe.wait_ge(s_lg, blk + 1)

        @block.scalar
        def _(act):
            sc = nc.scalar
            act.wait_ge(s_w, 96)
            with act.Fori(0, NBLK // 2) as ip:
                for s in range(2):
                    blk = ip * 2 + s
                    for a in range(2):
                        for k in range(KD):
                            act.wait_ge(s_at, blk * 4 + (2 * a + k + 1))
                            sc.activation(aoT[a][:, k, :], ps[2 * a + k][:, :], ACT.Copy).then_inc(s_aoT, 1)
                    act.wait_ge(s_xp, blk + 3)
                    for j in range(TPB):
                        ins = sc.activation(sq[:, j, :], xp[:, j, :], ACT.Square, accum_out=ms[:, j:j + 1])
                    ins.then_inc(s_sq, 1)
                    act.wait_ge(s_ms, blk + 1)
                    sc.activation(sd[:, :], msv[:, :], ACT.Sqrt).then_inc(s_sd, 1)
                    for k in range(KD):
                        act.wait_ge(s_ht, blk * KD + (k + 1))
                        sc.activation(h2T[:, k, ds(blk * BT, BT)], ps[k][:, :], ACT.Copy,
                                      scale=ln2[:, k:k + 1]).then_inc(s_hT, 1)
                    act.wait_ge(s_lt, blk + 1)
                    sc.activation(lgT[0:NE, :], ps[2][0:NE, :], ACT.Copy).then_inc(s_lc, 1)
            act.wait_ge(s_arg, 1)
            sc.activation(ex[:, :, :], ex[:, :, :], ACT.Exp).then_inc(s_ex, 1)

        @block.vector
        def _(dve):
            v = nc.vector
            ch = Chain(dve, s_dve)
            dve.sem_inc(s_xp, 2)
            dve.wait_ge(s_w, 96)
            with dve.Fori(0, NBLK // 2) as ip:
                ch.enter(ip, 2 * 6)
                for s in range(2):
                    blk = ip * 2 + s
                    dve.wait_ge(s_in[s], ip * 64 + 64)
                    dve.wait_ge(s_pj, blk * 2 + 1)
                    for q in range(2):
                        two = slice(2 * q, 2 * q + 2)
                        ch.did(v.tensor_tensor(r[:, two, :], ps[4 + q].rearrange("p (j d) -> p j d", j=2),
                                               x1[s][:, two, :], ALU.add))
                    ch.settle()
                    ch.did(v.tensor_tensor(r[:, :, :], r[:, :, :], bo[:, :].unsqueeze(1).to_broadcast([P, TPB, D]),
                                           ALU.add))
                    dve.wait_ge(s_pj, blk * 2 + 2)
                    for q in range(2):
                        two = slice(2 * q, 2 * q + 2)
                        ch.did(v.tensor_tensor(xp[:, two, :], ps[6 + q].rearrange("p (j d) -> p j d", j=2),
                                               xn[s][:, two, :], ALU.add))
                    ch.settle()
                    v.tensor_tensor(res[:, ds(blk * TPB, TPB), :], r[:, :, :], xp[:, :, :], ALU.add).then_inc(s_xp, 1)
                    dve.wait_ge(s_sq, blk + 1)
                    v.tensor_scalar(msv[:, :], ms[:, :], 1.0 / D, LN_EPS, ALU.mult, ALU.add).then_inc(s_ms, 1)
                    dve.wait_ge(s_sd, blk + 1)
                    ch.did(v.reciprocal(rs[:, :], sd[:, :]))
                    ch.settle()
                    for j in range(TPB):
                        ins = v.tensor_scalar(h2[:, j, :], xp[:, j, :], rs[:, j:j + 1], None, ALU.mult)
                    ins.then_inc(s_h, 1)
                    dve.wait_ge(s_lx, blk + 1)
                    v.tensor_copy(lg[:, ds(blk * TPB, TPB), :],
                                  ps[3].rearrange("p (j e) -> p j e", j=TPB)[:, :, 0:NE]).then_inc(s_lg, 1)
            ch.leave(NBLK // 2)
            dve.wait_ge(s_lg, NBLK)

            def wide(t):
                return t[:, :].unsqueeze(2).to_broadcast([P, NT, NE])

            def step(ins):
                ch.did(ins)
                ch.settle()

            step(v.tensor_reduce(m1[:, :], lg[:, :, :], AX.X, ALU.max))
            v.tensor_tensor(ex[:, :, :], lg[:, :, :], wide(m1), ALU.subtract).then_inc(s_arg, 1)
            dve.wait_ge(s_ex, 1)
            step(v.tensor_reduce(sm[:, :], ex[:, :, :], AX.X, ALU.add))
            step(v.reciprocal(rsm[:, :], sm[:, :]))
            step(v.tensor_tensor(pr[:, :, :], ex[:, :, :], wide(rsm), ALU.mult))
            ranks = rank[:, :].unsqueeze(1).to_broadcast([P, NT, NE])

            def first_of_largest(m, one, p):
                step(v.tensor_reduce(m[:, :], p[:, :, :], AX.X, ALU.max))
                step(v.tensor_tensor(eq[:, :, :], p[:, :, :], wide(m), ALU.is_equal))
                step(v.tensor_tensor(eq[:, :, :], eq[:, :, :], ranks, ALU.mult))
                step(v.tensor_reduce(rk[:, :], eq[:, :, :], AX.X, ALU.max))
                step(v.tensor_tensor(one[:, :, :], eq[:, :, :], wide(rk), ALU.is_equal))

            first_of_largest(m1, one1, pr)
            step(v.scalar_tensor_tensor(p2[:, :, :], one1[:, :, :], -2.0, pr[:, :, :], ALU.mult, ALU.add))
            first_of_largest(m2, one2, p2)
            step(v.tensor_tensor(sm[:, :], m1[:, :], m2[:, :], ALU.add))
            step(v.reciprocal(rsm[:, :], sm[:, :]))
            step(v.tensor_tensor(eq[:, :, :], one1[:, :, :], one2[:, :, :], ALU.add))
            step(v.tensor_tensor(eq[:, :, :], eq[:, :, :], pr[:, :, :], ALU.mult))
            step(v.tensor_tensor(wts[:, :, :], eq[:, :, :], wide(rsm), ALU.mult))


def experts(nc, A, M, out):
    with ExitStack() as ctx:
        def sb(name, shape, dt=F32):
            return ctx.enter_context(nc.sbuf_tensor(name, shape, dt))

        def sem(name):
            return nc.alloc_semaphore(name)

        ps, res, h2T, wts = M["ps"], M["res"], M["h2T"], M["wts"]
        w13 = [sb(f"e_w13{s}", [P, KD, 2 * FFN]) for s in range(2)]
        w2 = [sb(f"e_w2{s}", [P, FT, D]) for s in range(2)]
        act_out = [sb(f"e_silu{i}", [P, BT]) for i in range(2)]
        g = [sb(f"e_g{s}", [P, FT, BT]) for s in range(2)]
        s_w = [sem(f"exp_weights_loaded{s}") for s in range(2)]
        s_up, s_si = sem("exp_up_ready"), sem("exp_silu_ready")
        s_gp = sem("exp_product_ready")
        s_dn = sem("exp_down_ready")
        s_acc = sem("exp_added")
        s_out = sem("exp_stored")
        DOWN_AHEAD = (NBLK + 2) * TPB
        out_v = out.rearrange("(n p) d -> p n d", p=P)
        block = ctx.enter_context(nc.Block())

        @block.sync
        def _(sp):
            with sp.Fori(0, NE // 2) as ep:
                for es in range(2):
                    sp.wait_ge(s_dn, (ep * 2 + es) * (NBLK * TPB) + (DOWN_AHEAD - NBLK * TPB))
                    e = ds(ep * 2 + es, 1)
                    sp.dma_start(w13[es][:, :, :], A["w13"][e, :, :].rearrange("o (k p) m -> p (o k) m", p=P)
                                 ).then_inc(s_w[es], 16)
                    sp.dma_start(w2[es][:, :, :], A["w2"][e, :, :].rearrange("o (k p) m -> p (o k) m", p=P)
                                 ).then_inc(s_w[es], 16)
            for blk in range(NBLK):
                sp.wait_ge(s_acc, ((NE - 1) * NBLK + blk + 1) * TPB + TPB)
                sp.dma_start(out_v[:, blk * TPB:(blk + 1) * TPB, :],
                             res[:, blk * TPB:(blk + 1) * TPB, :]).then_inc(s_out, 16)
            sp.wait_ge(s_out, NBLK * 16)

        @block.tensor
        def _(pe):
            pe.sem_inc(s_dn, DOWN_AHEAD)
            with pe.Fori(0, NE // 2) as ep:
                for es in range(2):
                    with pe.Fori(0, NBLK // 2) as ip:
                        pe.wait_ge(s_w[es], ep * 32 + 32)
                        for s in range(2):
                            n = ep * (2 * NBLK) + ip * 2 + (es * NBLK + s)
                            for f in range(FT):
                                pe.wait_ge(s_gp, n * FT + (f + 1))
                                for part in range(2):
                                    at = part * FFN + f * P
                                    for k in range(KD):
                                        ins = pe.matmul(ps[2 * (f % 2) + part], w13[es][:, k, at:at + P],
                                                        h2T[:, k, ds((ip * 2 + s) * BT, BT)],
                                                        start=(k == 0), stop=(k == KD - 1))
                                ins.then_inc(s_up, 1)
                        for s in range(2):
                            n = ep * (2 * NBLK) + ip * 2 + (es * NBLK + s)
                            pe.wait_ge(s_gp, n * FT + (FT + 2))
                            for j in range(TPB):
                                pe.wait_ge(s_acc, n * TPB + (j + 1))
                                for f in range(FT):
                                    ins = pe.matmul(ps[4 + j][:, 0:D], g[s][:, f, j * P:(j + 1) * P],
                                                    w2[es][:, f, :], start=(f == 0), stop=(f == FT - 1))
                                ins.then_inc(s_dn, 1)

        @block.scalar
        def _(act):
            with act.Fori(0, NE // 2) as ep:
                for es in range(2):
                    with act.Fori(0, NBLK // 2) as ip:
                        for s in range(2):
                            n = ep * (2 * NBLK) + ip * 2 + (es * NBLK + s)
                            for f in range(FT):
                                act.wait_ge(s_up, n * FT + (f + 1))
                                act.wait_ge(s_gp, n * FT + (f + 1))
                                nc.scalar.activation(act_out[f % 2][:, :], ps[2 * (f % 2)], ACT.Silu
                                                     ).then_inc(s_si, 1)

        @block.vector
        def _(dve):
            v = nc.vector
            dve.sem_inc(s_gp, 2)
            dve.sem_inc(s_acc, TPB)
            with dve.Fori(0, NE // 2) as ep:
                for es in range(2):
                    with dve.Fori(0, NBLK // 2) as ip:
                        for s in range(2):
                            n = ep * (2 * NBLK) + ip * 2 + (es * NBLK + s)
                            dve.wait_ge(s_dn, n * TPB + (DOWN_AHEAD - TPB))
                            for f in range(FT):
                                dve.wait_ge(s_si, n * FT + (f + 1))
                                v.tensor_tensor(g[s][:, f, :], act_out[f % 2][:, :], ps[2 * (f % 2) + 1],
                                                ALU.mult).then_inc(s_gp, 1)
                        for s in range(2):
                            n = ep * (2 * NBLK) + ip * 2 + (es * NBLK + s)
                            for j in range(TPB):
                                dve.wait_ge(s_dn, n * TPB + (j + 1 + DOWN_AHEAD))
                                tile = ds((ip * 2 + s) * TPB + j, 1)
                                v.scalar_tensor_tensor(res[:, tile, :], ps[4 + j][:, 0:D].unsqueeze(1),
                                                       wts[:, tile, ds(ep * 2 + es, 1)].rearrange("p a b -> p (a b)"),
                                                       res[:, tile, :], ALU.mult, ALU.add).then_inc(s_acc, 1)


def program(nc, A, out):
    with ExitStack() as ctx:
        def dram(name, shape, dt=F32):
            return nc.dram_tensor(name, shape, dt).ap()

        M = {"x1_d": dram("x1_rows", (TOK, D)), "xn_d": dram("xn_rows", (TOK, D)),
             "qa_d": dram("qa_parts", (3, B * D, L), BF16), "ka_d": dram("ka_parts", (3, B * D, L), BF16),
             "qb_d": dram("qb_parts", (3, B * D, L), BF16), "kb_d": dram("kb_parts", (3, B * KV * HD, L), BF16),
             "va_d": dram("va_tiles", (TOK, HEADS * VW)), "vb_d": dram("vb_tiles", (TOK, KV * VW)),
             "ao_d": [dram(f"attention{i}_rows", (TOK, D)) for i in range(2)]}
        M["banks"] = ctx.enter_context(nc.psum_tensor("banks", [P, 8, 512], F32))
        M["ps"] = [M["banks"][:, i, :] for i in range(8)]
        M["ident"] = ctx.enter_context(nc.sbuf_tensor("ident", [P, P], F32))
        with ExitStack() as first:
            def sb(name, shape, dt=F32):
                return first.enter_context(nc.sbuf_tensor(name, shape, dt))

            M["xnT"] = sb("xnT", [P, KD, TOK])
            M["f1"], M["f2"] = sb("f1", [P, TOK]), sb("f2", [P, TOK])
            M["pw"] = sb("pw", [P, NPOW, 4])
            M["r1"], M["r2"], M["rtmp"] = sb("r1", [P, CHUNK]), sb("r2", [P, CHUNK]), sb("rtmp", [P, 2, CHUNK])
            front(nc, A, M)
            recurrence(nc, A, M)
            middle(nc, A, M)
        attention(nc, A, M)
        M["res"] = ctx.enter_context(nc.sbuf_tensor("res", [P, TOK // P, D], F32))
        M["h2T"] = ctx.enter_context(nc.sbuf_tensor("h2T", [P, KD, TOK], F32))
        M["wts"] = ctx.enter_context(nc.sbuf_tensor("wts", [P, TOK // P, NE], F32))
        after(nc, A, M)
        experts(nc, A, M, out)


def constants():
    import numpy as np
    bf = np.dtype("bfloat16")
    c = {"c_ident": np.eye(P, dtype=np.float32), "c_identb": np.eye(P, dtype=np.float32).astype(bf)}
    c["c_rank"] = np.tile(np.arange(NE, 0, -1, dtype=np.float32), (P, 1))
    q, k = np.arange(P)[:, None], np.arange(P)[None, :]
    c["c_maskq"] = np.where(k > q, MASKED, 0.0).astype(np.float32).astype(bf)
    c["c_maskk"] = np.ascontiguousarray(c["c_maskq"].T)
    inv = (1.0 / 10000.0 ** (np.arange(0, HD, 2, dtype=np.float32) / np.float32(HD))).astype(np.float32)
    ang = (np.arange(L, dtype=np.float32)[:, None] * inv[None, :]).astype(np.float32)
    emb = np.concatenate([ang, ang], axis=1).T
    sign = np.where(np.arange(HD) < HD // 2, -1.0, 1.0).astype(np.float32)[:, None]
    c["c_cos"] = np.tile(np.cos(emb), (P // HD, 1)).astype(np.float32)
    c["c_sin"] = np.tile(np.sin(emb) * sign, (P // HD, 1)).astype(np.float32)
    slope = np.array([2.0 ** -0.5 * (2.0 ** -0.5) ** i for i in range(HEADS)], np.float32)
    s1 = slope.astype(bf).astype(np.float32)
    s2 = (slope - s1).astype(bf).astype(np.float32)
    s3 = slope - s1 - s2
    pos = np.arange(L)
    hi, lo = (pos - pos % 16).astype(np.float32), (pos % 16).astype(np.float32)
    cq = np.zeros((HEADS, AUG, L), np.float32)
    ck = np.zeros((HEADS, AUG, L), np.float32)
    for n, s in enumerate((s1, s2, s3)):
        cq[:, n], cq[:, 3 + n] = s[:, None], s[:, None]
        ck[:, n], ck[:, 3 + n] = hi, lo
        cq[:, 6 + n], cq[:, 9 + n] = hi, lo
        ck[:, 6 + n], ck[:, 9 + n] = -s[:, None], -s[:, None]
    ck[:, MROW:MROW + 3] = 1.0
    c["c_qa"] = np.ascontiguousarray(cq.transpose(1, 0, 2)).astype(bf)
    c["c_qb"] = np.zeros((AUG, GH, L), np.float32).astype(bf)
    c["c_ka"] = np.ascontiguousarray(ck.transpose(1, 0, 2)).astype(bf)
    c["c_kb"] = np.ascontiguousarray(np.concatenate([np.zeros((MROW, L)), np.ones((3, L))]).astype(bf))
    return c


def kernel(**inputs):
    import numpy as _np
    import concourse.bacc as _bacc
    from concourse import mybir as _mybir
    from concourse.bass_utils import run_bass_kernel_spmd as _run

    g = {k: _np.asarray(v) for k, v in inputs.items()}
    wq = g["L1_ffn_wqkv"]
    nq, nk = HEADS * HD, KV * HD
    swap = _np.arange(nq + nk) // HD * HD + (_np.arange(nq + nk) % HD + HD // 2) % HD
    w_b = _np.concatenate([wq[:nq], wq[swap[:nq]], wq[nq:nq + nk], wq[swap[nq:]], wq[nq + nk:]]).T
    arrays = {
        "x": g["L0_attn_input_sequence"], "steps": g["L0_attn_steps_raw"], "G": g["L0_attn_G_raw"],
        "A": g["L0_attn_A_raw"], "D": g["L0_attn_D_vec"],
        "b_mat": g["L0_attn_B_mat"].transpose(1, 2, 0).reshape(D, P),
        "c_mat": g["L0_attn_C_mat"].transpose(2, 1, 0).reshape(P, D),
        "w_ffn": g["L0_ffn_weights"].T, "scale": g["L0_ffn_scale"], "bias": g["L0_ffn_bias"],
        "w_qkv": g["L1_attn_W_qkv"], "b_qkv": g["L1_attn_b_qkv"], "w_out": g["L1_attn_W_out"],
        "b_out": g["L1_attn_b_out"], "ln1": g["L1_ffn_ln1_w"], "ln2": g["L1_ffn_ln2_w"], "w_b": w_b,
        "wo": g["L1_ffn_wo"].T, "gate": g["L1_ffn_gate_w"].T,
        "w13": g["L1_ffn_w13"].transpose(0, 2, 1), "w2": g["L1_ffn_w2"].transpose(0, 2, 1),
    }
    arrays.update(constants())
    nc = _bacc.Bacc("TRN2", target_bir_lowering=False, num_devices=1)
    feed, A = {}, {}
    for name, a in arrays.items():
        a = _np.ascontiguousarray(a)
        feed[f"in_{name}"] = a
        A[name] = nc.dram_tensor(f"in_{name}", a.shape, _mybir.dt.from_np(a.dtype), kind="ExternalInput").ap()
    out = nc.dram_tensor("out_rows", (TOK, D), F32, kind="ExternalOutput").ap()
    program(nc, A, out)
    r = _run(nc, [feed], core_ids=[0])
    return r.results[0]["out_rows"].reshape(B, L, D)
```

```python
from contextlib import ExitStack

import concourse.bass as bass
from concourse import mybir

ALU = mybir.AluOpType
ACT = mybir.ActivationFunctionType
AX = mybir.AxisListType
F32 = mybir.dt.float32
BF16 = mybir.dt.bfloat16
ds = bass.ds

P = 128
B, L, D = 2, 2048, 256
TOK = B * L
KD = D // P
TPB = 4
BT = TPB * P
NBLK = TOK // BT
LN_EPS = 1e-5
CHUNK = 16
NCH = L // CHUNK
LOCAL_LEVELS = 4
CARRY_LEVELS = 7
NPOW = LOCAL_LEVELS + CARRY_LEVELS
CLIP = 100.0
HEADS, HD = 16, 16
GH = 4
NG = HEADS // GH
NGB = B * NG
KV = 4
VW = 32
AUG = 15
PROD_Q = (0, 0, 1, 1, 0, 2)
PROD_K = (0, 1, 0, 1, 2, 0)
NPROD = len(PROD_Q)
ROWS = AUG + NPROD * HD
MROW = 12
MASKED = -1e30
NE, FFN = 8, 512
FT = FFN // P
SCALE = HD ** -0.5


class Chain:

    def __init__(self, eng, sem):
        self.eng, self.sem, self.start, self.n = eng, sem, 0, 0

    def did(self, ins):
        ins.then_inc(self.sem, 1)
        self.n += 1

    def settle(self):
        self.eng.wait_ge(self.sem, self.start + self.n)

    def enter(self, i, per):
        self.first, self.per = self.start + self.n, per
        self.start, self.n = i * per + self.first, 0

    def leave(self, times):
        assert self.n == self.per, (self.n, self.per)
        self.start, self.n = self.first + times * self.per, 0


def front(nc, A, M):
    with ExitStack() as ctx:
        def sb(name, shape, dt=F32):
            return ctx.enter_context(nc.sbuf_tensor(name, shape, dt))

        def sem(name):
            return nc.alloc_semaphore(name)

        x_in = [sb(f"f_x{s}", [P, TPB, D]) for s in range(2)]
        xn = [sb(f"f_xn{s}", [P, TPB, D]) for s in range(2)]
        stats = sb("f_stats", [P, TPB, 6])
        rs_pad = sb("f_pad", [P, 1])
        mv = sb("f_mv", [P, TPB, 2])
        sd = sb("f_sd", [P, TPB])
        rs = sb("f_rs", [P, TPB])
        b_mat = sb("f_bmat", [P, KD, P])
        par = sb("f_par", [P, 3])
        cf = sb("f_cf", [P, 16])
        tmp = sb("f_tmp", [P, 16])
        tr = [M["ps"][k] for k in range(KD)]
        bu = M["ps"][2]
        ident, xnT, f1, f2, pw = M["ident"], M["xnT"], M["f1"], M["f2"], M["pw"]
        s_const, s_const2 = sem("front_consts_loaded"), sem("front_params_loaded")
        s_x = [sem(f"front_x_loaded{s}") for s in range(2)]
        s_xfree = sem("front_x_free")
        s_var, s_sd = sem("front_var_ready"), sem("front_sd_ready")
        s_xn, s_tr = sem("front_xn_ready"), sem("front_transposed")
        s_xnT, s_bu, s_f = sem("front_xnT_ready"), sem("front_bu_ready"), sem("front_bu_scaled")
        s_dve, s_exp, s_arg, s_tanh, s_cf = (sem("front_dve"), sem("front_exp"), sem("front_tanh_arg"),
                                             sem("front_tanh"), sem("front_coefs"))
        AHEAD = 2 * KD
        x_d = A["x"].rearrange("b (n p) d -> p (b n) d", p=P)
        block = ctx.enter_context(nc.Block())

        @block.sync
        def _(sp):
            for c, name in enumerate(("steps", "G", "A")):
                for half in range(2):
                    sp.dma_start(par[64 * half:64 * half + 64, c:c + 1],
                                 A[name].rearrange("(p a) -> p a", a=1)).then_inc(s_const2, 16)
            with sp.Fori(0, NBLK // 2) as ip:
                for s in range(2):
                    sp.wait_ge(s_xfree, ip * 2 + (s + 1))
                    sp.dma_start(x_in[s][:, :, :], x_d[:, ds((ip * 2 + s) * TPB, TPB), :]).then_inc(s_x[s], 16)

        @block.gpsimd
        def _(pool):
            pool.dma_start(ident[:, :], A["c_ident"]).then_inc(s_const, 16)
            pool.dma_start(b_mat[:, :, :], A["b_mat"].rearrange("(k p) m -> p k m", p=P)).then_inc(s_const, 16)

        C = {n: cf[:, i:i + 1] for i, n in enumerate(
            ("e", "e1", "step", "G", "A", "sg", "S", "iS", "s2", "al", "z", "th", "c1", "c2"))}

        @block.scalar
        def _(act):
            act.sem_inc(s_f, 2)
            act.wait_ge(s_const2, 96)
            nc.scalar.activation(C["e"], par[:, 0:1], ACT.Exp, scale=-1.0).then_inc(s_exp, 1)
            act.wait_ge(s_arg, 1)
            nc.scalar.activation(C["th"], C["z"], ACT.Tanh, scale=1.0 / 1.99).then_inc(s_tanh, 1)
            act.wait_ge(s_cf, 1)
            with act.Fori(0, NBLK // 2) as ip:
                for s in range(2):
                    blk = ip * 2 + s
                    act.wait_ge(s_var, blk + 1)
                    nc.scalar.activation(sd[:, :], mv[:, :, 1], ACT.Sqrt).then_inc(s_sd, 1)
                    for k in range(KD):
                        act.wait_ge(s_tr, blk * KD + (AHEAD + k + 1))
                        nc.scalar.activation(xnT[:, k, ds(blk * BT, BT)], tr[k][:, :], ACT.Copy).then_inc(s_xnT, 1)
                    act.wait_ge(s_bu, blk + 1)
                    nc.scalar.activation(f1[:, ds(blk * BT, BT)], bu[:, :], ACT.Copy,
                                         scale=C["c1"]).then_inc(s_f, 1)
                    nc.scalar.activation(f2[:, ds(blk * BT, BT)], bu[:, :], ACT.Copy,
                                         scale=C["c2"]).then_inc(s_f, 1)

        @block.tensor
        def _(pe):
            pe.sem_inc(s_tr, AHEAD)
            pe.wait_ge(s_const, 32)
            with pe.Fori(0, NBLK // 2) as ip:
                for s in range(2):
                    blk = ip * 2 + s
                    pe.wait_ge(s_xn, blk + 1)
                    for k in range(KD):
                        for j in range(TPB):
                            ins = pe.transpose(tr[k][:, j * P:(j + 1) * P], xn[s][:, j, k * P:(k + 1) * P],
                                               ident[:, :])
                        ins.then_inc(s_tr, 1)
                    pe.wait_ge(s_xnT, blk * KD + KD)
                    pe.wait_ge(s_f, blk * 2 + 2)
                    for k in range(KD):
                        ins = pe.matmul(bu[:, :], b_mat[:, k, :], xnT[:, k, ds(blk * BT, BT)],
                                        start=(k == 0), stop=(k == KD - 1))
                    ins.then_inc(s_bu, 1)

        @block.vector
        def _(dve):
            ch = Chain(dve, s_dve)
            dve.sem_inc(s_xfree, 2)
            v = nc.vector
            dve.wait_ge(s_exp, 1)
            ch.did(v.tensor_scalar(C["e1"], C["e"], 1.0, None, ALU.add))
            ch.did(v.tensor_scalar(C["G"], par[:, 1:2], 0.0, None, ALU.max))
            ch.did(v.tensor_scalar(C["A"], par[:, 2:3], 0.0, None, ALU.max))
            ch.settle()
            ch.did(v.reciprocal(C["step"], C["e1"]))
            ch.settle()
            ch.did(v.tensor_tensor(C["sg"], C["step"], C["G"], ALU.mult))
            ch.did(v.tensor_tensor(C["s2"], C["step"], C["step"], ALU.mult))
            ch.settle()
            ch.did(v.tensor_scalar(C["S"], C["sg"], 1.0, None, ALU.add))
            ch.did(v.tensor_tensor(C["al"], C["s2"], C["A"], ALU.mult))
            ch.settle()
            ch.did(v.reciprocal(C["iS"], C["S"]))
            ch.settle()
            v.tensor_tensor(C["z"], C["al"], C["iS"], ALU.mult).then_inc(s_arg, 1)
            ch.did(v.tensor_tensor(C["c1"], C["step"], C["iS"], ALU.mult))
            ch.settle()
            ch.did(v.tensor_tensor(C["c2"], C["step"], C["c1"], ALU.mult))
            ch.did(v.tensor_copy(pw[:, 0, 0:1], C["iS"]))
            ch.did(v.tensor_copy(pw[:, 0, 2:3], C["c1"]))
            dve.wait_ge(s_tanh, 1)
            ch.did(v.tensor_scalar(pw[:, 0, 3:4], C["th"], -1.99, 1.0, ALU.mult, ALU.add))
            ch.did(v.scalar_tensor_tensor(pw[:, 0, 1:2], C["th"], -1.99, C["e1"], ALU.mult, ALU.mult))
            ch.settle()
            for n in range(1, NPOW):
                a, b, c, d = (pw[:, n - 1, i:i + 1] for i in range(4))
                bc, trc = tmp[:, 0:1], tmp[:, 1:2]
                ch.did(v.tensor_tensor(bc, b, c, ALU.mult))
                ch.did(v.tensor_tensor(trc, a, d, ALU.add))
                ch.settle()
                ch.did(v.scalar_tensor_tensor(pw[:, n, 0:1], a, a, bc, ALU.mult, ALU.add))
                ch.did(v.scalar_tensor_tensor(pw[:, n, 3:4], d, d, bc, ALU.mult, ALU.add))
                ch.did(v.tensor_tensor(pw[:, n, 1:2], b, trc, ALU.mult))
                ch.did(v.tensor_tensor(pw[:, n, 2:3], c, trc, ALU.mult))
                ch.settle()
            r1, r2 = M["r1"], M["r2"]
            ch.did(v.tensor_copy(r1[:, 0:1], pw[:, 0, 2:3]))
            ch.did(v.tensor_copy(r2[:, 0:1], pw[:, 0, 3:4]))
            ch.settle()
            for n in range(LOCAL_LEVELS):
                w = 1 << n
                a, b, c, d = (pw[:, n, i:i + 1] for i in range(4))
                t = M["rtmp"]
                ch.did(v.tensor_scalar(t[:, 0, 0:w], r2[:, 0:w], c, None, ALU.mult))
                ch.did(v.tensor_scalar(t[:, 1, 0:w], r2[:, 0:w], d, None, ALU.mult))
                ch.settle()
                ch.did(v.scalar_tensor_tensor(r1[:, w:2 * w], r1[:, 0:w], a, t[:, 0, 0:w], ALU.mult, ALU.add))
                ch.did(v.scalar_tensor_tensor(r2[:, w:2 * w], r1[:, 0:w], b, t[:, 1, 0:w], ALU.mult, ALU.add))
                ch.settle()
            dve.sem_inc(s_cf, 1)
            with dve.Fori(0, NBLK // 2) as ip:
                ch.enter(ip, 2 * (2 * TPB + 1))
                for s in range(2):
                    blk = ip * 2 + s
                    dve.wait_ge(s_x[s], ip * 16 + 16)
                    for j in range(TPB):
                        ch.did(v.bn_stats(stats[:, j, :], x_in[s][:, j, :]))
                    ch.settle()
                    v.tensor_copy(rs_pad[:, :], stats[:, 0, 0:1])
                    for j in range(TPB):
                        ch.did(v.bn_aggr(mv[:, j, :], stats[:, j, :]))
                    ch.settle()
                    v.tensor_scalar(mv[:, :, 1], mv[:, :, 1], LN_EPS, None, ALU.add).then_inc(s_var, 1)
                    dve.wait_ge(s_sd, blk + 1)
                    ch.did(v.reciprocal(rs[:, :], sd[:, :]))
                    ch.settle()
                    dve.wait_ge(s_tr, blk * KD + (AHEAD - KD))
                    for j in range(TPB):
                        ins = v.tensor_scalar(xn[s][:, j, :], x_in[s][:, j, :], mv[:, j, 0:1], rs[:, j:j + 1],
                                              ALU.subtract, ALU.mult)
                    ins.then_inc(s_xn, 1)
                    dve.wait_ge(s_xn, blk + 1)
                    dve.sem_inc(s_xfree, 1)
            ch.leave(NBLK // 2)


def middle_weights(nc, ctx, M):
    for name, shape in (("c_mat", [P, D]), ("w_raw", [P, KD, D]), ("wa", [P, KD, 3 * D]), ("ba", [P, 4]),
                        ("bv", [P, D]), ("wb", [P, KD, 2 * D + 3 * KV * HD]), ("cos", [P, L]), ("sin", [P, L]),
                        ("cols", [P, KD, 4])):
        M[name] = ctx.enter_context(nc.sbuf_tensor("m_" + name, shape, F32))
    M["s_mid_weights"] = nc.alloc_semaphore("mid_weights_loaded")


def recurrence(nc, A, M):
    f1, f2, pw, r1, r2 = M["f1"], M["f2"], M["pw"], M["r1"], M["r2"]
    with ExitStack() as ctx:
        def sb(name, shape, dt=F32):
            return ctx.enter_context(nc.sbuf_tensor(name, shape, dt))

        t1 = sb("r_t1", [P, B * NCH])
        t2 = sb("r_t2", [P, B * NCH])
        g = [[sb(f"r_g{i}{c}", [P, B, NCH]) for c in range(2)] for i in range(2)]
        s_dve = nc.alloc_semaphore("rec_dve")
        block = ctx.enter_context(nc.Block())
        f1v = f1[:, :].rearrange("p (c i) -> p c i", i=CHUNK)
        f2v = f2[:, :].rearrange("p (c i) -> p c i", i=CHUNK)
        y = f2[:, :].rearrange("p (b c i) -> p b c i", b=B, i=CHUNK)

        @block.sync
        def _(sp):
            for dst, src in ((M["c_mat"][:, :], A["c_mat"]),
                             (M["w_raw"][:, :, :], A["w_ffn"].rearrange("(k p) m -> p k m", p=P)),
                             (M["wa"][:, :, :], A["w_qkv"].rearrange("(k p) m -> p k m", p=P)),
                             (M["wb"][:, :, :], A["w_b"].rearrange("(k p) m -> p k m", p=P)),
                             (M["cos"][:, :], A["c_cos"]), (M["sin"][:, :], A["c_sin"]),
                             (M["cols"][:, :, 0], A["D"].rearrange("(k p) -> p k", p=P)),
                             (M["cols"][:, :, 1], A["scale"].rearrange("(k p) -> p k", p=P)),
                             (M["cols"][:, :, 2], A["bias"].rearrange("(k p) -> p k", p=P)),
                             (M["cols"][:, :, 3], A["ln1"].rearrange("(k p) -> p k", p=P)),
                             (M["ba"][:, :], A["b_qkv"][0:2 * D].rearrange("(k p) -> p k", p=P))):
                with nc.allow_non_contiguous_dma(reason="a vector, one feature per partition"):
                    sp.dma_start(dst, src).then_inc(M["s_mid_weights"], 16)
            sp.dma_start(M["bv"][:, :], A["b_qkv"][2 * D:3 * D].partition_broadcast(P)).then_inc(M["s_mid_weights"], 16)

        @block.vector
        def _(dve):
            ch = Chain(dve, s_dve)
            v = nc.vector
            a, b, c, d = (pw[:, 0, i:i + 1] for i in range(4))
            with dve.Fori(0, CHUNK - 1) as i:
                ch.enter(i, 4)
                p1, p2 = f1v[:, :, ds(i, 1)], f2v[:, :, ds(i, 1)]
                n1, n2 = f1v[:, :, ds(i + 1, 1)], f2v[:, :, ds(i + 1, 1)]
                u1, u2 = (t[:, :].rearrange("p (c o) -> p c o", o=1) for t in (t1, t2))
                ch.did(v.scalar_tensor_tensor(u1, p2, b, n1, ALU.mult, ALU.add))
                ch.did(v.scalar_tensor_tensor(u2, p2, d, n2, ALU.mult, ALU.add))
                ch.settle()
                ch.did(v.scalar_tensor_tensor(n1, p1, a, u1, ALU.mult, ALU.add))
                ch.did(v.scalar_tensor_tensor(n2, p1, c, u2, ALU.mult, ALU.add))
                ch.settle()
            ch.leave(CHUNK - 1)
            fv = f1[:, :].rearrange("p (b c i) -> p b c i", b=B, i=CHUNK)
            ch.did(v.tensor_copy(g[0][0][:, :, :], fv[:, :, :, CHUNK - 1]))
            ch.did(v.tensor_copy(g[0][1][:, :, :], y[:, :, :, CHUNK - 1]))
            ch.settle()
            for lev in range(CARRY_LEVELS):
                w = 1 << lev
                a, b, c, d = (pw[:, LOCAL_LEVELS + lev, i:i + 1] for i in range(4))
                old, new = g[lev % 2], g[1 - lev % 2]
                u1 = t1[:, :].rearrange("p (b c) -> p b c", b=B)[:, :, w:]
                u2 = t2[:, :].rearrange("p (b c) -> p b c", b=B)[:, :, w:]
                ch.did(v.scalar_tensor_tensor(u1, old[1][:, :, 0:NCH - w], b, old[0][:, :, w:], ALU.mult, ALU.add))
                ch.did(v.scalar_tensor_tensor(u2, old[1][:, :, 0:NCH - w], d, old[1][:, :, w:], ALU.mult, ALU.add))
                ch.did(v.tensor_copy(new[0][:, :, 0:w], old[0][:, :, 0:w]))
                ch.did(v.tensor_copy(new[1][:, :, 0:w], old[1][:, :, 0:w]))
                ch.settle()
                ch.did(v.scalar_tensor_tensor(new[0][:, :, w:], old[0][:, :, 0:NCH - w], a, u1, ALU.mult, ALU.add))
                ch.did(v.scalar_tensor_tensor(new[1][:, :, w:], old[0][:, :, 0:NCH - w], c, u2, ALU.mult, ALU.add))
                ch.settle()
            g1, g2 = g[CARRY_LEVELS % 2]
            with dve.Fori(0, CHUNK // 4) as i4:
                ch.enter(i4, 8)
                for o in range(4):
                    yi = y[:, :, 1:, ds(i4 * 4 + o, 1)].rearrange("p b c o -> p b (c o)")
                    ch.did(v.scalar_tensor_tensor(yi, g1[:, :, 0:NCH - 1], r1[:, ds(i4 * 4 + o, 1)], yi,
                                                  ALU.mult, ALU.add))
                ch.settle()
                for o in range(4):
                    yi = y[:, :, 1:, ds(i4 * 4 + o, 1)].rearrange("p b c o -> p b (c o)")
                    ch.did(v.scalar_tensor_tensor(yi, g2[:, :, 0:NCH - 1], r2[:, ds(i4 * 4 + o, 1)], yi,
                                                  ALU.mult, ALU.add))
            ch.leave(CHUNK // 4)


def middle(nc, A, M):
    with ExitStack() as ctx:
        def sb(name, shape, dt=F32):
            return ctx.enter_context(nc.sbuf_tensor(name, shape, dt))

        def sem(name):
            return nc.alloc_semaphore(name)

        ps, ident, xnT, y = M["ps"], M["ident"], M["xnT"], M["f2"]
        x_in = [sb(f"m_x{s}", [P, TPB, D]) for s in range(2)]
        x1 = [sb(f"m_x1{s}", [P, TPB, D]) for s in range(2)]
        xn2 = [sb(f"m_xn2{s}", [P, TPB, D]) for s in range(2)]
        h = sb("m_h", [P, TPB, D])
        u = sb("m_u", [P, KD, BT])
        f = sb("m_f", [P, KD, BT])
        fs = sb("m_fs", [P, KD, BT])
        xTs = [sb(f"m_xT{s}", [P, KD, BT]) for s in range(2)]
        hTs = [sb(f"m_hT{s}", [P, KD, BT]) for s in range(2)]
        sq = sb("m_sq", [P, TPB, D])
        stats = sb("m_stats", [P, TPB, 6])
        rs_pad = sb("m_pad", [P, 1])
        mv = sb("m_mv", [P, TPB, 2])
        ms = sb("m_ms", [P, TPB])
        msv = sb("m_msv", [P, TPB])
        sd = sb("m_sd", [P, 2, TPB])
        rs = sb("m_rs", [P, 2, TPB])
        c_mat, w_raw, cols, wa, ba, bv, wb, cos, sin = (
            M[n] for n in ("c_mat", "w_raw", "cols", "wa", "ba", "bv", "wb", "cos", "sin"))
        w_sgn = sb("m_wsgn", [P, KD, D])
        baq = sb("m_baq", [P, KD])
        va = sb("m_va", [P, TPB, HEADS, VW])
        vb = sb("m_vb", [P, TPB, KV, VW])
        NS = 7
        xf = [sb(f"m_xf{i}", [P, BT]) for i in range(2)]
        rots = [sb(f"m_rot{i}", [P, BT]) for i in range(2)]
        rr = [sb(f"m_rr{i}", [P, BT]) for i in range(2)]
        part = [sb(f"m_part{m}", [P, 3, BT], BF16) for m in range(NS)]

        s_w = M["s_mid_weights"]
        s_wp = sem("mid_weights_prepared")
        s_x = [sem(f"mid_x_loaded{s}") for s in range(2)]
        s_c, s_f, s_fs = sem("mid_cy_ready"), sem("mid_ffn_ready"), sem("mid_ffn_scaled")
        s_u, s_ut = sem("mid_u_ready"), sem("mid_u_transposed")
        s_x1, s_var, s_sd, s_xn = sem("mid_x1_ready"), sem("mid_var_ready"), sem("mid_sd_ready"), sem("mid_xn_ready")
        s_sq, s_h = sem("mid_squares_summed"), sem("mid_h_ready")
        s_xt, s_xT = sem("mid_xn_transposed"), sem("mid_xT_ready")
        s_ht, s_hT = sem("mid_h_transposed"), sem("mid_hT_ready")
        s_pr, s_pa, s_pd = sem("mid_projected"), sem("mid_taken_by_act"), sem("mid_taken_by_dve")
        s_hi, s_mid, s_xf, s_r, s_lo = (sem("mid_high_part"), sem("mid_middle_part"), sem("mid_rope_ready"),
                                        sem("mid_rest"), sem("mid_low_part"))
        s_va = sem("mid_v_ready")
        s_st = [sem(f"mid_rows_stored{s}") for s in range(2)]
        s_pst = [sem(f"mid_parts_stored{m}") for m in range(NS)]
        s_vst = sem("mid_v_stored")
        s_ms, s_rsd = sem("mid_mean_square"), sem("mid_rms_ready")
        s_dve, s_act, s_zero = sem("mid_dve"), sem("mid_act"), sem("mid_zeroed")
        x_d = A["x"].rearrange("b (n p) d -> p (b n) d", p=P)
        x1_d = M["x1_d"].rearrange("(n p) d -> p n d", p=P)
        xn_d = M["xn_d"].rearrange("(n p) d -> p n d", p=P)
        va_d = M["va_d"].rearrange("(n p) c -> p n c", p=P)
        vb_d = M["vb_d"].rearrange("(n p) c -> p n c", p=P)
        NW = 12
        NDVE = 6
        BANK = [6, 7, 4, 5]

        def run(eng, alone, both):
            alone()
            with eng.Fori(0, NBLK // 2 - 1) as ip:
                for s in range(2):
                    both(ip, s, True, True)
            both(NBLK // 2 - 1, 0, True, False)
            both(NBLK // 2 - 1, 1, False, False)

        def behind(ip, s):
            return (ip, 1) if s == 0 else (ip + 1, 0)

        block = ctx.enter_context(nc.Block())

        @block.gpsimd
        def _(pool):
            nc.gpsimd.memset(va[:, :, :, :], 0.0)
            nc.gpsimd.memset(vb[:, :, :, :], 0.0).then_inc(s_zero, 1)
            pool.wait_ge(s_zero, 1)
            nc.gpsimd.memset(va[:, :, :, HD:HD + 1], 1.0)
            nc.gpsimd.memset(vb[:, :, :, HD:HD + 1], 1.0).then_inc(s_zero, 1)
            with pool.Fori(0, NBLK // 2) as ip:
                for s in range(2):
                    blk = ip * 2 + s
                    pool.wait_ge(s_x1, blk + 1)
                    pool.dma_start(x_in[s][:, :, :], x_d[:, ds(blk * TPB, TPB), :]).then_inc(s_x[s], 16)

        @block.sync
        def _(sp):
            for free in (*s_pst, *s_st, s_vst):
                sp.sem_inc(free, 16)
            with sp.Fori(0, NBLK // 2) as ip:
                b = ip // 2
                for s in range(2):
                    blk = ip * 2 + s
                    tok = (ip % 2) * (2 * BT) + s * BT
                    sp.wait_ge(s_xn, blk + 1)
                    sp.dma_start(x1_d[:, ds(blk * TPB, TPB), :], x1[s][:, :, :]).then_inc(s_st[s], 16)
                    sp.dma_start(xn_d[:, ds(blk * TPB, TPB), :], xn2[s][:, :, :]).then_inc(s_st[s], 16)
                    for m in range(NS):
                        if m == 4:
                            sp.wait_ge(s_va, blk * 2 + 1)
                            sp.dma_start(va_d[:, ds(blk * TPB, TPB), :],
                                         va[:, :, :, :].rearrange("p j h c -> p j (h c)")).then_inc(s_vst, 16)
                        sp.wait_ge(s_lo, blk * NS + (m + 3))
                        if m < 6:
                            dram = (M["qa_d"], M["qa_d"], M["ka_d"], M["ka_d"], M["qb_d"], M["qb_d"])[m]
                            row, n = b * D + (m % 2) * P, P
                        else:
                            dram, row, n = M["kb_d"], b * (KV * HD), KV * HD
                        sp.dma_start(dram[:, ds(row, n), ds(tok, BT)].rearrange("a f t -> f a t"),
                                     part[m][0:n, :, :]).then_inc(s_pst[m], 16)
                    sp.wait_ge(s_va, blk * 2 + 2)
                    sp.dma_start(vb_d[:, ds(blk * TPB, TPB), :],
                                 vb[:, :, :, :].rearrange("p j h c -> p j (h c)")).then_inc(s_vst, 16)
            for m in range(NS):
                sp.wait_ge(s_pst[m], NBLK * 16 + 16)
            for i in range(2):
                sp.wait_ge(s_st[i], NBLK // 2 * 32 + 16)
            sp.wait_ge(s_vst, NBLK * 32 + 16)

        @block.tensor
        def _(pe):
            def first_products(ip, s):
                blk = ip * 2 + s
                for k in range(KD):
                    pe.matmul(ps[k][:, :], c_mat[:, k * P:(k + 1) * P], y[:, ds(blk * BT, BT)],
                              start=True, stop=True).then_inc(s_c, 1)
                for k in range(KD):
                    for c in range(KD):
                        ins = pe.matmul(ps[2 + k][:, :], w_sgn[:, c, k * P:(k + 1) * P],
                                        xnT[:, c, ds(blk * BT, BT)], start=(c == 0), stop=(c == KD - 1))
                    ins.then_inc(s_f, 1)

            def turn_u(ip, s):
                blk = ip * 2 + s
                pe.wait_ge(s_u, blk * KD + KD)
                for j in range(TPB):
                    for k in range(KD):
                        o = (j % 2) * D + k * P
                        ins = pe.transpose(ps[2 + j // 2][:, o:o + P], u[:, k, j * P:(j + 1) * P], ident[:, :])
                    if j % 2:
                        ins.then_inc(s_ut, 1)

            def turn_xn(ip, s):
                pe.wait_ge(s_xn, ip * 2 + (s + 1))
                for k in range(KD):
                    for j in range(TPB):
                        ins = pe.transpose(ps[k][:, j * P:(j + 1) * P], xn2[s][:, j, k * P:(k + 1) * P],
                                           ident[:, :])
                    ins.then_inc(s_xt, 1)

            def turn_h(ip, s):
                pe.wait_ge(s_h, ip * 2 + (s + 1))
                for k in range(KD):
                    for j in range(TPB):
                        ins = pe.transpose(ps[2 + k][:, j * P:(j + 1) * P], h[:, j, k * P:(k + 1) * P],
                                           ident[:, :])
                    ins.then_inc(s_ht, 1)

            def features(n, w, at, m, src):
                for c in range(KD):
                    ins = pe.matmul(ps[BANK[n % 4]][0:m, :], w[:, c, at:at + m], src[:, c, :],
                                    start=(c == 0), stop=(c == KD - 1))
                ins.then_inc(s_pr, 1)

            def values(n, w, at, m, src, tiles):
                for i, j in enumerate(tiles):
                    for c in range(KD):
                        ins = pe.matmul(ps[BANK[n % 4]][:, i * m:(i + 1) * m], src[:, c, j * P:(j + 1) * P],
                                        w[:, c, at:at + m], start=(c == 0), stop=(c == KD - 1))
                ins.then_inc(s_pr, 1)

            def alone():
                first_products(0, 0)
                turn_u(0, 0)
                turn_xn(0, 0)
                turn_h(0, 0)
                pe.wait_ge(s_xT, KD)
                pe.wait_ge(s_hT, KD)
                first_products(0, 1)

            def both(ip, s, more, ahead):
                blk = ip * 2 + s
                xT, hT = xTs[s], hTs[s]
                pe.wait_ge(s_xT, blk * KD + KD)
                pe.wait_ge(s_hT, blk * KD + KD)
                pe.wait_ge(s_pa, blk * 4 + 4)
                pe.wait_ge(s_pd, blk * NDVE + 1)
                for n in range(2):
                    features(n, wa, n * P, P, xT)
                if more:
                    turn_u(*behind(ip, s))
                for n in range(2, 4):
                    features(n, wa, n * P, P, xT)
                pe.wait_ge(s_pa, blk * 4 + 5)
                values(4, wa, 2 * D, D, xT, (0, 1))
                pe.wait_ge(s_pa, blk * 4 + 6)
                values(5, wa, 2 * D, D, xT, (2, 3))
                pe.wait_ge(s_pa, blk * 4 + 7)
                features(6, wb, 0, P, hT)
                pe.wait_ge(s_pa, blk * 4 + 8)
                features(7, wb, D, P, hT)
                if more:
                    turn_xn(*behind(ip, s))
                pe.wait_ge(s_pd, blk * NDVE + 2)
                features(8, wb, P, P, hT)
                pe.wait_ge(s_pd, blk * NDVE + 3)
                features(9, wb, D + P, P, hT)
                if more:
                    turn_h(*behind(ip, s))
                pe.wait_ge(s_pd, blk * NDVE + 4)
                features(10, wb, 2 * D, KV * HD, hT)
                features(11, wb, 2 * D + KV * HD, KV * HD, hT)
                if ahead:
                    pe.wait_ge(s_xT, blk * KD + 2 * KD)
                    pe.wait_ge(s_hT, blk * KD + 2 * KD)
                    first_products(ip + 1, s)
                pe.wait_ge(s_pd, blk * NDVE + 5)
                values(12, wb, 2 * D + 2 * KV * HD, KV * HD, hT, range(TPB))

            pe.wait_ge(s_wp, 1)
            run(pe, alone, both)

        @block.scalar
        def _(act):
            sc = nc.scalar
            act.sem_inc(s_pa, 4)
            act.wait_ge(s_wp, 1)

            def scale_ffn(ip, s):
                blk = ip * 2 + s
                for k in range(KD):
                    act.wait_ge(s_f, blk * KD + (k + 1))
                    sc.activation(f[:, k, :], ps[2 + k][:, :], ACT.Identity, bias=cols[:, k, 2:3],
                                  scale=cols[:, k, 1:2]).then_inc(s_fs, 1)

            def deviation(ip, s):
                act.wait_ge(s_var, ip * 2 + (s + 1))
                sc.activation(sd[:, 0, :], mv[:, :, 1], ACT.Sqrt).then_inc(s_sd, 1)

            def squares(ip, s):
                act.wait_ge(s_xn, ip * 2 + (s + 1))
                for j in range(TPB):
                    ins = sc.activation(sq[:, j, :], xn2[s][:, j, :], ACT.Square, accum_out=ms[:, j:j + 1])
                ins.then_inc(s_sq, 1)

            def take_xT(ip, s):
                blk = ip * 2 + s
                for k in range(KD):
                    act.wait_ge(s_xt, blk * KD + (k + 1))
                    sc.activation(xTs[s][:, k, :], ps[k][:, :], ACT.Copy).then_inc(s_xT, 1)
                act.wait_ge(s_ms, blk + 1)
                sc.activation(sd[:, 1, :], msv[:, :], ACT.Sqrt).then_inc(s_rsd, 1)

            def take_hT(ip, s):
                blk = ip * 2 + s
                for k in range(KD):
                    act.wait_ge(s_ht, blk * KD + (k + 1))
                    sc.activation(hTs[s][:, k, :], ps[2 + k][:, :], ACT.Copy,
                                  scale=cols[:, k, 3:4]).then_inc(s_hT, 1)

            def alone():
                for stage in (scale_ffn, deviation, squares, take_xT, take_hT):
                    stage(0, 0)

            def both(ip, s, more, ahead):
                blk = ip * 2 + s

                def high(m):
                    i = (s * NS + m) % 2
                    n = P if m < 6 else KV * HD
                    act.wait_ge(s_pst[m], blk * 16 + 16)
                    sc.activation(part[m][0:n, 0, :], xf[i][0:n, :], ACT.Copy).then_inc(s_hi, 1)

                def mid(m):
                    i = (s * NS + m) % 2
                    n = P if m < 6 else KV * HD
                    act.wait_ge(s_r, blk * NS + (m + 3))
                    sc.activation(part[m][0:n, 1, :], rr[i][0:n, :], ACT.Copy).then_inc(s_mid, 1)

                def take(m):
                    act.wait_ge(s_pr, blk * 13 + (m + 1))
                    act.wait_ge(s_r, blk * NS + (m + 1))
                    sc.activation(xf[(s * NS + m) % 2][:, :], ps[BANK[m]][:, :], ACT.Identity,
                                  bias=(baq[:, m:m + 1] if m < 2 else ba[:, m:m + 1]),
                                  scale=(SCALE if m < 2 else 1.0)).then_inc(s_pa, 1)
                    act.wait_ge(s_pa, blk * 4 + (m + 5))
                    high(m)

                if more:
                    scale_ffn(*behind(ip, s))
                take(0)
                take(1)
                mid(0)
                mid(1)
                if more:
                    deviation(*behind(ip, s))
                take(2)
                take(3)
                mid(2)
                mid(3)
                if more:
                    squares(*behind(ip, s))
                    take_xT(*behind(ip, s))
                for m in (4, 5):
                    act.wait_ge(s_xf, blk * 3 + (m - 3))
                    high(m)
                mid(4)
                mid(5)
                if more:
                    take_hT(*behind(ip, s))
                act.wait_ge(s_xf, blk * 3 + 3)
                high(6)
                mid(6)

            run(act, alone, both)

        @block.vector
        def _(dve):
            ch = Chain(dve, s_dve)
            v = nc.vector
            dve.sem_inc(s_x1, 2)
            dve.sem_inc(s_pd, 1)
            dve.sem_inc(s_r, 2)
            dve.sem_inc(s_lo, 2)
            dve.wait_ge(s_w, NW * 16)
            dve.wait_ge(s_zero, 2)
            ch.did(v.tensor_scalar(w_sgn[:, :, :], w_raw[:, :, :], 0.0, 2.0, ALU.is_ge, ALU.mult))
            ch.did(v.tensor_scalar(c_mat[P // 2:P, :], c_mat[P // 2:P, :], -1.0, None, ALU.mult))
            ch.did(v.tensor_scalar(baq[:, :], ba[:, 0:KD], SCALE, None, ALU.mult))
            ch.settle()
            v.tensor_scalar(w_sgn[:, :, :], w_sgn[:, :, :], -1.0, None, ALU.add).then_inc(s_wp, 1)

            def form_u(ip, s):
                blk = ip * 2 + s
                for k in range(KD):
                    dve.wait_ge(s_fs, blk * KD + (k + 1))
                    ch.did(v.tensor_scalar(fs[:, k, :], f[:, k, :], -CLIP, CLIP, ALU.max, ALU.min))
                    dve.wait_ge(s_c, blk * KD + (k + 1))
                    ch.did(v.scalar_tensor_tensor(u[:, k, :], xnT[:, k, ds(blk * BT, BT)], cols[:, k, 0:1],
                                                  ps[k][:, :], ALU.mult, ALU.add))
                    ch.settle()
                    v.tensor_tensor(u[:, k, :], u[:, k, :], fs[:, k, :], ALU.add).then_inc(s_u, 1)

            def add_residual(ip, s):
                blk = ip * 2 + s
                dve.wait_ge(s_x[s], ip * 16 + 16)
                dve.wait_ge(s_st[s], ip * 32 + 16)
                for q in range(2):
                    dve.wait_ge(s_ut, blk * 2 + (q + 1))
                    ins = v.tensor_tensor(x1[s][:, 2 * q:2 * q + 2, :],
                                          ps[2 + q][:, :].rearrange("p (j d) -> p j d", j=2),
                                          x_in[s][:, 2 * q:2 * q + 2, :], ALU.add)
                ins.then_inc(s_x1, 1)
                dve.wait_ge(s_x1, blk + 3)
                for j in range(TPB):
                    ch.did(v.bn_stats(stats[:, j, :], x1[s][:, j, :]))
                ch.settle()
                v.tensor_copy(rs_pad[:, :], stats[:, 0, 0:1])
                for j in range(TPB):
                    ch.did(v.bn_aggr(mv[:, j, :], stats[:, j, :]))
                ch.settle()
                v.tensor_scalar(mv[:, :, 1], mv[:, :, 1], LN_EPS, None, ALU.add).then_inc(s_var, 1)

            def normalise(ip, s):
                dve.wait_ge(s_sd, ip * 2 + (s + 1))
                ch.did(v.reciprocal(rs[:, 0, :], sd[:, 0, :]))
                ch.settle()
                for j in range(TPB):
                    ins = v.tensor_scalar(xn2[s][:, j, :], x1[s][:, j, :], mv[:, j, 0:1], rs[:, 0, j:j + 1],
                                          ALU.subtract, ALU.mult)
                ins.then_inc(s_xn, 1)

            def mean_square(ip, s):
                dve.wait_ge(s_sq, ip * 2 + (s + 1))
                v.tensor_scalar(msv[:, :], ms[:, :], 1.0 / D, LN_EPS, ALU.mult, ALU.add).then_inc(s_ms, 1)

            def form_h(ip, s):
                dve.wait_ge(s_rsd, ip * 2 + (s + 1))
                ch.did(v.reciprocal(rs[:, 1, :], sd[:, 1, :]))
                ch.settle()
                for j in range(TPB):
                    ins = v.tensor_scalar(h[:, j, :], xn2[s][:, j, :], rs[:, 1, j:j + 1], None, ALU.mult)
                ins.then_inc(s_h, 1)

            def alone():
                for stage in (form_u, add_residual, normalise, mean_square, form_h):
                    stage(0, 0)

            def both(ip, s, more, ahead):
                blk, b = ip * 2 + s, ip // 2
                tok = (ip % 2) * (2 * BT) + s * BT

                def rest(m):
                    i = (s * NS + m) % 2
                    n = P if m < 6 else KV * HD
                    dve.wait_ge(s_lo, blk * NS + (m + 1))
                    dve.wait_ge(s_hi, blk * NS + (m + 1))
                    v.tensor_tensor(rr[i][0:n, :], xf[i][0:n, :], part[m][0:n, 0, :], ALU.subtract).then_inc(s_r, 1)

                def low(m):
                    i = (s * NS + m) % 2
                    n = P if m < 6 else KV * HD
                    dve.wait_ge(s_mid, blk * NS + (m + 1))
                    v.tensor_tensor(part[m][0:n, 2, :], rr[i][0:n, :], part[m][0:n, 1, :],
                                    ALU.subtract).then_inc(s_lo, 1)

                def rope(m):
                    rot = rots[m % 2]
                    i = (s * NS + m) % 2
                    n = P if m < 6 else KV * HD
                    a, r = (6, 8, 10)[m - 4], (7, 9, 11)[m - 4]
                    sc = SCALE if m < 6 else 1.0
                    dve.wait_ge(s_pr, blk * 13 + (r + 1))
                    ch.did(v.scalar_tensor_tensor(xf[i][0:n, :], ps[BANK[a % 4]][0:n, :], sc,
                                                  cos[0:n, ds(tok, BT)], ALU.mult, ALU.mult))
                    v.scalar_tensor_tensor(rot[0:n, :], ps[BANK[r % 4]][0:n, :], sc, sin[0:n, ds(tok, BT)],
                                           ALU.mult, ALU.mult).then_inc(s_pd, 1)
                    dve.wait_ge(s_pd, blk * NDVE + m)
                    v.tensor_tensor(xf[i][0:n, :], xf[i][0:n, :], rot[0:n, :], ALU.add).then_inc(s_xf, 1)

                if more:
                    form_u(*behind(ip, s))
                for stage in (rest, low):
                    stage(0)
                    stage(1)
                if more:
                    add_residual(*behind(ip, s))
                rest(2)
                rest(3)
                if more:
                    normalise(*behind(ip, s))
                low(2)
                low(3)
                dve.wait_ge(s_vst, blk * 32 + 16)
                for q in range(2):
                    dve.wait_ge(s_pr, blk * 13 + (5 + q))
                    for i in range(2):
                        ins = v.tensor_tensor(
                            va[:, 2 * q + i, :, 0:HD],
                            ps[BANK[q]][:, i * D:(i + 1) * D].rearrange("p (h c) -> p h c", c=HD),
                            bv[:, :].rearrange("p (h c) -> p h c", c=HD), ALU.add)
                    ins.then_inc(s_pd, 1)
                dve.wait_ge(s_pd, blk * NDVE + 3)
                dve.sem_inc(s_va, 1)
                if more:
                    mean_square(*behind(ip, s))
                rope(4)
                if more:
                    form_h(*behind(ip, s))
                rope(5)
                for stage in (rest, low):
                    stage(4)
                    stage(5)
                rope(6)
                rest(6)
                low(6)
                dve.wait_ge(s_pr, blk * 13 + 13)
                v.tensor_copy(vb[:, :, :, 0:HD].rearrange("p j h c -> p (j h) c"),
                              ps[BANK[0]][:, 0:TPB * KV * HD].rearrange("p (n c) -> p n c", c=HD)).then_inc(s_pd, 1)
                dve.wait_ge(s_pd, blk * NDVE + 7)
                dve.sem_inc(s_va, 1)

            alone()
            with dve.Fori(0, NBLK // 2 - 1) as ip:
                ch.enter(ip, 2 * (2 * KD + 2 * TPB + 2 + 3))
                for s in range(2):
                    both(ip, s, True, True)
            ch.leave(NBLK // 2 - 1)
            both(NBLK // 2 - 1, 0, True, False)
            both(NBLK // 2 - 1, 1, False, False)


STEPS = 2 * NGB
QB = 512
NQB = L // QB
KT = L // P
LAG = 3 * GH
NPB = 12
WIDE = 512
RING = 3


LOWEST = -3.0e38
APART = 1024


def score_tiles():
    return [(qb, kt, h) for qb in range(NQB) for kt in range(4 * (qb + 1)) for h in range(GH)]


def max_tiles():
    return [(h, qt, k0, min(WIDE, (qt + 1) * P - k0))
            for h in range(GH) for qt in range(KT) for k0 in range(0, (qt + 1) * P, WIDE)]


def columns(qb, kt):
    return max(0, kt * P - qb * QB)


def order(first, last):
    scores, maxes = ([] if first else score_tiles()), ([] if last else max_tiles())
    total_s = sum(QB - columns(qb, kt) for qb, kt, _ in scores)
    total_m = sum(w for *_, w in maxes)
    pe, act, dve, link, out = 0.0, 0.0, 0.0, 185.0, []
    exped, copied, reduced = {}, {}, {}
    u, v, m, done_s, done_m, rows_at, turns = 0, 0, 0, 0, 0, None, []
    while v < len(scores) or m < len(maxes):
        if rows_at is not None and u >= min(rows_at, len(scores)):
            out.append(("rows", 0))
            dve = max(dve, reduced[m - 1]) + 1100
            pe = max(pe, dve + link) + 170
            dve = max(dve, pe + link) + 260
            rows_at = None
            continue
        if turns and u >= turns[0][0] and copied[turns[0][1]] + link <= pe + 50:
            out.append(("turn", turns.pop(0)[1]))
            pe += 440
            dve = max(dve, pe + link) + 560
            continue
        ready = {}
        if u < len(scores) and u - v < LAG:
            ready["score"] = max(pe, exped.get(u - RING, 0) + link)
        if v + GH <= u:
            ready["value"] = max(pe, exped[v + GH - 1] + link,
                                 copied.get(scores[v][0] - 1, 0) + link if scores[v][1] == 0 else 0)
        if m < len(maxes):
            ready["max"] = max(pe, reduced.get(m - RING, 0) + link)
        soonest = min(ready.values())
        now = {what for what, at in ready.items() if at <= soonest}
        if "value" in now and (u - v >= LAG or u == len(scores)):
            what = "value"
        elif "max" in now and done_m * total_s <= total_m * 1.02 * done_s:
            what = "max"
        else:
            what = [w for w in ("score", "value", "max") if w in now][0]
        pe = ready[what]
        if what == "score":
            out.append(("score", u))
            qb, kt, _ = scores[u]
            c = QB - columns(qb, kt)
            pe += c / 2.4 + (59 if kt >= 4 * qb else 3)
            act = max(act, pe + link) + 51 + c / 1.2
            exped[u] = act
            done_s += c
            u += 1
        elif what == "value":
            out += [("value", v + h) for h in range(GH)]
            qb, kt, _ = scores[v]
            pe += GH * (QB - columns(qb, kt)) / 2.4 + 62
            v += GH
            if v == len(scores) or scores[v][0] != qb:
                act = max(act, pe + link) + 51 + QB / 1.2
                copied[qb] = act
                turns.append((u + GH, qb))
        else:
            out.append(("max", m))
            w = maxes[m][3]
            pe += w / 2.4 + 62
            dve = max(dve, pe + link) + 65 + w / 0.96
            reduced[m] = dve
            done_m += w
            m += 1
            if m == len(maxes):
                rows_at = u + 6
    if rows_at is not None:
        out.append(("rows", 0))
    return out + [("turn", qb) for _, qb in turns]


def attention(nc, A, M):
    with ExitStack() as ctx:
        def sb(name, shape, dt=F32):
            return ctx.enter_context(nc.sbuf_tensor(name, shape, dt))

        def sem(name):
            return nc.alloc_semaphore(name)

        ps, ident = M["ps"], M["ident"]
        q_op = [sb(f"a_q{i}", [ROWS, GH, L], BF16) for i in range(3)]
        k_op = [sb(f"a_k{i}", [ROWS, GH, L], BF16) for i in range(3)]
        v_op = [sb(f"a_v{i}", [P, KT, GH * VW]) for i in range(3)]
        prob = [sb(f"a_p{i}", [P, QB]) for i in range(NPB)]
        identb = sb("a_identb", [P, P], BF16)
        mask_q = sb("a_maskq", [P, P], BF16)
        mask_k = sb("a_maskk", [P, P], BF16)
        mx = sb("a_mx", [P, GH, KT, L // WIDE])
        mneg = sb("a_mneg", [P, GH, KT])
        mrest = sb("a_mrest", [P, GH * KT])
        mpart = sb("a_mpart", [P, 3, P], BF16)
        mrow = sb("a_mrow", [GH * KT, 3, P], BF16)
        o_sb = [sb(f"a_o{i}", [P, QB]) for i in range(2)]
        rec = sb("a_rec", [P, 4, GH])
        o_row = [sb(f"a_orow{i}", [P, 4, GH * HD]) for i in range(2)]
        ps_max, ps_s = ps[0:RING], ps[RING:2 * RING]
        ps_o, ps_t = ps[6], ps[7]
        ps_tb = ps_t.bitcast(BF16)
        turned = ps_t.rearrange("p (j h c) -> p j h c", j=4, h=GH)

        s_c, s_z = sem("att_consts_loaded"), sem("att_zeroed")
        s_q = [sem(f"att_operands_loaded{i}") for i in range(3)]
        s_v = [sem(f"att_values_loaded{i}") for i in range(3)]
        s_mr = [sem(f"att_max_rows_stored{i}") for i in range(3)]
        s_mt = sem("att_max_tile_scored")
        s_md = sem("att_max_tile_reduced")
        s_sc = sem("att_scored")
        s_ex = sem("att_exp_done")
        s_pv = sem("att_value_product")
        s_oe = sem("att_out_copied")
        s_tt = sem("att_turned")
        s_te = sem("att_turned_taken")
        s_mp = sem("att_max_parts_ready")
        s_os = [sem(f"att_rows_stored{i}") for i in range(2)]
        s_dve, s_zs = sem("att_dve"), sem("att_zeros_stored")
        zeros = sb("a_zeros", [P, 4, D])
        TURNS_AHEAD = NQB + 1
        tiles, maxes = score_tiles(), max_tiles()
        NSC, NMX = len(tiles), len(maxes)
        USES = NQB + 1
        NL = (2 * NPROD + 2) * 16
        va_d = M["va_d"].rearrange("(k p) c -> p k c", p=P)
        vb_d = M["vb_d"].rearrange("(k p) c -> p k c", p=P)

        def run(eng, step):
            for r0 in (0, NGB):
                with eng.Fori(0, 2) as i:
                    for r in range(3):
                        step(r0 + r, i)
                step(r0 + 6, 0)
                step(r0 + 7, 0)

        def before(t, n):
            return t * n

        def filled(r, i):
            return i + (r // 3 + 1)

        def uses_in(work):
            return {e: n for n, e in enumerate(e for e in work if e[0] in ("rows", "turn"))}

        def work_of(r):
            return order(False, r == STEPS - 1)

        def uses_before(t):
            return t * USES + 1

        WORK = order(False, False)
        LAST_TURNS = {n: uses_in(WORK)[("turn", n)] for n in range(NQB)}
        block = ctx.enter_context(nc.Block())

        @block.sync
        def _(sp):
            def load(r, i):
                t, o = r + i * 3, r % 3
                second = r >= NGB
                heads = 1 if second else GH
                tb = t - NGB if second else t
                b = tb // NG
                g = tb % NG
                q_d, k_d = (M["qb_d"], M["kb_d"]) if second else (M["qa_d"], M["ka_d"])
                for n in range(NPROD):
                    at = AUG + n * HD
                    sp.dma_start(q_op[o][at:at + HD, :, :],
                                 q_d[PROD_Q[n], ds(tb * (GH * HD), GH * HD), :].rearrange("(h d) t -> d h t", d=HD)
                                 ).then_inc(s_q[o], 16)
                    sp.dma_start(k_op[o][at:at + HD, 0:heads, :],
                                 k_d[PROD_K[n], ds(tb * (heads * HD), heads * HD), :].rearrange(
                                     "(h d) t -> d h t", d=HD)).then_inc(s_q[o], 16)
                if second:
                    sp.dma_start(q_op[o][0:AUG, :, :], A["c_qb"]).then_inc(s_q[o], 16)
                    sp.dma_start(k_op[o][0:AUG, 0, :], A["c_kb"]).then_inc(s_q[o], 16)
                    sp.dma_start(v_op[o][:, :, 0:VW],
                                 vb_d[:, ds(b * KT, KT), ds(g * VW, VW)]).then_inc(s_v[o], 16)
                else:
                    sp.dma_start(q_op[o][0:AUG, :, :], A["c_qa"][:, ds(g * GH, GH), :]).then_inc(s_q[o], 16)
                    sp.dma_start(k_op[o][0:AUG, :, :], A["c_ka"][:, ds(g * GH, GH), :]).then_inc(s_q[o], 16)
                    sp.dma_start(v_op[o][:, :, :],
                                 va_d[:, ds(b * KT, KT), ds(g * GH * VW, GH * VW)]).then_inc(s_v[o], 16)

            def rows(r, i, use):
                sp.wait_ge(s_te, use + 2)
                for c in range(3):
                    sp.dma_start(q_op[r % 3][MROW + c:MROW + c + 1, :, :].rearrange("o h (k p) -> o (h k) p", p=P),
                                 mrow[:, c, :]
                                 ).then_inc(s_mr[r % 3], 16)

            for o in range(2):
                sp.sem_inc(s_os[o], 16)
            for dst, src in ((identb, "c_identb"), (mask_q, "c_maskq"), (mask_k, "c_maskk")):
                sp.dma_start(dst[:, :], A[src]).then_inc(s_c, 16)
            load(0, 0)
            load(1, 0)
            rows(0, 0, 0)

            def step(r, i):
                t = r + i * 3
                if r + 2 < STEPS:
                    sp.wait_ge(s_pv, before(t, NSC) + NPB)
                    load(r + 2, i)
                tb = t - NGB if r >= NGB else t
                b, g = tb // NG, tb % NG
                ao = M["ao_d"][r // NGB].rearrange("(k p) c -> p k c", p=P)
                for (what, n), use in uses_in(work_of(r)).items():
                    if what == "rows":
                        rows(r + 1, i, uses_before(t) + use)
                    else:
                        sp.wait_ge(s_te, uses_before(t) + (use + 2))
                        sp.dma_start(ao[:, ds(b * KT + n * 4, 4), ds(g * (GH * HD), GH * HD)],
                                     o_row[n % 2][:, :, :]).then_inc(s_os[n % 2], 16)

            run(sp, step)
            for o in range(2):
                sp.wait_ge(s_os[o], STEPS * NQB // 2 * 16 + 16)

        @block.gpsimd
        def _(pool):
            nc.gpsimd.memset(mpart[:, :, :], 0.0).then_inc(s_z, 1)
            nc.gpsimd.memset(mx[:, :, :, :], LOWEST).then_inc(s_z, 1)
            nc.gpsimd.memset(zeros[:, :, :], 0.0).then_inc(s_z, 1)
            pool.wait_ge(s_z, 3)
            hs = M["hs_d"].rearrange("(n p) d -> p n d", p=P)
            for n in range(0, NTILES, 4):
                pool.dma_start(hs[:, n:n + 4, :], zeros[:, :, :]).then_inc(s_zs, 16)
            pool.wait_ge(s_zs, NTILES // 4 * 16)

        @block.tensor
        def _(pe):
            pe.sem_inc(s_tt, TURNS_AHEAD)
            pe.sem_inc(s_pv, NPB)
            pe.wait_ge(s_c, 48)
            pe.wait_ge(s_z, 2)

            def max_tile(r, i, t, m):
                h, qt, k0, w = maxes[m]
                o, hk = r % 3, (0 if r >= NGB else h)
                if m == 0 and r > 0:
                    pe.wait_ge(s_q[o], filled(r, i) * NL)
                pe.wait_ge(s_md, before(t, NMX) + (max(m + 1, RING) + APART))
                out = ps_max[m % RING][:, 0:w]
                diagonal = k0 + w == (qt + 1) * P
                ins = pe.matmul(out, q_op[o][:, h, qt * P:(qt + 1) * P], k_op[o][:, hk, k0:k0 + w],
                                start=True, stop=not diagonal)
                if diagonal:
                    ins = pe.matmul(out[:, w - P:w], identb[:, :], mask_q[:, :], start=False, stop=True)
                ins.then_inc(s_mt, 1)

            def turn_rows(n_step, use):
                pe.wait_ge(s_mp, n_step + 1)
                pe.wait_ge(s_te, use + 1)
                for c in range(3):
                    ins = pe.transpose(ps_tb[:, c * P:(c + 1) * P], mpart[:, c, :], identb[:, :])
                ins.then_inc(s_tt, 1)

            pe.wait_ge(s_q[0], NL)
            for what, m in order(True, False):
                if what == "max":
                    max_tile(0, 0, 0, m)
                else:
                    turn_rows(0, 0)

            def step(r, i):
                t, o = r + i * 3, r % 3
                work = work_of(r)
                use = uses_in(work)
                for what, n in work:
                    if what == "max":
                        max_tile(r + 1, i, t + 1, n)
                    elif what == "rows":
                        turn_rows(t + 1, uses_before(t) + use[("rows", 0)])
                    elif what == "score":
                        qb, kt, h = tiles[n]
                        c0, hk = columns(qb, kt), (0 if r >= NGB else h)
                        out = ps_s[n % RING]
                        if n == 0:
                            pe.wait_ge(s_mr[o], filled(r, i) * 48)
                        pe.wait_ge(s_ex, before(t, NSC) + max(n + 1, RING))
                        diagonal = kt >= 4 * qb
                        ins = pe.matmul(out[:, c0:QB], k_op[o][:, hk, kt * P:(kt + 1) * P],
                                        q_op[o][:, h, qb * QB + c0:(qb + 1) * QB], start=True, stop=not diagonal)
                        if diagonal:
                            ins = pe.matmul(out[:, c0:c0 + P], identb[:, :], mask_k[:, :], start=False, stop=True)
                        ins.then_inc(s_sc, 1)
                    elif what == "value":
                        qb, kt, h = tiles[n]
                        c0, hk = columns(qb, kt), (0 if r >= NGB else h)
                        if n == 0:
                            pe.wait_ge(s_v[o], filled(r, i) * 16)
                        if kt == 0 and h == 0:
                            pe.wait_ge(s_oe, before(t, NQB) + (qb + 1))
                        if h == 0:
                            pe.wait_ge(s_ex, before(t, NSC) + (n + GH + RING))
                        pe.matmul(ps_o[VW * h:VW * h + VW, c0:QB], v_op[o][:, kt, hk * VW:hk * VW + VW],
                                  prob[n % NPB][:, c0:QB], start=(kt == 0), stop=(kt == 4 * qb + 3)
                                  ).then_inc(s_pv, 1)
                    else:
                        pe.wait_ge(s_oe, before(t, NQB) + (n + 2))
                        pe.wait_ge(s_te, uses_before(t) + (use[("turn", n)] + 1))
                        for j in range(4):
                            ins = pe.transpose(ps_t[:, j * P:(j + 1) * P], o_sb[n % 2][:, j * P:(j + 1) * P],
                                               ident[:, :])
                        ins.then_inc(s_tt, 1)

            run(pe, step)

        @block.scalar
        def _(act):
            act.sem_inc(s_ex, RING)
            act.sem_inc(s_oe, 1)

            def step(r, i):
                t = r + i * 3
                for what, n in work_of(r):
                    if what == "score":
                        qb, kt, h = tiles[n]
                        c0 = columns(qb, kt)
                        act.wait_ge(s_sc, before(t, NSC) + (n + 1))
                        act.wait_ge(s_pv, before(t, NSC) + max(n + 1, NPB))
                        nc.scalar.activation(prob[n % NPB][:, c0:QB], ps_s[n % RING][:, c0:QB], ACT.Exp
                                             ).then_inc(s_ex, 1)
                    elif what == "value" and (n + 1 == NSC or tiles[n + 1][0] != tiles[n][0]):
                        qb = tiles[n][0]
                        act.wait_ge(s_pv, before(t, NSC) + (n + 1 + NPB))
                        at = (uses_before(t) + LAST_TURNS[qb - 2] if qb >= 2
                              else uses_before(t) - USES + LAST_TURNS[qb + 2])
                        act.wait_ge(s_tt, at + (1 + TURNS_AHEAD))
                        nc.scalar.activation(o_sb[qb % 2][:, :], ps_o[:, :], ACT.Copy).then_inc(s_oe, 1)

            run(act, step)

        @block.vector
        def _(dve):
            v = nc.vector
            ch = Chain(dve, s_dve)
            dve.sem_inc(s_md, RING + APART)
            dve.sem_inc(s_te, 1)
            dve.wait_ge(s_z, 2)
            NSTEP = 4 + NQB

            def max_tile(t, m):
                h, qt, k0, w = maxes[m]
                dve.wait_ge(s_mt, before(t, NMX) + (m + 1))
                v.tensor_reduce(mx[:, h, qt, k0 // WIDE:k0 // WIDE + 1], ps_max[m % RING][:, 0:w], AX.X,
                                ALU.max).then_inc(s_md, 1)

            def rows(t, use, link, settle):
                dve.wait_ge(s_md, before(t, NMX) + (NMX + RING + APART))
                link(v.tensor_reduce(mneg[:, :, :], mx[:, :, :, :], AX.X, ALU.max, negate=True))
                settle()
                flat = mneg[:, :, :].rearrange("p h k -> p (h k)")
                n = GH * KT
                link(v.tensor_copy(mpart[:, 0, 0:n], flat))
                settle()
                link(v.tensor_tensor(mrest[:, :], flat, mpart[:, 0, 0:n], ALU.subtract))
                settle()
                link(v.tensor_copy(mpart[:, 1, 0:n], mrest[:, :]))
                settle()
                v.tensor_tensor(mpart[:, 2, 0:n], mrest[:, :], mpart[:, 1, 0:n], ALU.subtract).then_inc(s_mp, 1)
                dve.wait_ge(s_tt, use + (1 + TURNS_AHEAD))
                v.tensor_copy(mrow[:, :, :], ps_tb[0:n, 0:3 * P].rearrange("p (c q) -> p c q", c=3)
                              ).then_inc(s_te, 1)

            for what, m in order(True, False):
                if what == "max":
                    max_tile(0, m)
                else:
                    rows(0, 0, ch.did, ch.settle)

            def step(r, i):
                t = r + i * 3
                work = work_of(r)
                use = uses_in(work)
                for what, n in work:
                    if what == "max":
                        max_tile(t + 1, n)
                    elif what == "rows":
                        dve.wait_ge(s_mr[r % 3], filled(r, i) * 48)
                        rows(t + 1, uses_before(t) + use[("rows", 0)], ch.did, ch.settle)
                    elif what == "turn":
                        dve.wait_ge(s_tt, uses_before(t) + (use[("turn", n)] + 1 + TURNS_AHEAD))
                        ch.did(v.reciprocal(rec[:, :, :], turned[:, :, :, HD]))
                        ch.settle()
                        dve.wait_ge(s_os[n % 2], before(t, NQB // 2 * 16) + (n // 2 * 16 + 16))
                        v.tensor_tensor(o_row[n % 2][:, :, :].rearrange("p j (h c) -> p j h c", h=GH),
                                        turned[:, :, :, 0:HD],
                                        rec[:, :, :].unsqueeze(3).to_broadcast([P, 4, GH, HD]), ALU.mult
                                        ).then_inc(s_te, 1)

            for r0 in (0, NGB):
                with dve.Fori(0, 2) as i:
                    ch.enter(i, 3 * NSTEP)
                    for r in range(3):
                        step(r0 + r, i)
                ch.leave(2)
                step(r0 + 6, 0)
                step(r0 + 7, 0)


def after(nc, A, M):
    with ExitStack() as ctx:
        def sb(name, shape, dt=F32):
            return ctx.enter_context(nc.sbuf_tensor(name, shape, dt))

        def sem(name):
            return nc.alloc_semaphore(name)

        ps, ident, res, h2r, lg = M["ps"], M["ident"], M["res"], M["h2_rows"], M["logits"]
        ao = [[sb(f"p_ao{a}{s}", [P, TPB, D]) for s in range(2)] for a in range(2)]
        x1 = [sb(f"p_x1{s}", [P, TPB, D]) for s in range(2)]
        xn = [sb(f"p_xn{s}", [P, TPB, D]) for s in range(2)]
        aoT = [sb(f"p_aoT{a}", [P, KD, BT]) for a in range(2)]
        w = [sb(f"p_w{a}", [P, KD, D]) for a in range(2)]
        bo = sb("p_bo", [P, D])
        xp = sb("p_xp", [P, TPB, D])
        r = sb("p_r", [P, TPB, D])
        sq = sb("p_sq", [P, TPB, D], BF16)
        h2 = sb("p_h2", [P, TPB, D])
        h2T = sb("p_h2T", [P, KD, BT])
        ms, msv, sd, rs = (sb(f"p_{n}", [P, TPB]) for n in ("ms", "msv", "sd", "rs"))
        ln2 = sb("p_ln2", [P, D])
        gate = sb("p_gate", [P, KD, NE])
        lgT = sb("p_lgT", [P, BT])

        s_w, s_z = sem("post_weights_loaded"), sem("post_zeroed")
        s_in = [sem(f"post_rows_loaded{s}") for s in range(2)]
        s_at, s_aoT = sem("post_attention_turned"), sem("post_aoT_ready")
        s_pj, s_xp = sem("post_projected"), sem("post_residual_ready")
        s_sq, s_ms, s_sd = sem("post_squares_summed"), sem("post_mean_square"), sem("post_rms_ready")
        s_h, s_ht, s_hT = sem("post_h_ready"), sem("post_h_turned"), sem("post_hT_ready")
        s_lt, s_lc, s_lx, s_lg = (sem("post_logits_transposed"), sem("post_logits_copied"),
                                  sem("post_logits_turned"), sem("post_logits_ready"))
        s_hk = sem("post_h_kept")
        s_dve = sem("post_dve")
        rows = [M["ao_d"][0], M["ao_d"][1], M["x1_d"], M["xn_d"]]
        rows = [d.rearrange("(n p) d -> p n d", p=P) for d in rows]
        block = ctx.enter_context(nc.Block())

        @block.sync
        def _(sp):
            for dst, src in ((w[0][:, :, :], A["w_out"].rearrange("(k p) m -> p k m", p=P)),
                             (w[1][:, :, :], A["wo"].rearrange("(k p) m -> p k m", p=P)),
                             (gate[:, :, :], A["gate"].rearrange("(k p) m -> p k m", p=P)),
                             (ln2[:, :], A["ln2"].partition_broadcast(P)),
                             (bo[:, :], A["b_out"].partition_broadcast(P))):
                sp.dma_start(dst, src).then_inc(s_w, 16)
            with sp.Fori(0, NBLK // 2) as ip:
                for s in range(2):
                    blk = ip * 2 + s
                    sp.wait_ge(s_xp, blk + 1)
                    for tile, d in zip((ao[0][s], ao[1][s], x1[s], xn[s]), rows):
                        sp.dma_start(tile[:, :, :], d[:, ds(blk * TPB, TPB), :]).then_inc(s_in[s], 16)
            sp.dma_start(M["w13"][:, :, :], A["w13"].rearrange("e (k p) m -> p (e k) m", p=P)).then_inc(M["s_w13"], 16)

        @block.gpsimd
        def _(pool):
            nc.gpsimd.memset(lgT[:, :], 0.0).then_inc(s_z, 1)
            pool.sem_inc(s_hk, 1)
            with pool.Fori(0, NBLK) as blk:
                pool.wait_ge(s_h, blk + 1)
                nc.gpsimd.tensor_copy(h2r[:, ds(blk * TPB, TPB), :], h2[:, :, :]).then_inc(s_hk, 1)

        def run(eng, first, both, last):
            first(0, 0)
            with eng.Fori(0, NBLK // 2 - 1) as ip:
                both(ip, 0, ip, 1)
                both(ip, 1, ip + 1, 0)
            ip = NBLK // 2 - 1
            both(ip, 0, ip, 1)
            last(ip, 1)

        @block.tensor
        def _(pe):
            def front(ip, s):
                blk = ip * 2 + s
                pe.wait_ge(s_in[s], ip * 64 + 64)
                for a in range(2):
                    for k in range(KD):
                        for j in range(TPB):
                            ins = pe.transpose(ps[2 * a + k][:, j * P:(j + 1) * P],
                                               ao[a][s][:, j, k * P:(k + 1) * P], ident[:, :])
                        ins.then_inc(s_at, 1)
                pe.wait_ge(s_xp, blk + 2)
                for a in range(2):
                    pe.wait_ge(s_aoT, blk * 4 + (2 * a + 2))
                    for j in range(TPB):
                        for k in range(KD):
                            ins = pe.matmul(ps[4 + 2 * a + j // 2][:, j % 2 * D:(j % 2 + 1) * D],
                                            aoT[a][:, k, j * P:(j + 1) * P], w[a][:, k, :],
                                            start=(k == 0), stop=(k == KD - 1))
                    ins.then_inc(s_pj, 1)

            def back(ip, s):
                blk = ip * 2 + s
                pe.wait_ge(s_h, blk + 1)
                for k in range(KD):
                    for j in range(TPB):
                        ins = pe.transpose(ps[k][:, j * P:(j + 1) * P], h2[:, j, k * P:(k + 1) * P], ident[:, :])
                    ins.then_inc(s_ht, 1)
                pe.wait_ge(s_hT, blk * KD + KD)
                for k in range(KD):
                    ins = pe.matmul(ps[2][0:NE, :], gate[:, k, :], h2T[:, k, :],
                                    start=(k == 0), stop=(k == KD - 1))
                ins.then_inc(s_lt, 1)
                pe.wait_ge(s_lc, blk + 1)
                for j in range(TPB):
                    ins = pe.transpose(ps[3][:, j * P:(j + 1) * P], lgT[:, j * P:(j + 1) * P], ident[:, :])
                ins.then_inc(s_lx, 1)
                pe.wait_ge(s_lg, blk + 1)

            def both(ip, s, ip_next, s_next):
                front(ip_next, s_next)
                back(ip, s)

            pe.wait_ge(s_w, 80)
            pe.wait_ge(s_z, 1)
            run(pe, front, both, back)

        @block.scalar
        def _(act):
            sc = nc.scalar
            act.wait_ge(s_w, 80)

            def turned(ip, s):
                blk = ip * 2 + s
                for a in range(2):
                    for k in range(KD):
                        act.wait_ge(s_at, blk * 4 + (2 * a + k + 1))
                        sc.activation(aoT[a][:, k, :], ps[2 * a + k][:, :], ACT.Copy).then_inc(s_aoT, 1)

            def norm(ip, s):
                blk = ip * 2 + s
                act.wait_ge(s_xp, blk + 3)
                for j in range(TPB):
                    ins = sc.activation(sq[:, j, :], xp[:, j, :], ACT.Square, accum_out=ms[:, j:j + 1])
                ins.then_inc(s_sq, 1)
                act.wait_ge(s_ms, blk + 1)
                sc.activation(sd[:, :], msv[:, :], ACT.Sqrt).then_inc(s_sd, 1)

            def back(ip, s):
                blk = ip * 2 + s
                for k in range(KD):
                    act.wait_ge(s_ht, blk * KD + (k + 1))
                    sc.activation(h2T[:, k, :], ps[k][:, :], ACT.Copy).then_inc(s_hT, 1)
                act.wait_ge(s_lt, blk + 1)
                sc.activation(lgT[0:NE, :], ps[2][0:NE, :], ACT.Copy).then_inc(s_lc, 1)

            def first(ip, s):
                turned(ip, s)
                norm(ip, s)

            def both(ip, s, ip_next, s_next):
                turned(ip_next, s_next)
                back(ip, s)
                norm(ip_next, s_next)

            run(act, first, both, back)

        @block.vector
        def _(dve):
            v = nc.vector
            ch = Chain(dve, s_dve)
            dve.sem_inc(s_xp, 2)
            dve.wait_ge(s_w, 80)

            def residual(ip, s):
                blk = ip * 2 + s
                dve.wait_ge(s_in[s], ip * 64 + 64)
                dve.wait_ge(s_pj, blk * 2 + 1)
                for q in range(2):
                    two = slice(2 * q, 2 * q + 2)
                    ch.did(v.tensor_tensor(r[:, two, :], ps[4 + q].rearrange("p (j d) -> p j d", j=2),
                                           x1[s][:, two, :], ALU.add))
                ch.settle()
                ch.did(v.tensor_tensor(r[:, :, :], r[:, :, :], bo[:, :].unsqueeze(1).to_broadcast([P, TPB, D]),
                                       ALU.add))
                dve.wait_ge(s_pj, blk * 2 + 2)
                for q in range(2):
                    two = slice(2 * q, 2 * q + 2)
                    ch.did(v.tensor_tensor(xp[:, two, :], ps[6 + q].rearrange("p (j d) -> p j d", j=2),
                                           xn[s][:, two, :], ALU.add))
                ch.settle()
                v.tensor_tensor(res[:, ds(blk * TPB, TPB), :], r[:, :, :], xp[:, :, :], ALU.add).then_inc(s_xp, 1)

            def norm(ip, s):
                blk = ip * 2 + s
                dve.wait_ge(s_sq, blk + 1)
                v.tensor_scalar(msv[:, :], ms[:, :], 1.0 / D, LN_EPS, ALU.mult, ALU.add).then_inc(s_ms, 1)
                dve.wait_ge(s_sd, blk + 1)
                ch.did(v.reciprocal(rs[:, :], sd[:, :]))
                ch.settle()
                dve.wait_ge(s_hk, blk + 1)
                for j in range(TPB):
                    ins = v.scalar_tensor_tensor(h2[:, j, :], xp[:, j, :], rs[:, j:j + 1], ln2[:, :],
                                                 ALU.mult, ALU.mult)
                ins.then_inc(s_h, 1)

            def back(ip, s):
                blk = ip * 2 + s
                dve.wait_ge(s_lx, blk + 1)
                v.tensor_copy(lg[:, ds(blk * TPB, TPB), :],
                              ps[3].rearrange("p (j e) -> p j e", j=TPB)[:, :, 0:NE]).then_inc(s_lg, 1)

            def both(ip, s, ip_next, s_next):
                residual(ip_next, s_next)
                back(ip, s)
                norm(ip_next, s_next)

            residual(0, 0)
            norm(0, 0)
            with dve.Fori(0, NBLK // 2 - 1) as ip:
                ch.enter(ip, 2 * 6)
                both(ip, 0, ip, 1)
                both(ip, 1, ip + 1, 0)
            ch.leave(NBLK // 2 - 1)
            ip = NBLK // 2 - 1
            both(ip, 0, ip, 1)
            back(ip, 1)


TR = P
NTILES = TOK * 2 // TR + NE
PER = TOK // TR


def route(nc, A, M):
    with ExitStack() as ctx:
        def sb(name, shape, dt=F32):
            return ctx.enter_context(nc.sbuf_tensor(name, shape, dt))

        def sem(name):
            return nc.alloc_semaphore(name)

        ps, lg, h2r, pos, wt = M["ps"], M["logits"], M["h2_rows"], M["pos"], M["wt"]
        NT = TOK // P
        rank = sb("r_rank", [P, NE])
        steps = sb("r_steps", [P, NE, PER])
        tiles = sb("r_tiles", [P, NTILES])
        upper = sb("r_upper", [P, P])
        ones = sb("r_ones", [P, NE * NT])
        ex, pr, eq, p2 = (sb(f"r_{n}", [P, NT, NE]) for n in ("ex", "pr", "eq", "p2"))
        one = [sb(f"r_one{n}", [P, NT, NE]) for n in range(2)]
        m = [sb(f"r_m{n}", [P, NT]) for n in range(2)]
        rk, sm, rsm = (sb(f"r_{n}", [P, NT]) for n in ("rk", "sm", "rsm"))
        sel = sb("r_sel", [P, NE, NT])
        cum = sb("r_cum", [P, NE, NT])
        tot, base, full, need, end, count = (sb(f"r_{n}", [P, NE]) for n in
                                             ("tot", "base", "full", "need", "end", "count"))
        more = sb("r_more", [P, NE, PER])
        at = sb("r_at", [P, NTILES, NE])
        et = sb("r_et", [P, NTILES])
        posf = [sb(f"r_posf{n}", [P, NT]) for n in range(2)]

        s_w = sem("route_consts_loaded")
        s_arg, s_ex = sem("route_exp_argument"), sem("route_exp")
        s_tot, s_cnt = sem("route_totals_ready"), sem("route_counts_ready")
        s_pos, s_sc = sem("route_places_ready"), sem("route_rows_scattered")
        s_one, s_dve = sem("route_ones"), sem("route_dve")
        block = ctx.enter_context(nc.Block())

        @block.sync
        def _(sp):
            for dst, src in ((rank[:, :], "c_rank"), (steps[:, :, :], "c_steps"), (tiles[:, :], "c_tiles"),
                             (upper[:, :], "c_upper")):
                sp.dma_start(dst, A[src]).then_inc(s_w, 16)
            sp.dma_start(M["w2"][:, :, :], A["w2"].rearrange("e (k p) m -> p (e k) m", p=P)).then_inc(M["s_w2"], 16)

        @block.scalar
        def _(act):
            act.wait_ge(s_arg, 1)
            nc.scalar.activation(ex[:, :, :], ex[:, :, :], ACT.Exp).then_inc(s_ex, 1)

        @block.tensor
        def _(pe):
            pe.wait_ge(s_w, 64)
            pe.wait_ge(s_one, 1)
            pe.wait_ge(s_tot, 1)
            pe.matmul(ps[0][:, 0:NE], upper[:, :], tot[:, :], start=True, stop=True).then_inc(s_cnt, 1)
            pe.matmul(ps[1][:, 0:NE], ones[:, 0:P], tot[:, :], start=True, stop=True).then_inc(s_cnt, 1)

        @block.gpsimd
        def _(pool):
            nc.gpsimd.memset(ones[:, :], 1.0).then_inc(s_one, 1)
            pool.wait_ge(s_pos, 1)
            for n in range(NT):
                for c in range(2):
                    pool.indirect_dma_start(
                        out=M["hs_d"], out_offset=bass.IndirectOffsetOnAxis(ap=pos[c][:, n:n + 1], axis=0),
                        in_=h2r[:, n, :], in_offset=None).then_inc(s_sc, 16)
            pool.wait_ge(s_sc, NT * 2 * 16)

        @block.vector
        def _(dve):
            v = nc.vector
            ch = Chain(dve, s_dve)

            def wide(t):
                return t[:, :].unsqueeze(2).to_broadcast([P, NT, NE])

            def step(ins):
                ch.did(ins)
                ch.settle()

            dve.wait_ge(s_w, 64)
            step(v.tensor_reduce(m[0][:, :], lg[:, :, :], AX.X, ALU.max))
            v.tensor_tensor(ex[:, :, :], lg[:, :, :], wide(m[0]), ALU.subtract).then_inc(s_arg, 1)
            dve.wait_ge(s_ex, 1)
            step(v.tensor_reduce(sm[:, :], ex[:, :, :], AX.X, ALU.add))
            step(v.reciprocal(rsm[:, :], sm[:, :]))
            step(v.tensor_tensor(pr[:, :, :], ex[:, :, :], wide(rsm), ALU.mult))
            ranks = rank[:, :].unsqueeze(1).to_broadcast([P, NT, NE])

            def first_of_largest(m, one, p):
                step(v.tensor_reduce(m[:, :], p[:, :, :], AX.X, ALU.max))
                step(v.tensor_tensor(eq[:, :, :], p[:, :, :], wide(m), ALU.is_equal))
                step(v.tensor_tensor(eq[:, :, :], eq[:, :, :], ranks, ALU.mult))
                step(v.tensor_reduce(rk[:, :], eq[:, :, :], AX.X, ALU.max))
                step(v.tensor_tensor(one[:, :, :], eq[:, :, :], wide(rk), ALU.is_equal))

            first_of_largest(m[0], one[0], pr)
            step(v.scalar_tensor_tensor(p2[:, :, :], one[0][:, :, :], -2.0, pr[:, :, :], ALU.mult, ALU.add))
            first_of_largest(m[1], one[1], p2)
            step(v.tensor_tensor(sm[:, :], m[0][:, :], m[1][:, :], ALU.add))
            step(v.reciprocal(rsm[:, :], sm[:, :]))
            for c in range(2):
                step(v.tensor_tensor(wt[c][:, :], m[c][:, :], rsm[:, :], ALU.mult))
            dve.wait_ge(s_one, 1)
            step(v.tensor_tensor(sel[:, :, :].rearrange("p e n -> p n e"), one[0][:, :, :], one[1][:, :, :], ALU.add))
            step(v.tensor_tensor_scan(cum[:, :, :].rearrange("p e n -> p (e n)"), ones[:, :],
                                      sel[:, :, :].rearrange("p e n -> p (e n)"), 0.0, ALU.mult, ALU.add))
            step(v.tensor_copy(tot[:, 0:1], cum[:, 0:1, NT - 1]))
            v.tensor_tensor(tot[:, 1:], cum[:, 1:, NT - 1], cum[:, 0:NE - 1, NT - 1], ALU.subtract).then_inc(s_tot, 1)
            dve.wait_ge(s_cnt, 2)
            step(v.tensor_copy(count[:, :], ps[1][:, 0:NE]))
            step(v.tensor_tensor(more[:, :, :], count[:, :].unsqueeze(2).to_broadcast([P, NE, PER]), steps[:, :, :],
                                 ALU.is_gt))
            step(v.tensor_reduce(need[:, :], more[:, :, :], AX.X, ALU.add))
            step(v.tensor_tensor_scan(end[:, :], ones[:, 0:NE], need[:, :], 0.0, ALU.mult, ALU.add))
            step(v.tensor_tensor(full[:, :], end[:, :], need[:, :], ALU.subtract))
            step(v.scalar_tensor_tensor(base[:, :], full[:, :], float(TR), ps[0][:, 0:NE], ALU.mult, ALU.add))
            step(v.tensor_scalar(base[:, :], base[:, :], -1.0, None, ALU.add))
            step(v.tensor_tensor(base[:, 1:], base[:, 1:], cum[:, 0:NE - 1, NT - 1], ALU.subtract))
            step(v.tensor_tensor(cum[:, :, :], cum[:, :, :], base[:, :].unsqueeze(2).to_broadcast([P, NE, NT]),
                                 ALU.add))
            for c in range(2):
                step(v.tensor_tensor(eq[:, :, :], one[c][:, :, :], cum[:, :, :].rearrange("p e n -> p n e"), ALU.mult))
                step(v.tensor_reduce(posf[c][:, :], eq[:, :, :], AX.X, ALU.add))
                step(v.tensor_copy(pos[c][:, :], posf[c][:, :]))
            dve.sem_inc(s_pos, 1)
            step(v.tensor_tensor(at[:, :, :], tiles[:, :].unsqueeze(2).to_broadcast([P, NTILES, NE]),
                                 end[:, :].unsqueeze(1).to_broadcast([P, NTILES, NE]), ALU.is_ge))
            step(v.tensor_reduce(et[:, :], at[:, :, :], AX.X, ALU.add))
            step(v.tensor_scalar(et[:, :], et[:, :], float(NE - 1), None, ALU.min))
            step(v.tensor_copy(M["tile_expert"][:, :], et[:, :]))


def experts(nc, A, M, out):
    with ExitStack() as ctx:
        def sb(name, shape, dt=F32):
            return ctx.enter_context(nc.sbuf_tensor(name, shape, dt))

        def sem(name):
            return nc.alloc_semaphore(name)

        ps, ident, w13, w2 = M["ps"], M["ident"], M["w13"], M["w2"]
        x_in = [sb(f"e_x{s}", [P, D]) for s in range(2)]
        hT = [sb(f"e_hT{s}", [P, KD, P]) for s in range(2)]
        si = [sb(f"e_silu{s}", [P, FFN]) for s in range(2)]
        g = [sb(f"e_g{s}", [P, FFN]) for s in range(2)]
        gT = [sb(f"e_gT{s}", [P, FT, P]) for s in range(2)]
        y = [sb(f"e_y{s}", [P, D]) for s in range(2)]
        ps_g, ps_u = ps[0:2], ps[2:4]
        ps_t, ps_h, ps_y = ps[4:7]
        s_x = [sem(f"exp_rows_loaded{s}") for s in range(2)]
        s_ht, s_hT = sem("exp_rows_turned"), sem("exp_hT_ready")
        s_up, s_si, s_g = sem("exp_up_ready"), sem("exp_silu_ready"), sem("exp_product_ready")
        s_gt, s_gT = sem("exp_product_turned"), sem("exp_gT_ready")
        s_dn, s_y = sem("exp_down_ready"), sem("exp_result_copied")
        s_st = [sem(f"exp_results_stored{s}") for s in range(2)]
        AHEAD = 2
        hs_d = M["hs_d"].rearrange("(n p) d -> p n d", p=P)
        ys_d = M["ys_d"].rearrange("(n p) d -> p n d", p=P)
        block = ctx.enter_context(nc.Block())

        @block.sync
        def _(sp):
            for s in range(2):
                sp.sem_inc(s_st[s], 16)

            def load(n, s):
                sp.wait_ge(s_ht, n + 1)
                sp.dma_start(x_in[s][:, :], hs_d[:, ds(n, 1), :].rearrange("p o d -> p (o d)")).then_inc(s_x[s], 16)

            def store(n, s):
                sp.wait_ge(s_y, n + (1 + AHEAD))
                sp.dma_start(ys_d[:, ds(n, 1), :].rearrange("p o d -> p (o d)"), y[s][:, :]).then_inc(s_st[s], 16)

            for n in range(4):
                load(n, n % 2)
            with sp.Fori(0, NTILES // 2 - 2) as i:
                for s in range(2):
                    load(i * 2 + (s + 4), s)
                    store(i * 2 + s, s)
            for n in range(NTILES - 4, NTILES):
                store(n, n % 2)
            for s in range(2):
                sp.wait_ge(s_st[s], NTILES // 2 * 16 + 16)

        @block.tensor
        def _(pe):
            pe.sem_inc(s_ht, AHEAD)
            pe.sem_inc(s_gt, AHEAD)
            pe.sem_inc(s_dn, AHEAD)
            pe.wait_ge(M["s_w13"], 16)
            pe.wait_ge(M["s_w2"], 16)

            def expert(n):
                return pe.value_load(M["tile_expert"][0:1, ds(n, 1)], min_val=0, max_val=NE - 1)

            def turn_rows(i, n, s):
                pe.wait_ge(s_x[s], i * 16 + 16)
                pe.wait_ge(s_hT, n + AHEAD)
                for k in range(KD):
                    ins = pe.transpose(ps_h[:, k * P:(k + 1) * P], x_in[s][:, k * P:(k + 1) * P],
                                       ident[:, :])
                ins.then_inc(s_ht, 1)

            def up(n, s):
                e = expert(n)
                pe.wait_ge(s_hT, n + (1 + AHEAD))
                pe.wait_ge(s_g, n + 1)
                for part, bank in enumerate((ps_g[s], ps_u[s])):
                    for k in range(KD):
                        ins = pe.matmul(bank[:, :], hT[s][:, k, :],
                                        w13[:, ds(e * KD + k, 1), part * FFN:(part + 1) * FFN].rearrange(
                                            "p o m -> p (o m)"), start=(k == 0), stop=(k == KD - 1))
                ins.then_inc(s_up, 1)

            def turn_products(n, s):
                pe.wait_ge(s_g, n + (1 + AHEAD))
                pe.wait_ge(s_gT, n + AHEAD)
                for f in range(FT):
                    ins = pe.transpose(ps_t[:, f * P:(f + 1) * P], g[s][:, f * P:(f + 1) * P], ident[:, :])
                ins.then_inc(s_gt, 1)

            def down(n, s):
                e = expert(n)
                pe.wait_ge(s_gT, n + (1 + AHEAD))
                pe.wait_ge(s_y, n + AHEAD)
                for f in range(FT):
                    ins = pe.matmul(ps_y[:, 0:D], gT[s][:, f, :],
                                    w2[:, ds(e * FT + f, 1), :].rearrange("p o m -> p (o m)"),
                                    start=(f == 0), stop=(f == FT - 1))
                ins.then_inc(s_dn, 1)

            turn_rows(0, 0, 0)
            up(0, 0)
            turn_rows(0, 1, 1)
            up(1, 1)
            turn_rows(1, 2, 0)
            turn_products(0, 0)
            with pe.Fori(0, NTILES // 2 - 2) as i:
                for s in range(2):
                    n = i * 2 + (s + 2)
                    up(n, s)
                    turn_rows(i + (1 + s), n + 1, 1 - s)
                    turn_products(n - 1, 1 - s)
                    down(n - 2, s)
            n = NTILES - 2
            up(n, 0)
            turn_rows(NTILES // 2 - 1, n + 1, 1)
            turn_products(n - 1, 1)
            down(n - 2, 0)
            up(n + 1, 1)
            turn_products(n, 0)
            down(n - 1, 1)
            turn_products(n + 1, 1)
            down(n, 0)
            down(n + 1, 1)

        @block.scalar
        def _(act):
            act.sem_inc(s_hT, AHEAD)
            act.sem_inc(s_gT, AHEAD)

            def rows(n, s):
                act.wait_ge(s_ht, n + (1 + AHEAD))
                act.wait_ge(s_up, n + 1)
                nc.scalar.activation(hT[s][:, :, :].rearrange("p k t -> p (k t)"), ps_h[:, 0:D],
                                     ACT.Copy).then_inc(s_hT, 1)

            def silu(n, s):
                act.wait_ge(s_up, n + (1 + AHEAD))
                act.wait_ge(s_g, n + 1)
                nc.scalar.activation(si[s][:, :], ps_g[s][:, :], ACT.Silu).then_inc(s_si, 1)

            def products(n, s):
                act.wait_ge(s_gt, n + (1 + AHEAD))
                act.wait_ge(s_dn, n + 1)
                nc.scalar.activation(gT[s][:, :, :].rearrange("p f t -> p (f t)"), ps_t[:, :],
                                     ACT.Copy).then_inc(s_gT, 1)

            rows(0, 0)
            rows(1, 1)
            silu(0, 0)
            with act.Fori(0, NTILES // 2 - 1) as i:
                for s in range(2):
                    n = i * 2 + (s + 2)
                    rows(n, s)
                    silu(n - 1, 1 - s)
                    products(n - 2, s)
            n = NTILES
            silu(n - 1, 1)
            products(n - 2, 0)
            products(n - 1, 1)

        @block.vector
        def _(dve):
            v = nc.vector
            dve.sem_inc(s_up, AHEAD)
            dve.sem_inc(s_g, AHEAD)
            dve.sem_inc(s_y, AHEAD)

            def product(n, s):
                dve.wait_ge(s_si, n + 1)
                dve.wait_ge(s_gt, n + 1)
                v.tensor_tensor(g[s][:, :], si[s][:, :], ps_u[s][:, :], ALU.mult).then_inc(s_g, 1)

            def result(i, n, s):
                dve.wait_ge(s_dn, n + (1 + AHEAD))
                dve.wait_ge(s_st[s], i * 16 + 16)
                v.tensor_copy(y[s][:, :], ps_y[:, 0:D]).then_inc(s_y, 1)

            product(0, 0)
            product(1, 1)
            with dve.Fori(0, NTILES // 2 - 1) as i:
                for s in range(2):
                    n = i * 2 + (s + 2)
                    product(n, s)
                    result(i, n - 2, s)
            for s in range(2):
                result(NTILES // 2 - 1, NTILES - 2 + s, s)


def combine(nc, A, M, out):
    with ExitStack() as ctx:
        def sem(name):
            return nc.alloc_semaphore(name)

        NT, R = TOK // P, 4
        res, pos, wt = M["res"], M["pos"], M["wt"]
        y = [[ctx.enter_context(nc.sbuf_tensor(f"c_y{c}{i}", [P, D], F32)) for i in range(R)] for c in range(2)]
        s_g = [[sem(f"comb_gathered{c}{i}") for i in range(R)] for c in range(2)]
        s_a, s_b, s_out = sem("comb_first_added"), sem("comb_second_added"), sem("comb_stored")
        out_v = out.rearrange("(n p) d -> p n d", p=P)
        block = ctx.enter_context(nc.Block())

        @block.gpsimd
        def _(pool):
            for n in range(NT):
                if n >= R:
                    pool.wait_ge(s_b, n - R + 1)
                for c in range(2):
                    pool.indirect_dma_start(
                        out=y[c][n % R][:, :], out_offset=None, in_=M["ys_d"],
                        in_offset=bass.IndirectOffsetOnAxis(ap=pos[c][:, n:n + 1], axis=0)
                    ).then_inc(s_g[c][n % R], 16)

        @block.vector
        def _(dve):
            v = nc.vector
            for n in range(NT):
                dve.wait_ge(s_g[0][n % R], (n // R + 1) * 16)
                v.scalar_tensor_tensor(res[:, n, :], y[0][n % R][:, :], wt[0][:, n:n + 1], res[:, n, :],
                                       ALU.mult, ALU.add).then_inc(s_a, 1)
                dve.wait_ge(s_g[1][n % R], (n // R + 1) * 16)
                dve.wait_ge(s_a, n + 1)
                v.scalar_tensor_tensor(res[:, n, :], y[1][n % R][:, :], wt[1][:, n:n + 1], res[:, n, :],
                                       ALU.mult, ALU.add).then_inc(s_b, 1)

        @block.sync
        def _(sp):
            for b in range(NBLK):
                sp.wait_ge(s_b, (b + 1) * TPB)
                sp.dma_start(out_v[:, b * TPB:(b + 1) * TPB, :],
                             res[:, b * TPB:(b + 1) * TPB, :]).then_inc(s_out, 16)
            sp.wait_ge(s_out, NBLK * 16)


def program(nc, A, out):
    with ExitStack() as ctx:
        def dram(name, shape, dt=F32):
            return nc.dram_tensor(name, shape, dt).ap()

        M = {"x1_d": dram("x1_rows", (TOK, D)), "xn_d": dram("xn_rows", (TOK, D)),
             "qa_d": dram("qa_parts", (3, B * D, L), BF16), "ka_d": dram("ka_parts", (3, B * D, L), BF16),
             "qb_d": dram("qb_parts", (3, B * D, L), BF16), "kb_d": dram("kb_parts", (3, B * KV * HD, L), BF16),
             "va_d": dram("va_tiles", (TOK, HEADS * VW)), "vb_d": dram("vb_tiles", (TOK, KV * VW)),
             "hs_d": dram("expert_rows", (NTILES * TR, D)), "ys_d": dram("expert_results", (NTILES * TR, D)),
             "ao_d": [dram(f"attention{i}_rows", (TOK, D)) for i in range(2)]}
        M["banks"] = ctx.enter_context(nc.psum_tensor("banks", [P, 8, 512], F32))
        M["ps"] = [M["banks"][:, i, :] for i in range(8)]
        M["ident"] = ctx.enter_context(nc.sbuf_tensor("ident", [P, P], F32))
        with ExitStack() as first:
            def sb(name, shape, dt=F32):
                return first.enter_context(nc.sbuf_tensor(name, shape, dt))

            M["xnT"] = sb("xnT", [P, KD, TOK])
            M["f1"], M["f2"] = sb("f1", [P, TOK]), sb("f2", [P, TOK])
            M["pw"] = sb("pw", [P, NPOW, 4])
            M["r1"], M["r2"], M["rtmp"] = sb("r1", [P, CHUNK]), sb("r2", [P, CHUNK]), sb("rtmp", [P, 2, CHUNK])
            middle_weights(nc, first, M)
            front(nc, A, M)
            recurrence(nc, A, M)
            middle(nc, A, M)
        attention(nc, A, M)
        def keep(name, shape, dt=F32):
            return ctx.enter_context(nc.sbuf_tensor(name, shape, dt))

        NT = TOK // P
        M["res"] = keep("res", [P, NT, D])
        M["logits"] = keep("logits", [P, NT, NE])
        M["pos"] = [keep(f"place{c}", [P, NT], mybir.dt.uint32) for c in range(2)]
        M["wt"] = [keep(f"weight{c}", [P, NT]) for c in range(2)]
        M["tile_expert"] = keep("tile_expert", [P, NTILES], mybir.dt.int32)
        M["w13"] = keep("w13", [P, NE * KD, 2 * FFN])
        M["s_w13"], M["s_w2"] = nc.alloc_semaphore("w13_loaded"), nc.alloc_semaphore("w2_loaded")
        with ExitStack() as rows:
            M["h2_rows"] = rows.enter_context(nc.sbuf_tensor("h2_rows", [P, NT, D], F32))
            after(nc, A, M)
            M["w2"] = rows.enter_context(nc.sbuf_tensor("w2", [P, NE * FT, D], F32))
            route(nc, A, M)
            experts(nc, A, M, out)
        combine(nc, A, M, out)


def constants():
    import numpy as np
    bf = np.dtype("bfloat16")
    c = {"c_ident": np.eye(P, dtype=np.float32), "c_identb": np.eye(P, dtype=np.float32).astype(bf)}
    c["c_rank"] = np.tile(np.arange(NE, 0, -1, dtype=np.float32), (P, 1))
    c["c_steps"] = np.tile(np.arange(PER, dtype=np.float32) * TR, (P, NE, 1))
    c["c_tiles"] = np.tile(np.arange(NTILES, dtype=np.float32), (P, 1))
    c["c_upper"] = np.triu(np.ones((P, P), np.float32), 1)
    q, k = np.arange(P)[:, None], np.arange(P)[None, :]
    c["c_maskq"] = np.where(k > q, MASKED, 0.0).astype(np.float32).astype(bf)
    c["c_maskk"] = np.ascontiguousarray(c["c_maskq"].T)
    inv = (1.0 / 10000.0 ** (np.arange(0, HD, 2, dtype=np.float32) / np.float32(HD))).astype(np.float32)
    ang = (np.arange(L, dtype=np.float32)[:, None] * inv[None, :]).astype(np.float32)
    emb = np.concatenate([ang, ang], axis=1).T
    sign = np.where(np.arange(HD) < HD // 2, -1.0, 1.0).astype(np.float32)[:, None]
    c["c_cos"] = np.tile(np.cos(emb), (P // HD, 1)).astype(np.float32)
    c["c_sin"] = np.tile(np.sin(emb) * sign, (P // HD, 1)).astype(np.float32)
    slope = np.array([2.0 ** -0.5 * (2.0 ** -0.5) ** i for i in range(HEADS)], np.float32)
    s1 = slope.astype(bf).astype(np.float32)
    s2 = (slope - s1).astype(bf).astype(np.float32)
    s3 = slope - s1 - s2
    pos = np.arange(L)
    hi, lo = (pos - pos % 16).astype(np.float32), (pos % 16).astype(np.float32)
    cq = np.zeros((HEADS, AUG, L), np.float32)
    ck = np.zeros((HEADS, AUG, L), np.float32)
    for n, s in enumerate((s1, s2, s3)):
        cq[:, n], cq[:, 3 + n] = s[:, None], s[:, None]
        ck[:, n], ck[:, 3 + n] = hi, lo
        cq[:, 6 + n], cq[:, 9 + n] = hi, lo
        ck[:, 6 + n], ck[:, 9 + n] = -s[:, None], -s[:, None]
    ck[:, MROW:MROW + 3] = 1.0
    c["c_qa"] = np.ascontiguousarray(cq.transpose(1, 0, 2)).astype(bf)
    c["c_qb"] = np.zeros((AUG, GH, L), np.float32).astype(bf)
    c["c_ka"] = np.ascontiguousarray(ck.transpose(1, 0, 2)).astype(bf)
    c["c_kb"] = np.ascontiguousarray(np.concatenate([np.zeros((MROW, L)), np.ones((3, L))]).astype(bf))
    return c


def kernel(**inputs):
    import numpy as _np
    import concourse.bacc as _bacc
    from concourse import mybir as _mybir
    from concourse.bass_utils import run_bass_kernel_spmd as _run

    g = {k: _np.asarray(v) for k, v in inputs.items()}
    wq = g["L1_ffn_wqkv"]
    nq, nk = HEADS * HD, KV * HD
    swap = _np.arange(nq + nk) // HD * HD + (_np.arange(nq + nk) % HD + HD // 2) % HD
    w_b = _np.concatenate([wq[:nq], wq[swap[:nq]], wq[nq:nq + nk], wq[swap[nq:]], wq[nq + nk:]]).T
    arrays = {
        "x": g["L0_attn_input_sequence"], "steps": g["L0_attn_steps_raw"], "G": g["L0_attn_G_raw"],
        "A": g["L0_attn_A_raw"], "D": g["L0_attn_D_vec"],
        "b_mat": g["L0_attn_B_mat"].transpose(1, 2, 0).reshape(D, P),
        "c_mat": g["L0_attn_C_mat"].transpose(2, 1, 0).reshape(P, D),
        "w_ffn": g["L0_ffn_weights"].T, "scale": g["L0_ffn_scale"], "bias": g["L0_ffn_bias"],
        "w_qkv": g["L1_attn_W_qkv"], "b_qkv": g["L1_attn_b_qkv"], "w_out": g["L1_attn_W_out"],
        "b_out": g["L1_attn_b_out"], "ln1": g["L1_ffn_ln1_w"], "ln2": g["L1_ffn_ln2_w"], "w_b": w_b,
        "wo": g["L1_ffn_wo"].T, "gate": g["L1_ffn_gate_w"].T,
        "w13": g["L1_ffn_w13"].transpose(0, 2, 1), "w2": g["L1_ffn_w2"].transpose(0, 2, 1),
    }
    arrays.update(constants())
    nc = _bacc.Bacc("TRN2", target_bir_lowering=False, num_devices=1)
    feed, A = {}, {}
    for name, a in arrays.items():
        a = _np.ascontiguousarray(a)
        feed[f"in_{name}"] = a
        A[name] = nc.dram_tensor(f"in_{name}", a.shape, _mybir.dt.from_np(a.dtype), kind="ExternalInput").ap()
    out = nc.dram_tensor("out_rows", (TOK, D), F32, kind="ExternalOutput").ap()
    program(nc, A, out)
    r = _run(nc, [feed], core_ids=[0])
    return r.results[0]["out_rows"].reshape(B, L, D)
```
